# Optimizing a Trainium2 kernel written in Bass

```python
import numpy as np
import jax
import jax.numpy as jnp

def _softmax(x, axis=-1):
    return jax.nn.softmax(x, axis=axis)

def _gelu(x):
    return jax.nn.gelu(x, approximate=True)

def _silu(x):
    return jax.nn.silu(x)

def _sigmoid(x):
    return jax.nn.sigmoid(x)

def _layernorm(x, axis=-1, eps=1e-05):
    m = jnp.mean(x, axis=axis, keepdims=True)
    v = jnp.var(x, axis=axis, keepdims=True)
    return (x - m) / jnp.sqrt(v + eps)

def _scatter_add(tgt, idx, src, axis=0):
    return tgt.at[idx].add(src)

def _segment_sum(src, seg, n):
    return jax.ops.segment_sum(src, seg, n)
kernel_name = 'mk_cond_seq_d4_seqx_r4_70a457'

def setup_inputs(seed: int=0):
    np.random.seed(seed)
    _w = jnp.asarray

    def _rec_inputs():
        import jax
        import jax.numpy as jnp
        _rk = jax.random.key(seed)
        x = 0.5 + 0.2887 * jax.random.normal(jax.random.fold_in(_rk, 1), (64, 64, 256), jnp.float32)
        _lenS = 64 - jax.random.randint(jax.random.fold_in(_rk, 7), (64,), 0, max(1, 64 // 4) + 1, jnp.int32)
        _lenS2 = 64 - jax.random.randint(jax.random.fold_in(_rk, 8), (64,), 0, max(1, 64 // 4) + 1, jnp.int32)
        cond_1024 = jax.random.uniform(jax.random.fold_in(_rk, 11), (64, 256), jnp.float32, 0.0, 0.999994)
        _validS = jnp.arange(64)[None, :] < _lenS[:, None]
        _validS2 = jnp.arange(64)[None, :] < _lenS2[:, None]
        _causal = jnp.tril(jnp.ones((64, 64), dtype=bool))
        mask_BxSxSx11_ik0 = jnp.where(jnp.ones((64, 64, 64, 11), dtype=bool), 0, 1).astype(jnp.int32)
        return (x, cond_1024, mask_BxSxSx11_ik0)
    x, cond_1024, mask_BxSxSx11_ik0 = _rec_inputs()

    def _L0_cond_setup():
        import jax, jax.numpy as jnp
        import numpy as np
        N, HW, C = (32, 1024, 256)
        WRS_RATIO = 0.5
        P = 0.9
        M = int(WRS_RATIO * C)
        key = jax.random.key(seed)
        k1, k2, k3 = jax.random.split(key, 3)
        x = jax.random.uniform(k1, (N, HW, C), dtype=jnp.float32)
        r = jax.random.uniform(k2, (N, C), dtype=jnp.float32)
        u = jax.random.uniform(k3, (N, C), dtype=jnp.float32)
        return {'x': x, 'r': r, 'u': u}
    _L0_cond_all = _L0_cond_setup()
    _L0_cond_in = {k: v for k, v in _L0_cond_all.items() if k in ()}
    del _L0_cond_all

    def _L1_cond_setup():
        import jax, jax.numpy as jnp
        import numpy as np
        EPS = 1e-05

        def _sln(h, w, ln_g, ln_b, Wg, bg, Wb, bb):
            mu = jnp.mean(h, axis=-1, keepdims=True)
            var = jnp.mean((h - mu) ** 2, axis=-1, keepdims=True)
            ln = (h - mu) / jnp.sqrt(var + EPS) * ln_g + ln_b
            gamma = (w @ Wg.T + bg)[:, None, :]
            beta = (w @ Wb.T + bb)[:, None, :]
            return gamma * ln + beta
        key = jax.random.key(seed)
        ks = jax.random.split(key, 20)
        B, N, D = (4, 256, 256)
        F = 4 * D
        s = lambda fan: 1.0 / np.sqrt(fan)
        inp = {'hidden': jax.random.normal(ks[0], (B, N, D), jnp.float32), 'w': jax.random.normal(ks[1], (B, D), jnp.float32), 'ln_g': jnp.ones((D,), jnp.float32), 'ln_b': jnp.zeros((D,), jnp.float32), 'Wg': jax.random.normal(ks[2], (D, D), jnp.float32) * s(D), 'bg': jnp.zeros((D,), jnp.float32), 'Wb': jax.random.normal(ks[3], (D, D), jnp.float32) * s(D), 'bb': jnp.zeros((D,), jnp.float32), 'Wqkv': jax.random.normal(ks[4], (3 * D, D), jnp.float32) * s(D), 'bqkv': jnp.zeros((3 * D,), jnp.float32), 'Wp': jax.random.normal(ks[5], (D, D), jnp.float32) * s(D), 'bp': jnp.zeros((D,), jnp.float32), 'W1': jax.random.normal(ks[6], (F, D), jnp.float32) * s(D), 'b1': jnp.zeros((F,), jnp.float32), 'W2': jax.random.normal(ks[7], (D, F), jnp.float32) * s(F), 'b2': jnp.zeros((D,), jnp.float32), 'num_heads': 16}
        return inp
    _L1_cond_all = _L1_cond_setup()
    _L1_cond_in = {k: v for k, v in _L1_cond_all.items() if k in ('ln_g', 'ln_b', 'Wg', 'bg', 'Wb', 'bb', 'Wqkv', 'bqkv', 'Wp', 'bp', 'W1', 'b1', 'W2', 'b2')}
    del _L1_cond_all

    def _L2_cond_setup():
        import jax, jax.numpy as jnp
        import numpy as np
        H = 16
        EPS = 1e-05

        def layer_norm(x, g, b):
            mu = jnp.mean(x, axis=-1, keepdims=True)
            var = jnp.var(x, axis=-1, keepdims=True)
            return (x - mu) * jax.lax.rsqrt(var + EPS) * g + b
        key = jax.random.key(seed)
        ks = jax.random.split(key, 8)
        B, T, D, TE = (4, 1024, 256, 256)
        s = 0.02
        return {'x': jax.random.normal(ks[0], (B, T, D), jnp.float32), 'emb': jax.random.normal(ks[1], (B, 1, TE), jnp.float32), 'gate_msa': jax.random.normal(ks[2], (B, 1, D), jnp.float32), 'norm_g': jnp.ones((D,), jnp.float32), 'norm_b': jnp.zeros((D,), jnp.float32), 'Wq': jax.random.normal(ks[3], (D, D), jnp.float32) * s, 'bq': jnp.zeros((D,), jnp.float32), 'Wk': jax.random.normal(ks[4], (D, D), jnp.float32) * s, 'bk': jnp.zeros((D,), jnp.float32), 'Wv': jax.random.normal(ks[5], (D, D), jnp.float32) * s, 'bv': jnp.zeros((D,), jnp.float32), 'emb_W': jax.random.normal(ks[6], (TE, 2 * D), jnp.float32) * s, 'emb_b': jnp.zeros((2 * D,), jnp.float32), 'sn_g': jnp.ones((D,), jnp.float32), 'sn_b': jnp.zeros((D,), jnp.float32), 'out_W': jax.random.normal(ks[7], (D, D), jnp.float32) * s, 'out_b': jnp.zeros((D,), jnp.float32)}
    _L2_cond_all = _L2_cond_setup()
    _L2_cond_in = {k: v for k, v in _L2_cond_all.items() if k in ('norm_g', 'norm_b', 'Wq', 'bq', 'Wk', 'bk', 'Wv', 'bv', 'emb_W', 'emb_b', 'sn_g', 'sn_b', 'out_W', 'out_b')}
    del _L2_cond_all

    def _L3_cond_setup():
        import jax, jax.numpy as jnp
        import numpy as np
        NONGT = 20
        H = 16
        NEG = -9000000000000000.0

        def _gat_attention(self_feat, cond_adj, label_bias, Wq, bq, Wk, bk, Wout, bout):
            B, N, F = self_feat.shape
            ng = min(NONGT, N)
            dh = F // H
            kv = self_feat[:, :ng]
            qh = (self_feat @ Wq.T + bq).reshape(B, N, H, dh)
            kh = (kv @ Wk.T + bk).reshape(B, ng, H, dh)
            aff = jnp.einsum('bnhd,bmhd->bnhm', qh, kh) * (1.0 / np.sqrt(dh))
            mask = cond_adj[:, :, None, :] > 0
            aff = jnp.where(mask, aff, NEG) + label_bias[:, :, None, :]
            w = jax.nn.softmax(aff, axis=-1)
            out_t = jnp.einsum('bnhm,bmf->bnhf', w, kv)
            out = jnp.einsum('bnhf,hgf->bnhg', out_t, Wout) + bout.reshape(H, F // H)
            return out.reshape(B, N, F)

        def _forward(v, q, adj, W_self, b_self, w_bias, b_bias, Wq, bq, Wk, bk, Wout, bout):
            adj_f = adj.astype(jnp.float32)
            exp_v = v
            row_zero = exp_v.sum(-1) == 0
            q_exp = jnp.where(row_zero[..., None], 0.0, q[:, None, :])
            vcq = jnp.concatenate([exp_v, q_exp], axis=-1)
            self_feat = vcq @ W_self.T + b_self
            output = self_feat
            for d in range(2):
                A = adj_f if d == 0 else jnp.swapaxes(adj_f, 1, 2)
                A = A[:, :, :NONGT, :]
                cond = A.sum(-1)
                vb = A @ w_bias + b_bias
                output = output + _gat_attention(self_feat, cond, vb, Wq[d], bq[d], Wk[d], bk[d], Wout[d], bout[d])
            rel = jax.nn.relu(output)
            return exp_v + rel
        key = jax.random.key(seed)
        ks = jax.random.split(key, 8)
        B, N, L, F, Q = (64, 36, 11, 256, 256)
        IN = F + Q
        s = 0.02
        return {'v': jax.random.normal(ks[0], (B, N, F), jnp.float32), 'q': jax.random.normal(ks[1], (B, Q), jnp.float32), 'adj': jax.random.randint(ks[2], (B, N, N, L), 0, 2, jnp.int32), 'W_self': jax.random.normal(ks[3], (F, IN), jnp.float32) * s, 'b_self': jnp.zeros((F,), jnp.float32), 'w_bias': jax.random.normal(ks[4], (L,), jnp.float32) * s, 'b_bias': jnp.zeros((), jnp.float32), 'Wq': jax.random.normal(ks[5], (2, F, F), jnp.float32) * s, 'bq': jnp.zeros((2, F), jnp.float32), 'Wk': jax.random.normal(ks[6], (2, F, F), jnp.float32) * s, 'bk': jnp.zeros((2, F), jnp.float32), 'Wout': jax.random.normal(ks[7], (2, H, F // H, F), jnp.float32) * s, 'bout': jnp.zeros((2, F), jnp.float32)}
    _L3_cond_all = _L3_cond_setup()
    _L3_cond_in = {k: v for k, v in _L3_cond_all.items() if k in ('W_self', 'b_self', 'w_bias', 'b_bias', 'Wq', 'bq', 'Wk', 'bk', 'Wout', 'bout')}
    del _L3_cond_all
    return {'x': x, 'cond_1024': cond_1024, 'mask_BxSxSx11_ik0': mask_BxSxSx11_ik0, 'L1_cond_ln_g': _L1_cond_in['ln_g'], 'L1_cond_ln_b': _L1_cond_in['ln_b'], 'L1_cond_Wg': _L1_cond_in['Wg'], 'L1_cond_bg': _L1_cond_in['bg'], 'L1_cond_Wb': _L1_cond_in['Wb'], 'L1_cond_bb': _L1_cond_in['bb'], 'L1_cond_Wqkv': _L1_cond_in['Wqkv'], 'L1_cond_bqkv': _L1_cond_in['bqkv'], 'L1_cond_Wp': _L1_cond_in['Wp'], 'L1_cond_bp': _L1_cond_in['bp'], 'L1_cond_W1': _L1_cond_in['W1'], 'L1_cond_b1': _L1_cond_in['b1'], 'L1_cond_W2': _L1_cond_in['W2'], 'L1_cond_b2': _L1_cond_in['b2'], 'L2_cond_norm_g': _L2_cond_in['norm_g'], 'L2_cond_norm_b': _L2_cond_in['norm_b'], 'L2_cond_Wq': _L2_cond_in['Wq'], 'L2_cond_bq': _L2_cond_in['bq'], 'L2_cond_Wk': _L2_cond_in['Wk'], 'L2_cond_bk': _L2_cond_in['bk'], 'L2_cond_Wv': _L2_cond_in['Wv'], 'L2_cond_bv': _L2_cond_in['bv'], 'L2_cond_emb_W': _L2_cond_in['emb_W'], 'L2_cond_emb_b': _L2_cond_in['emb_b'], 'L2_cond_sn_g': _L2_cond_in['sn_g'], 'L2_cond_sn_b': _L2_cond_in['sn_b'], 'L2_cond_out_W': _L2_cond_in['out_W'], 'L2_cond_out_b': _L2_cond_in['out_b'], 'L3_cond_W_self': _L3_cond_in['W_self'], 'L3_cond_b_self': _L3_cond_in['b_self'], 'L3_cond_w_bias': _L3_cond_in['w_bias'], 'L3_cond_b_bias': _L3_cond_in['b_bias'], 'L3_cond_Wq': _L3_cond_in['Wq'], 'L3_cond_bq': _L3_cond_in['bq'], 'L3_cond_Wk': _L3_cond_in['Wk'], 'L3_cond_bk': _L3_cond_in['bk'], 'L3_cond_Wout': _L3_cond_in['Wout'], 'L3_cond_bout': _L3_cond_in['bout']}

def reference(x, cond_1024, mask_BxSxSx11_ik0, L1_cond_ln_g, L1_cond_ln_b, L1_cond_Wg, L1_cond_bg, L1_cond_Wb, L1_cond_bb, L1_cond_Wqkv, L1_cond_bqkv, L1_cond_Wp, L1_cond_bp, L1_cond_W1, L1_cond_b1, L1_cond_W2, L1_cond_b2, L2_cond_norm_g, L2_cond_norm_b, L2_cond_Wq, L2_cond_bq, L2_cond_Wk, L2_cond_bk, L2_cond_Wv, L2_cond_bv, L2_cond_emb_W, L2_cond_emb_b, L2_cond_sn_g, L2_cond_sn_b, L2_cond_out_W, L2_cond_out_b, L3_cond_W_self, L3_cond_b_self, L3_cond_w_bias, L3_cond_b_bias, L3_cond_Wq, L3_cond_bq, L3_cond_Wk, L3_cond_bk, L3_cond_Wout, L3_cond_bout):
    import jax
    import jax.numpy as jnp

    def _L0_cond_ref(x, r, u):
        import jax, jax.numpy as jnp
        import numpy as np
        N, HW, C = (32, 1024, 256)
        WRS_RATIO = 0.5
        P = 0.9
        M = int(WRS_RATIO * C)
        xt = jnp.swapaxes(x, 1, 2)
        score = jnp.mean(xt, axis=2)
        key = r ** (1.0 / score)
        thr = jnp.sort(key, axis=1)[:, C - M][:, None]
        sel = key >= thr
        sel_score = jnp.sum(jnp.where(sel, score, 0.0), axis=1, keepdims=True)
        alpha = jnp.sum(score, axis=1, keepdims=True) / sel_score
        rng = u < P
        maskf = (sel & rng).astype(x.dtype) * alpha
        out = xt * maskf[:, :, None]
        return jnp.swapaxes(out, 1, 2)

    def _L1_cond_ref(hidden, w, ln_g, ln_b, Wg, bg, Wb, bb, Wqkv, bqkv, Wp, bp, W1, b1, W2, b2, num_heads):
        import jax, jax.numpy as jnp
        import numpy as np
        EPS = 1e-05

        def _sln(h, w, ln_g, ln_b, Wg, bg, Wb, bb):
            mu = jnp.mean(h, axis=-1, keepdims=True)
            var = jnp.mean((h - mu) ** 2, axis=-1, keepdims=True)
            ln = (h - mu) / jnp.sqrt(var + EPS) * ln_g + ln_b
            gamma = (w @ Wg.T + bg)[:, None, :]
            beta = (w @ Wb.T + bb)[:, None, :]
            return gamma * ln + beta
        B, N, D = hidden.shape
        hd = D // num_heads
        h = _sln(hidden, w, ln_g, ln_b, Wg, bg, Wb, bb)
        qkv = (h @ Wqkv.T + bqkv).reshape(B, N, num_heads, hd, 3)
        q = jnp.moveaxis(qkv[..., 0], 2, 1)
        k = jnp.moveaxis(qkv[..., 1], 2, 1)
        v = jnp.moveaxis(qkv[..., 2], 2, 1)
        energy = jnp.einsum('bhqd,bhkd->bhqk', q, k)
        att = jax.nn.softmax(energy, axis=-1) / D ** 0.5
        out = jnp.einsum('bhqk,bhkd->bhqd', att, v)
        out = jnp.moveaxis(out, 1, 2).reshape(B, N, D)
        out = out @ Wp.T + bp
        h1 = out + hidden
        h2 = _sln(h1, w, ln_g, ln_b, Wg, bg, Wb, bb)
        return h2 + h1

    def _L2_cond_ref(x, emb, gate_msa, norm_g, norm_b, Wq, bq, Wk, bk, Wv, bv, emb_W, emb_b, sn_g, sn_b, out_W, out_b):
        import jax, jax.numpy as jnp
        import numpy as np
        H = 16
        EPS = 1e-05

        def layer_norm(x, g, b):
            mu = jnp.mean(x, axis=-1, keepdims=True)
            var = jnp.var(x, axis=-1, keepdims=True)
            return (x - mu) * jax.lax.rsqrt(var + EPS) * g + b
        B, T, D = x.shape
        dh = D // H
        xn = layer_norm(x, norm_g, norm_b)
        q = (xn @ Wq + bq).reshape(B, T, H, dh)
        k = (xn @ Wk + bk).reshape(B, T, H, dh)
        v = (xn @ Wv + bv).reshape(B, T, H, dh)
        q = jax.nn.softmax(q, axis=-1)
        k = jax.nn.softmax(k, axis=1)
        ctx = jnp.einsum('bnhd,bnhl->bhdl', k, v)
        y = jnp.einsum('bnhd,bhdl->bnhl', q, ctx).reshape(B, T, D)
        emb_out = jax.nn.silu(emb) @ emb_W + emb_b
        scale, shift = jnp.split(emb_out, 2, axis=-1)
        h = layer_norm(y, sn_g, sn_b) * (1.0 + scale) + shift
        h = jax.nn.silu(h) @ out_W + out_b
        return x + gate_msa * h

    def _L3_cond_ref(v, q, adj, W_self, b_self, w_bias, b_bias, Wq, bq, Wk, bk, Wout, bout):
        import jax, jax.numpy as jnp
        import numpy as np
        NONGT = 20
        H = 16
        NEG = -9000000000000000.0

        def _gat_attention(self_feat, cond_adj, label_bias, Wq, bq, Wk, bk, Wout, bout):
            B, N, F = self_feat.shape
            ng = min(NONGT, N)
            dh = F // H
            kv = self_feat[:, :ng]
            qh = (self_feat @ Wq.T + bq).reshape(B, N, H, dh)
            kh = (kv @ Wk.T + bk).reshape(B, ng, H, dh)
            aff = jnp.einsum('bnhd,bmhd->bnhm', qh, kh) * (1.0 / np.sqrt(dh))
            mask = cond_adj[:, :, None, :] > 0
            aff = jnp.where(mask, aff, NEG) + label_bias[:, :, None, :]
            w = jax.nn.softmax(aff, axis=-1)
            out_t = jnp.einsum('bnhm,bmf->bnhf', w, kv)
            out = jnp.einsum('bnhf,hgf->bnhg', out_t, Wout) + bout.reshape(H, F // H)
            return out.reshape(B, N, F)

        def _forward(v, q, adj, W_self, b_self, w_bias, b_bias, Wq, bq, Wk, bk, Wout, bout):
            adj_f = adj.astype(jnp.float32)
            exp_v = v
            row_zero = exp_v.sum(-1) == 0
            q_exp = jnp.where(row_zero[..., None], 0.0, q[:, None, :])
            vcq = jnp.concatenate([exp_v, q_exp], axis=-1)
            self_feat = vcq @ W_self.T + b_self
            output = self_feat
            for d in range(2):
                A = adj_f if d == 0 else jnp.swapaxes(adj_f, 1, 2)
                A = A[:, :, :NONGT, :]
                cond = A.sum(-1)
                vb = A @ w_bias + b_bias
                output = output + _gat_attention(self_feat, cond, vb, Wq[d], bq[d], Wk[d], bk[d], Wout[d], bout[d])
            rel = jax.nn.relu(output)
            return exp_v + rel
        return _forward(v, q, adj, W_self, b_self, w_bias, b_bias, Wq, bq, Wk, bk, Wout, bout)
    x = _L0_cond_ref(x, cond_1024, cond_1024)
    x = _L1_cond_ref(x, cond_1024, L1_cond_ln_g, L1_cond_ln_b, L1_cond_Wg, L1_cond_bg, L1_cond_Wb, L1_cond_bb, L1_cond_Wqkv, L1_cond_bqkv, L1_cond_Wp, L1_cond_bp, L1_cond_W1, L1_cond_b1, L1_cond_W2, L1_cond_b2, 16)
    x = _L2_cond_ref(x, cond_1024[:, None, :], cond_1024[:, None, :], L2_cond_norm_g, L2_cond_norm_b, L2_cond_Wq, L2_cond_bq, L2_cond_Wk, L2_cond_bk, L2_cond_Wv, L2_cond_bv, L2_cond_emb_W, L2_cond_emb_b, L2_cond_sn_g, L2_cond_sn_b, L2_cond_out_W, L2_cond_out_b)
    x = _L3_cond_ref(x, cond_1024, mask_BxSxSx11_ik0, L3_cond_W_self, L3_cond_b_self, L3_cond_w_bias, L3_cond_b_bias, L3_cond_Wq, L3_cond_bq, L3_cond_Wk, L3_cond_bk, L3_cond_Wout, L3_cond_bout)
    return x

_drawn_inputs = setup_inputs


def setup_inputs(seed=0):
    import zlib

    import numpy as np

    out = dict(_drawn_inputs(seed))
    spreads = {'L1_cond_ln_g': (1.0, 0.2),
     'L1_cond_ln_b': (0.0, 0.1),
     'L1_cond_bg': (0.0, 0.1),
     'L1_cond_bb': (0.0, 0.1),
     'L1_cond_bqkv': (0.0, 0.8),
     'L1_cond_bp': (0.0, 0.1),
     'L1_cond_b1': (0.0, 0.1),
     'L1_cond_b2': (0.0, 0.1),
     'L2_cond_norm_g': (1.0, 0.6),
     'L2_cond_norm_b': (0.0, 0.783),
     'L2_cond_bq': (0.0, 0.8),
     'L2_cond_bk': (0.0, 0.8),
     'L2_cond_bv': (0.0, 0.1),
     'L2_cond_emb_b': (0.0, 0.484),
     'L2_cond_sn_g': (1.0, 0.6),
     'L2_cond_sn_b': (0.0, 0.8),
     'L2_cond_out_b': (0.0, 0.1),
     'L3_cond_b_self': (0.0, 0.1),
     'L3_cond_bq': (0.0, 0.1),
     'L3_cond_bk': (0.0, 0.1),
     'L3_cond_bout': (0.0, 0.1)}
    factors = {'L2_cond_Wq': 8.0, 'L2_cond_Wk': 8.0, 'L2_cond_emb_W': 3.113}
    for name, (base, spread) in spreads.items():
        noise = np.random.default_rng([zlib.crc32(name.encode()), seed]).standard_normal(out[name].shape)
        drawn = base * np.exp(spread * noise) if base else spread * noise
        out[name] = jnp.asarray(drawn.astype(out[name].dtype))
    for name, factor in factors.items():
        out[name] = (out[name] * factor).astype(out[name].dtype)
    return out
```

```python
from contextlib import ExitStack

import concourse.bass as bass
from concourse import mybir

P = 128
B, S, C = 64, 64, 256
H, D = 16, 16
KC = C // P
GB = 4
GR = GB * S
GROUPS = B // GB
HC = H // KC
NG, L = 20, 11
HQ = 4
KQ = HQ * NG
EPS = 1e-5
NEG = -9000000000000000.0
KEEP = C // 2
P_KEEP = 0.9
LOG_MIN, LOG_MAX = -103.972, 88.7229

F32 = mybir.dt.float32
I32 = mybir.dt.int32
ALU = mybir.AluOpType
ACT = mybir.ActivationFunctionType
AX = mybir.AxisListType

FIRST_WEIGHTS = ["L1g", "L1b", "L2scale", "L2shift", "L3sq"]
WEIGHTS = ["L1q", "L1k", "L1v", "L1p", "L2q", "L2k", "L2v", "L2o", "L3s", "L3q0", "L3q1", "L3k0", "L3k1", "L3o0", "L3o1"]
VECTORS = ["L1ln_g", "L1ln_b", "L1bg", "L1bb", "L1bq", "L1bk", "L1bp", "L2norm_g", "L2norm_b", "L2bk",
           "L2scale_b", "L2shift_b", "L2sn_g", "L2sn_b", "L2out_b", "L3b_self", "L3bq0", "L3bq1",
           "L3bk0", "L3bk1", "L3bout0", "L3bout1"]
ROWVECS = ["L1bv", "L2bq", "L2bv"]


def bc(ap, axis, n):
    a = ap.unsqueeze(axis)
    shape = list(a.shape)
    shape[axis] = n
    return a.to_broadcast(shape)


def reach(eng, sem, value):
    if not (isinstance(value, int) and value <= 0):
        eng.wait_ge(sem, value)


def slots(*streams):
    heads = [[next(s), k, s] for k, s in enumerate(streams)]
    while heads:
        heads.sort(key=lambda x: x[:2])
        at = heads[0]
        try:
            at[0] = next(at[2])
        except StopIteration:
            heads.pop(0)


def build(nc, a, out):
    ctx = ExitStack()
    with ctx:
        def sb(name, shape, dt=F32):
            return ctx.enter_context(nc.sbuf_tensor(name, shape, dt))

        def bank(name):
            return ctx.enter_context(nc.psum_tensor(name, [P, 512], F32))

        def sem(name):
            return ctx.enter_context(nc.semaphore(name))

        w = sb("w", [P, len(WEIGHTS), KC, C])
        vec = sb("vec", [P, len(VECTORS), KC])
        rowvec = sb("rowvec", [P, len(ROWVECS), C])
        ident = sb("ident", [P, P])
        ones = sb("ones", [P, P])
        mask_h = sb("mask_h", [P, HC])
        mask_bd = sb("mask_bd", [P, P])
        mask_q = sb("mask_q", [KQ, HQ])
        w_label = sb("w_label", [P, L])
        b_label = sb("b_label", [P, 1])
        neg_half = sb("neg_half", [P, 2])

        def W(name, k, lo, hi):
            if name in FIRST_WEIGHTS:
                return first_w[:, FIRST_WEIGHTS.index(name), k, lo:hi]
            return w[:, WEIGHTS.index(name), k, lo:hi]

        def V(name, k=None):
            i = VECTORS.index(name)
            return vec[:, i, :] if k is None else vec[:, i, k:k + 1]

        cond_t = sb("cond_t", [P, KC, B])
        mask_t = sb("mask_t", [P, KC, B])
        gain1 = sb("gain1", [P, KC, B])
        bias1 = sb("bias1", [P, KC, B])
        gain2 = sb("gain2", [P, KC, B])
        bias2 = sb("bias2", [P, KC, B])
        qself = sb("qself", [P, KC, B])
        q0b = sb("q0b", [P, 2, KC])
        bout = sb("bout", [P, KC])

        x_all = sb("x_all", [P, KC, B, S])
        score_t = sb("score_t", [P, KC, B])
        top8 = sb("top8", [B, 8])
        sums = sb("sums", [B, 4])

        x1 = sb("x1", [P, KC, GB, S])
        z1 = sb("z1", [P, 2, C])
        ht = sb("ht", [P, KC, GR])
        g1 = sb("g1", [P, KC, GB, S])
        q1t = sb("q1t", [P, KC, GR])
        k1t = sb("k1t", [P, KC, GR])
        kbd = sb("kbd", [P, 4, 2, HC, S])
        vbd = sb("vbd", [P, GB, H // 2, 2, D + 1])
        prob = sb("prob", [P, 2, HC, S])
        probt = sb("probt", [P, 2, HC // 2, P])
        nmax1 = sb("nmax1", [P, 2, HC])
        rec1 = sb("rec1", [P, H])
        orow = sb("orow", [P, 2, C])
        ot = sb("ot", [P, KC, GR])
        h1 = sb("h1", [P, KC, GB, S])
        x2 = sb("x2", [P, KC, GB, S])
        st1, mv1, ve1, rs1 = sb("st1", [P, 2, 6]), sb("mv1", [P, 2, 2]), sb("ve1", [P, 2]), sb("rs1", [P, 2])
        xr2 = sb("xr2", [P, KC, GB, S])
        z2 = sb("z2", [P, 2, C])
        xn = sb("xn", [P, KC, GR])
        k2t = sb("k2t", [P, KC, GB, S])
        ekrow = sb("ekrow", [P, 2, C])
        vsep = sb("vsep", [P, 4, 2, P])
        kmax = sb("kmax", [P, KC * GB])
        krec = sb("krec", [P, KC * GB])
        q2 = sb("q2", [P, 2, H, D])
        qmax = sb("qmax", [P, 2 * H])
        qrec = sb("qrec", [P, 2, H])
        eqt = sb("eqt", [P, KC, GR])
        ctxbd = sb("ctxbd", [P, 2, KC, 2, P])
        yrow = sb("yrow", [P, 2, C])
        h2 = sb("h2", [P, KC, GB, S])
        e2 = sb("e2", [P, KC, GB, S])
        s2 = sb("s2", [P, KC, GR])
        x3 = sb("x3", [P, KC, GB, S])
        st2, mv2, ve2, rs2 = sb("st2", [P, 2, 6]), sb("mv2", [P, 2, 2]), sb("ve2", [P, 2]), sb("rs2", [P, 2])
        xr3 = sb("xr3", [P, KC, GB, S])
        nzq = sb("nzq", [P, KC, GB, S])
        sf = sb("sf", [P, KC, GB, S])
        q3t = sb("q3t", [P, 2, KC, GR])
        k3t = sb("k3t", [P, 2, KC, GB, NG])
        kbd3 = sb("kbd3", [P, 2, KC, GB, HC, NG])
        sfrep = sb("sfrep", [P, KC, GB, HQ, NG])
        vbd3 = sb("vbd3", [KQ, GB, 2, H, D + 1])
        adj = sb("adj", [P, 4, NG * L], I32)
        adjw = sb("adjw", [P, 4, NG * L])
        cnt = sb("cnt", [P, 4, NG])
        vb = sb("vb", [P, 4, NG])
        tmask = sb("tmask", [P, 4, NG])
        z3 = sb("z3", [P, 2, H, NG])
        max3 = sb("max3", [P, 2, H])
        p3t = sb("p3t", [KQ, 2, 4, P])
        rec3 = sb("rec3", [P, 2, H])
        att = sb("att", [P, 2, 2, C])
        atts = sb("atts", [P, 2, C])
        fin = sb("fin", [P, KC, GB, S])

        spare = kbd[:].rearrange("p u b h r -> p (u b h r)")
        cond, score, lnr, lkey, work, keepm = (spare[0:B, j * C:(j + 1) * C] for j in range(6))
        esil, fsil = (spare[:, 6 * C + j * KC * B:6 * C + (j + 1) * KC * B].rearrange("p (k b) -> p k b", k=KC) for j in range(2))
        first_w = kbd3[:].rearrange("p d k b h j -> p (d k b h j)").rearrange("p (w k n) -> p w k n", k=KC, n=C)

        bA, bE, bT = bank("bA"), bank("bE"), bank("bT")
        bX, bY = bank("bX"), bank("bY")
        b0, b1, b2 = bank("b0"), bank("b1"), bank("b2")

        names = """held ld_w ld_c ld_x ld_x2 ld_x3 ld_x4 ld_one pro_v pro_pe pro_a pro_g zeros
        l1_x1 l1_row l1_st l1_mv l1_ve l1_rs l1_z l1_zt l1_g l1_h l1_q l1_qt l1_k l1_kt l1_v l1_vs l1_kbd l1_e l1_max
        l1_sub l1_p l1_pt l1_pts l1_av l1_rec l1_o l1_ot l1_ots l1_wp l1_h1 l1_row2 l1_zt2 l1_g2 l1_b2 l1_x2
        l2_x l2_row l2_st l2_mv l2_ve l2_rs l2_z l2_zt l2_xn l2_k l2_kt l2_kmax l2_ksub l2_ke l2_ksum l2_krec l2_q l2_qb
        l2_qmax l2_qsub l2_qe l2_qsum l2_qrec l2_v l2_vs l2_ekt l2_ek l2_eqt l2_eq l2_ctx l2_ctxs l2_y l2_yr l2_yz
        l2_yt l2_g l2_h l2_e l2_e1 l2_r l2_s l2_o l2_og l2_x3
        l3_x l3_sfp l3_nz l3_sf l3_rep l3_q l3_qt l3_k l3_kt l3_kbd l3_v l3_vs l3_adj l3_aw l3_cnt l3_vb l3_t0 l3_t l3_aff l3_z
        l3_max l3_sub l3_p l3_pt l3_pts l3_av l3_rec l3_o l3_sum l3_at l3_r l3_fin l3_out""".split()
        s = {name: sem(name) for name in names}


        block = ctx.enter_context(nc.Block())
        PARTS = [s["ld_x"], s["ld_x2"], s["ld_x3"], s["ld_x4"]]
        out_v = out.rearrange("(k p) r -> p k r", p=P)

        def hold(eng, sem_, value):
            eng.wait_ge(sem_, value)
            eng.sem_inc(s["held"], 1)

        def bodies(eng, stream1, stream2, stream3):
            for i in range(3):
                slots(*[f(i - k) for k, f in enumerate((stream1, stream2, stream3)) if i >= k])
            with eng.Fori(3, GROUPS) as i:
                slots(stream1(i), stream2(i - 1), stream3(i - 2))
            slots(stream2(GROUPS - 1), stream3(GROUPS - 2))
            slots(stream3(GROUPS - 1))

        @block.sync
        def _(sp):
            for part in range(4):
                n = B // 4
                sp.dma_start(x_all[:, :, part * n:(part + 1) * n, :],
                             a["x_t"].rearrange("(k p) (b r) -> p k b r", p=P, r=S)[:, :, part * n:(part + 1) * n, :]
                             ).then_inc(PARTS[part], 16)

            def stream3(n):
                yield 1
                if not (isinstance(n, int) and n == 0):
                    sp.wait_ge(s["l3_cnt"], n)
                for d in range(2):
                    sp.dma_start(adj[:, 2 * d:2 * d + 2, :],
                                 a["adj"][d].rearrange("(t p) e -> p t e", p=P)[:, bass.ds(2 * n, 2), :]
                                 ).then_inc(s["l3_adj"], 16)
                yield 99
                sp.wait_ge(s["l3_fin"], n + 1)
                sp.dma_start(out_v[:, :, bass.ds(GR * n, GR)], fin[:, :, :, :].rearrange("p k b r -> p k (b r)")
                             ).then_inc(s["l3_out"], 16)

            def none(n):
                yield 0
            bodies(sp, none, none, stream3)
            sp.wait_ge(s["l3_out"], 16 * GROUPS)

        @block.gpsimd
        def _(pool):
            pool.memset(neg_half[:], -0.5).then_inc(s["zeros"], 1)
            pool.memset(vbd[:], 0.0).then_inc(s["zeros"], 1)
            pool.memset(vsep[:], 0.0).then_inc(s["zeros"], 1)
            pool.wait_ge(s["zeros"], 3)
            for j in range(2):
                pool.memset(vbd[64 * j:64 * j + 64, :, :, j, D:D + 1], 1.0).then_inc(s["zeros"], 1)
                pool.wait_ge(s["zeros"], 4 + j)
            pool.wait_ge(s["ld_c"], 16 * 11)
            for b in range(GB):
                for d in range(2):
                    i = pool.tensor_copy(vbd3[:, b, d, :, D].rearrange("p (q h) -> p q h", h=HQ), bc(mask_q[:], 1, 4))
            i.then_inc(s["zeros"], 1)

            def norm_rs(ve, rs, s_ve, s_rs, count):
                pool.wait_ge(s_ve, count)
                pool.tensor_tensor(rs[:], ve[:], neg_half[:], ALU.pow).then_inc(s_rs, 1)

            def stream1(n):
                yield 3
                norm_rs(ve1, rs1, s["l1_ve"], s["l1_rs"], 2 * n + 1)
                yield 5
                hold(pool, s["l1_g"], n + 1)
                pool.tensor_tensor(ht[:].rearrange("p k (b r) -> p k b r", b=GB), g1[:],
                                   bc(bias1[:, :, bass.ds(GB * n, GB)], 3, S), ALU.add).then_inc(s["l1_h"], 1)
                yield 8
                pool.wait_ge(s["l1_kt"], n + 1)
                kv = k1t[:].rearrange("p k (b r) -> p k b r", b=GB)
                for u in range(4):
                    t, c = u // 2, u % 2
                    for b in range(2):
                        i = pool.tensor_tensor(kbd[:, u, b, :, :], bc(kv[:, c, 2 * t + b, :], 1, HC),
                                               bc(mask_h[:], 2, S), ALU.mult)
                    i.then_inc(s["l1_kbd"], 1)
                yield 31
                norm_rs(ve1, rs1, s["l1_ve"], s["l1_rs"], 2 * n + 2)
                yield 33
                hold(pool, s["l1_g2"], n + 1)
                pool.tensor_tensor(g1[:], g1[:], bc(bias1[:, :, bass.ds(GB * n, GB)], 3, S), ALU.add).then_inc(s["l1_b2"], 1)

            def stream2(n):
                yield 0
                reach(pool, s["l2_x3"], n)
                hold(pool, s["l1_x2"], n + 1)
                pool.tensor_copy(xr2[:], x2[:]).then_inc(s["l2_x"], 1)
                yield 3
                norm_rs(ve2, rs2, s["l2_ve"], s["l2_rs"], 2 * n + 1)
                yield 10
                pool.wait_ge(s["l2_kmax"], n + 1)
                kk = k2t[:].rearrange("p k b r -> p (k b) r")
                pool.tensor_tensor(kk, kk, bc(kmax[:], 2, S), ALU.add).then_inc(s["l2_ksub"], 1)
                yield 11
                pool.wait_ge(s["l2_qmax"], n + 1)
                qq = q2[:].rearrange("p t h d -> p (t h) d")
                pool.tensor_tensor(qq, qq, bc(qmax[:], 2, D), ALU.add).then_inc(s["l2_qsub"], 1)
                yield 25
                norm_rs(ve2, rs2, s["l2_ve"], s["l2_rs"], 2 * n + 2)
                yield 27
                hold(pool, s["l2_g"], n + 1)
                pool.tensor_tensor(h2[:], h2[:], bc(bias2[:, :, bass.ds(GB * n, GB)], 3, S), ALU.add).then_inc(s["l2_h"], 1)
                yield 30
                pool.wait_ge(s["l2_r"], n + 1)
                pool.tensor_tensor(s2[:].rearrange("p k (b r) -> p k b r", b=GB), h2[:], e2[:], ALU.mult).then_inc(s["l2_s"], 1)
                yield 34
                pool.wait_ge(s["l2_og"], n + 1)
                reach(pool, s["l3_x"], n)
                pool.tensor_tensor(x3[:], e2[:], xr2[:], ALU.add).then_inc(s["l2_x3"], 1)

            def stream3(n):
                yield 0
                reach(pool, s["l3_fin"], n)
                hold(pool, s["l2_x3"], n + 1)
                pool.tensor_copy(xr3[:], x3[:]).then_inc(s["l3_x"], 1)
                yield 4
                hold(pool, s["l3_sf"], n + 1)
                pool.tensor_copy(sfrep[:].rearrange("p k b h j -> p (k b) h j"),
                                 bc(sf[:].rearrange("p k b r -> p (k b) r")[:, :, 0:NG], 2, HQ)).then_inc(s["l3_rep"], 1)
                yield 6
                pool.wait_ge(s["l3_kt"], n + 1)
                for d in range(2):
                    for k in range(KC):
                        for b in range(GB):
                            i = pool.tensor_tensor(kbd3[:, d, k, b, :, :], bc(k3t[:, d, k, b, :], 1, HC),
                                                   bc(mask_h[:], 2, NG), ALU.mult)
                i.then_inc(s["l3_kbd"], 1)

            bodies(pool, stream1, stream2, stream3)

        @block.scalar
        def _(act):
            act.dma_start(cond_t[:], a["cond_t"].rearrange("(k p) b -> p k b", p=P)).then_inc(s["ld_c"], 16)
            act.dma_start(cond[:], a["cond"]).then_inc(s["ld_c"], 16)
            act.dma_start(vec[:], a["vec"]).then_inc(s["ld_c"], 16)
            act.dma_start(rowvec[:], a["rowvec"].rearrange("(o v) c -> o v c", o=1).to_broadcast([P, len(ROWVECS), C])
                          ).then_inc(s["ld_c"], 16)
            act.dma_start(ident[:], a["ident"]).then_inc(s["ld_c"], 16)
            act.dma_start(mask_h[:], a["mask_h"]).then_inc(s["ld_c"], 16)
            act.dma_start(mask_bd[:], a["mask_bd"]).then_inc(s["ld_c"], 16)
            act.dma_start(mask_q[:], a["mask_q"]).then_inc(s["ld_c"], 16)
            act.dma_start(w_label[:], a["w_label"].rearrange("(o l) -> o l", o=1).to_broadcast([P, L])).then_inc(s["ld_c"], 16)
            act.dma_start(b_label[:], a["b_label"].rearrange("(o l) -> o l", o=1).to_broadcast([P, 1])).then_inc(s["ld_c"], 16)
            act.dma_start(ones[:], a["ones"]).then_inc(s["ld_c"], 16)
            for i in range(len(FIRST_WEIGHTS)):
                act.dma_start(first_w[:, i, :, :], a["first_w"][i].rearrange("(k p) n -> p k n", p=P)).then_inc(s["ld_w"], 16)
            for i in range(len(WEIGHTS)):
                act.dma_start(w[:, i, :, :], a["w"][i].rearrange("(k p) n -> p k n", p=P)).then_inc(s["ld_w"], 16)
            act.wait_ge(s["pro_v"], 1)
            act.activation(lnr[:], cond[:], ACT.Ln).then_inc(s["pro_a"], 1)
            act.activation(esil[:], cond_t[:], ACT.Exp, scale=-1.0).then_inc(s["pro_a"], 1)

            def stream1(n):
                yield 6
                act.wait_ge(s["l1_q"], n + 1)
                for k in range(KC):
                    i = act.activation(q1t[:, k, :], bA[:, k * GR:(k + 1) * GR], ACT.Identity, bias=V("L1bq", k))
                i.then_inc(s["l1_qt"], 1)
                act.wait_ge(s["l1_k"], n + 1)
                for k in range(KC):
                    i = act.activation(k1t[:, k, :], bE[:, k * GR:(k + 1) * GR], ACT.Identity, bias=V("L1bk", k))
                i.then_inc(s["l1_kt"], 1)
                for u in range(4):
                    yield 10 + 4 * u
                    act.wait_ge(s["l1_sub"], 4 * n + u + 1)
                    pv = prob[:, u % 2, :, :]
                    act.activation(pv, pv, ACT.Exp).then_inc(s["l1_p"], 1)
                    yield 12 + 4 * u
                    act.wait_ge(s["l1_pt"], 4 * n + u + 1)
                    act.activation(probt[:, u % 2, :, :], bT[:].rearrange("p (j r) -> p j r", r=P), ACT.Copy).then_inc(s["l1_pts"], 1)
                yield 28
                act.wait_ge(s["l1_ot"], n + 1)
                act.activation(ot[:], bA[:].rearrange("p (k r) -> p k r", k=KC), ACT.Copy).then_inc(s["l1_ots"], 1)

            def stream2(n):
                yield 5
                act.wait_ge(s["l2_zt"], n + 1)
                for k in range(KC):
                    i = act.activation(xn[:, k, :], bX[:, k * GR:(k + 1) * GR], ACT.Identity, bias=V("L2norm_b", k),
                                       scale=V("L2norm_g", k))
                i.then_inc(s["l2_xn"], 1)
                yield 7
                act.wait_ge(s["l2_k"], n + 1)
                for k in range(KC):
                    i = act.activation(k2t[:, k, :, :], bX[:, k * GR:(k + 1) * GR].rearrange("p (b r) -> p b r", b=GB),
                                       ACT.Identity, bias=V("L2bk", k))
                i.then_inc(s["l2_kt"], 1)
                yield 11
                act.wait_ge(s["l2_ksub"], n + 1)
                act.activation(k2t[:], k2t[:], ACT.Exp).then_inc(s["l2_ke"], 1)
                yield 12
                act.wait_ge(s["l2_qsub"], n + 1)
                act.activation(q2[:], q2[:], ACT.Exp).then_inc(s["l2_qe"], 1)
                yield 15
                act.wait_ge(s["l2_ekt"], n + 1)
                act.activation(ekrow[:], bX[:].rearrange("p (t c) -> p t c", t=2), ACT.Copy).then_inc(s["l2_ek"], 1)
                act.wait_ge(s["l2_eqt"], n + 1)
                act.activation(eqt[:], bY[:].rearrange("p (k r) -> p k r", k=KC), ACT.Copy).then_inc(s["l2_eq"], 1)
                yield 28
                act.wait_ge(s["l2_h"], n + 1)
                act.activation(e2[:], h2[:], ACT.Exp, scale=-1.0).then_inc(s["l2_e"], 1)

            def stream3(n):
                yield 5
                act.wait_ge(s["l3_q"], n + 1)
                for d, bk in enumerate((b0, b1)):
                    for k in range(KC):
                        i = act.activation(q3t[:, d, k, :], bk[:, k * GR:(k + 1) * GR], ACT.Identity,
                                           bias=q0b[:, d, k:k + 1], scale=0.25)
                i.then_inc(s["l3_qt"], 1)
                act.wait_ge(s["l3_k"], n + 1)
                for d in range(2):
                    for k in range(KC):
                        at = (d * KC + k) * GB * NG
                        i = act.activation(k3t[:, d, k, :, :], b2[:, at:at + GB * NG].rearrange("p (b j) -> p b j", b=GB),
                                           ACT.Identity, bias=V(f"L3bk{d}", k))
                i.then_inc(s["l3_kt"], 1)
                for u in range(4):
                    yield 17 + 4 * u
                    act.wait_ge(s["l3_sub"], 4 * n + u + 1)
                    act.activation(z3[:, u % 2], z3[:, u % 2], ACT.Exp).then_inc(s["l3_p"], 1)
                    yield 19 + 4 * u
                    act.wait_ge(s["l3_pt"], 4 * n + u + 1)
                    act.activation(p3t[:, u % 2, :, :], b2[0:KQ, :].rearrange("p (j r) -> p j r", r=P), ACT.Copy).then_inc(s["l3_pts"], 1)

            bodies(act, stream1, stream2, stream3)

        @block.tensor
        def _(pe):
            def project_t(bk, name, rhs, done, cols=None, at=0):
                nn = GR if cols is None else cols
                for mh in range(KC):
                    for k in range(KC):
                        i = pe.matmul(bk[:, at + mh * nn:at + (mh + 1) * nn], W(name, k, mh * P, mh * P + P), rhs(k),
                                      start=(k == 0), stop=(k == KC - 1))
                if done is not None:
                    i.then_inc(done, 1)

            def project_row(bk, name, src, done):
                for t in range(2):
                    for k in range(KC):
                        i = pe.matmul(bk[:, t * C:(t + 1) * C], src[:, k, t * P:(t + 1) * P], W(name, k, 0, C),
                                      start=(k == 0), stop=(k == KC - 1))
                i.then_inc(done, 1)

            def swap(bk, src, done):
                for x in range(2):
                    for y in range(2):
                        i = pe.transpose(bk[:, (y * 2 + x) * P:(y * 2 + x + 1) * P], src[:, x, y * P:(y + 1) * P], ident[:])
                i.then_inc(done, 1)

            def flat(t):
                return t[:].rearrange("p k b r -> p k (b r)")

            pe.wait_ge(s["ld_c"], 16 * 11)
            pe.wait_ge(s["ld_w"], 16 * (len(FIRST_WEIGHTS) + len(WEIGHTS)))
            rhs = lambda k: cond_t[:, k, :]
            project_t(b0, "L1g", rhs, None, B, 0)
            project_t(b0, "L1b", rhs, None, B, 128)
            project_t(b0, "L3sq", rhs, s["pro_pe"], B, 256)
            pe.wait_ge(s["pro_g"], 1)
            project_t(b1, "L2scale", lambda k: fsil[:, k, :], None, B, 0)
            project_t(b1, "L2shift", lambda k: fsil[:, k, :], s["pro_pe"], B, 128)
            pe.wait_ge(s["pro_v"], 2)
            for k in range(KC):
                i = pe.transpose(bX[0:B, k * P:(k + 1) * P], score_t[:, k, :], ident[:])
            i.then_inc(s["pro_pe"], 1)
            pe.wait_ge(s["pro_v"], 3)
            for k in range(KC):
                i = pe.transpose(bY[:, k * B:(k + 1) * B], keepm[:, k * P:(k + 1) * P], ident[0:B, 0:B])
            i.then_inc(s["pro_pe"], 1)

            def stream1(n):
                yield 2
                pe.wait_ge(s["l1_x1"], n + 1)
                reach(pe, s["l1_g2"], n)
                swap(bA, flat(x1), s["l1_row"])
                yield 4
                pe.wait_ge(s["l1_z"], 2 * n + 1)
                swap(bA, z1, s["l1_zt"])
                yield 6
                pe.wait_ge(s["l1_h"], n + 1)
                project_t(bA, "L1q", lambda k: ht[:, k, :], s["l1_q"])
                reach(pe, s["l1_sub"], 4 * n)
                project_t(bE, "L1k", lambda k: ht[:, k, :], s["l1_k"])
                reach(pe, s["l1_pts"], 4 * n)

                project_row(bT, "L1v", ht, s["l1_v"])

                def energies(u):
                    t, c = u // 2, u % 2
                    pe.wait_ge(s["l1_kbd"], 4 * n + u + 1)
                    if u == 0:
                        pe.wait_ge(s["l1_kt"], n + 1)
                    else:
                        pe.wait_ge(s["l1_sub"], 4 * n + u)
                    for b in range(2):
                        i = pe.matmul(bE[64 * b:64 * b + 64, :], q1t[:, c, (2 * t + b) * S:(2 * t + b + 1) * S],
                                      kbd[:, u, b, :, :].rearrange("p h r -> p (h r)"), start=True, stop=True)
                    i.then_inc(s["l1_e"], 1)
                for u in range(4):
                    t = u // 2
                    yield 9 + 4 * u
                    energies(u)
                    yield 11 + 4 * u
                    pe.wait_ge(s["l1_p"], 4 * n + u + 1)
                    if u == 0:
                        pe.wait_ge(s["l1_vs"], n + 1)
                    else:
                        pe.wait_ge(s["l1_pts"], 4 * n + u)
                    for j in range(HC // 2):
                        i = pe.transpose(bT[:, j * P:(j + 1) * P],
                                         prob[:, u % 2, 2 * j:2 * j + 2, :].rearrange("p h r -> p (h r)"), ident[:])
                    i.then_inc(s["l1_pt"], 1)
                    yield 13 + 4 * u
                    pe.wait_ge(s["l1_pts"], 4 * n + u + 1)
                    if u == 0:
                        pe.wait_ge(s["l1_qt"], n + 1)
                    elif u == 2:
                        pe.wait_ge(s["l1_o"], 2 * n + 1)
                    c = u % 2
                    for b in range(2):
                        for j in range(HC // 2):
                            at = (c * HC + 2 * j) * (D + 1)
                            i = pe.matmul(bA[64 * b:64 * b + 64, at:at + 2 * (D + 1)],
                                          probt[:, u % 2, j, 64 * b:64 * b + 64],
                                          vbd[:, 2 * t + b, c * (HC // 2) + j, :, :].rearrange("p h d -> p (h d)"),
                                          start=True, stop=True)
                    i.then_inc(s["l1_av"], 1)
                yield 27
                pe.wait_ge(s["l1_o"], 2 * n + 2)
                swap(bA, orow, s["l1_ot"])
                yield 29
                pe.wait_ge(s["l1_ots"], n + 1)
                project_t(bA, "L1p", lambda k: ot[:, k, :], s["l1_wp"])
                yield 30
                pe.wait_ge(s["l1_h1"], n + 1)
                swap(bA, flat(h1), s["l1_row2"])
                yield 32
                pe.wait_ge(s["l1_z"], 2 * n + 2)
                swap(bA, z1, s["l1_zt2"])

            def stream2(n):
                yield 2
                pe.wait_ge(s["l2_x"], n + 1)
                reach(pe, s["l2_og"], n)
                swap(bX, flat(xr2), s["l2_row"])
                yield 4
                pe.wait_ge(s["l2_z"], n + 1)
                swap(bX, z2, s["l2_zt"])
                yield 6
                pe.wait_ge(s["l2_xn"], n + 1)
                reach(pe, s["l2_yr"], n)
                project_t(bX, "L2k", lambda k: xn[:, k, :], s["l2_k"])
                project_row(bY, "L2q", xn, s["l2_q"])
                yield 8
                pe.wait_ge(s["l2_kt"], n + 1)
                project_row(bX, "L2v", xn, s["l2_v"])
                yield 14
                pe.wait_ge(s["l2_vs"], n + 1)
                pe.wait_ge(s["l2_ke"], n + 1)
                swap(bX, flat(k2t), s["l2_ekt"])
                pe.wait_ge(s["l2_qe"], n + 1)
                swap(bY, q2[:].rearrange("p t h d -> p t (h d)"), s["l2_eqt"])
                yield 16
                pe.wait_ge(s["l2_ek"], n + 1)
                pe.wait_ge(s["l2_eq"], n + 1)
                for t, bk in enumerate((bX, bY)):
                    for c in range(KC):
                        i = pe.matmul(bk[:, c * 256:(c + 1) * 256], ekrow[:, t, c * P:(c + 1) * P],
                                      vsep[:, 2 * t + c, :, :].rearrange("p b d -> p (b d)"), start=True, stop=True)
                i.then_inc(s["l2_ctx"], 1)
                yield 20
                pe.wait_ge(s["l2_ctxs"], n + 1)
                for t, bk in enumerate((bX, bY)):
                    for c in range(KC):
                        i = pe.matmul(bk[:, c * 256:(c + 1) * 256], eqt[:, c, t * P:(t + 1) * P],
                                      ctxbd[:, t, c, :, :].rearrange("p b d -> p (b d)"), start=True, stop=True)
                i.then_inc(s["l2_y"], 1)
                yield 26
                pe.wait_ge(s["l2_yz"], n + 1)
                swap(bX, z2, s["l2_yt"])
                yield 31
                pe.wait_ge(s["l2_s"], n + 1)
                project_t(bX, "L2o", lambda k: s2[:, k, :], s["l2_o"])

            def stream3(n):
                yield 2
                pe.wait_ge(s["l3_x"], n + 1)
                reach(pe, s["l3_r"], n)
                project_t(b0, "L3s", lambda k: flat(xr3)[:, k, :], None)
                for k in range(KC):
                    i = pe.matmul(b1[:, 0:GR], ones[:], flat(xr3)[:, k, :], start=(k == 0), stop=(k == KC - 1))
                i.then_inc(s["l3_sfp"], 1)
                yield 4
                pe.wait_ge(s["l3_sf"], n + 1)
                project_t(b0, "L3q0", lambda k: flat(sf)[:, k, :], None)
                project_t(b1, "L3q1", lambda k: flat(sf)[:, k, :], s["l3_q"])
                reach(pe, s["l3_o"], 4 * n)
                for d in range(2):
                    project_t(b2, f"L3k{d}", lambda k: sf[:, k, :, 0:NG], s["l3_k"] if d else None, GB * NG, d * KC * GB * NG)

                def values(b, bk):
                    for d in range(2):
                        for k in range(KC):
                            i = pe.matmul(bk[0:KQ, d * C:(d + 1) * C], sfrep[:, k, b, :, :].rearrange("p h j -> p (h j)"), W(f"L3o{d}", k, 0, C),
                                          start=(k == 0), stop=(k == KC - 1))
                    i.then_inc(s["l3_v"], 1)
                yield 7
                pe.wait_ge(s["l3_kt"], n + 1)
                pe.wait_ge(s["l3_rep"], n + 1)
                values(0, b0)
                values(1, b1)
                values(2, b2)
                yield 9
                pe.wait_ge(s["l3_vs"], 4 * n + 1)
                values(3, b0)
                for u in range(4):
                    t, d = u // 2, u % 2
                    yield 15 + 4 * u
                    if u == 0:
                        pe.wait_ge(s["l3_kbd"], n + 1)
                        pe.wait_ge(s["l3_vs"], 4 * n + 4)
                    else:
                        pe.wait_ge(s["l3_z"], 4 * n + u)
                    for c, bk in enumerate((b0, b1)):
                        i = pe.matmul(bk[:, 0:2 * HC * NG], q3t[:, d, c, t * P:(t + 1) * P],
                                      kbd3[:, d, c, 2 * t:2 * t + 2, :, :].rearrange("p b h j -> p (b h j)"),
                                      start=True, stop=True)
                    i.then_inc(s["l3_aff"], 1)
                    yield 18 + 4 * u
                    pe.wait_ge(s["l3_p"], 4 * n + u + 1)
                    if u > 0:
                        pe.wait_ge(s["l3_o"], 4 * n + u)
                    for j in range(4):
                        i = pe.transpose(b2[0:KQ, j * P:(j + 1) * P],
                                         z3[:, u % 2, HQ * j:HQ * j + HQ, :].rearrange("p h j -> p (h j)"), ident[:])
                    i.then_inc(s["l3_pt"], 1)
                    yield 20 + 4 * u
                    pe.wait_ge(s["l3_pts"], 4 * n + u + 1)
                    for b in range(2):
                        for j in range(4):
                            at = j * HQ * (D + 1)
                            i = pe.matmul(b2[64 * b:64 * b + 64, at:at + HQ * (D + 1)], p3t[:, u % 2, j, 64 * b:64 * b + 64],
                                          vbd3[:, 2 * t + b, d, HQ * j:HQ * j + HQ, :].rearrange("p h d -> p (h d)"),
                                          start=True, stop=True)
                    i.then_inc(s["l3_av"], 1)
                yield 34
                pe.wait_ge(s["l3_sum"], n + 1)
                swap(b0, atts, s["l3_at"])

            bodies(pe, stream1, stream2, stream3)

        @block.vector
        def _(dve):
            own = sem("own")
            count = [0]

            def link(i):
                count[0] += 1
                i.then_inc(own, 1)
                dve.wait_ge(own, count[0])

            dve.wait_ge(s["ld_c"], 16 * 11)
            dve.tensor_scalar(work[:], cond[:], P_KEEP, None, ALU.is_lt).then_inc(own, 1)
            count[0] += 1
            dve.wait_ge(own, count[0])
            dve.tensor_scalar(cond[:], cond[:], 1e-18, None, ALU.max).then_inc(s["pro_v"], 1)
            dve.wait_ge(s["pro_a"], 2)
            link(dve.tensor_scalar(esil[:], esil[:], 1.0, None, ALU.add))
            link(dve.reciprocal(esil[:], esil[:]))
            dve.tensor_tensor(fsil[:], cond_t[:], esil[:], ALU.mult).then_inc(s["pro_g"], 1)
            dve.wait_ge(s["pro_pe"], 1)

            def part(bk, at):
                return bk[:, at:at + KC * B].rearrange("p (k b) -> p k b", k=KC)

            def chan(name):
                return bc(V(name), 2, B)
            link(dve.tensor_tensor(gain1[:], part(b0, 0), chan("L1bg"), ALU.add))
            link(dve.tensor_tensor(bias1[:], gain1[:], chan("L1ln_b"), ALU.mult))
            link(dve.tensor_tensor(gain1[:], gain1[:], chan("L1ln_g"), ALU.mult))
            link(dve.tensor_tensor(bias1[:], part(b0, 128), bias1[:], ALU.add))
            link(dve.tensor_tensor(bias1[:], bias1[:], chan("L1bb"), ALU.add))
            link(dve.tensor_copy(qself[:], part(b0, 256)))
            dve.wait_ge(s["pro_pe"], 2)
            link(dve.tensor_tensor(gain2[:], part(b1, 0), chan("L2scale_b"), ALU.add))
            link(dve.tensor_scalar(gain2[:], gain2[:], 1.0, None, ALU.add))
            link(dve.tensor_tensor(bias2[:], gain2[:], chan("L2sn_b"), ALU.mult))
            link(dve.tensor_tensor(gain2[:], gain2[:], chan("L2sn_g"), ALU.mult))
            link(dve.tensor_tensor(bias2[:], part(b1, 128), bias2[:], ALU.add))
            link(dve.tensor_tensor(bias2[:], bias2[:], chan("L2shift_b"), ALU.add))
            for d in range(2):
                link(dve.tensor_scalar(q0b[:, d, :], V(f"L3bq{d}"), 0.25, None, ALU.mult))
            link(dve.tensor_tensor(bout[:], V("L3bout0"), V("L3bout1"), ALU.add))
            q = B // 4
            for p_ in range(4):
                dve.wait_ge(PARTS[p_], 16)
                for k in range(KC):
                    link(dve.tensor_reduce(score_t[:, k, p_ * q:(p_ + 1) * q], x_all[:, k, p_ * q:(p_ + 1) * q, :], AX.X, ALU.add))
            dve.tensor_scalar(score_t[:], score_t[:], 1.0 / S, None, ALU.mult).then_inc(s["pro_v"], 1)
            dve.wait_ge(s["pro_pe"], 3)
            link(dve.tensor_copy(score[:], bX[0:B, 0:C]))
            link(dve.reciprocal(lkey[:], score[:]))
            link(dve.tensor_tensor(lkey[:], lkey[:], lnr[:], ALU.mult))
            link(dve.tensor_scalar(lkey[:], lkey[:], LOG_MIN, LOG_MAX, ALU.max, ALU.min))
            link(dve.tensor_copy(keepm[:], lkey[:]))
            for r in range(KEEP // 8):
                link(dve.max(top8[:], keepm[:]))
                if r < KEEP // 8 - 1:
                    link(dve.match_replace(keepm[:], top8[:], keepm[:], -1e30))
            link(dve.tensor_scalar(keepm[:], lkey[:], top8[:, 7:8], None, ALU.is_ge))
            link(dve.tensor_tensor(lkey[:], keepm[:], score[:], ALU.mult))
            link(dve.tensor_reduce(sums[:, 0:1], lkey[:], AX.X, ALU.add))
            link(dve.tensor_reduce(sums[:, 1:2], score[:], AX.X, ALU.add))
            link(dve.reciprocal(sums[:, 2:3], sums[:, 0:1]))
            link(dve.tensor_tensor(sums[:, 3:4], sums[:, 2:3], sums[:, 1:2], ALU.mult))
            link(dve.tensor_tensor(keepm[:], keepm[:], work[:], ALU.mult))
            dve.tensor_scalar(keepm[:], keepm[:], sums[:, 3:4], None, ALU.mult).then_inc(s["pro_v"], 1)
            dve.wait_ge(s["pro_pe"], 4)
            link(dve.tensor_copy(mask_t[:], part(bY, 0)))
            dve.wait_ge(s["zeros"], 6)

            def norm(src, z, st, mv, ve, rs, prefix, c, s_z):
                s_st, s_mv, s_ve, s_rs = (s[prefix + x] for x in ("_st", "_mv", "_ve", "_rs"))
                for t in range(2):
                    i = dve.bn_stats(st[:, t, :], src(t))
                i.then_inc(s_st, 1)
                hold(dve, s_st, c)
                for t in range(2):
                    i = dve.bn_aggr(mv[:, t, :], st[:, t, :])
                i.then_inc(s_mv, 1)
                dve.wait_ge(s_mv, c)
                dve.tensor_scalar(ve[:], mv[:, :, 1], EPS, None, ALU.add).then_inc(s_ve, 1)
                dve.wait_ge(s_rs, c)
                for t in range(2):
                    i = dve.tensor_scalar(z[:, t, :], src(t), mv[:, t, 0:1], rs[:, t:t + 1], ALU.subtract, ALU.mult)
                i.then_inc(s_z, 1)

            def grp(bk):
                return bk[:].rearrange("p (k b r) -> p k b r", k=KC, b=GB)

            def stream1(n):
                at = bass.ds(GB * n, GB)
                yield 1
                dve.tensor_tensor(x1[:], x_all[:, :, at, :], bc(mask_t[:, :, at], 3, S), ALU.mult).then_inc(s["l1_x1"], 1)
                yield 3
                dve.wait_ge(s["l1_row"], n + 1)
                norm(lambda t: bA[:, t * C:(t + 1) * C], z1, st1, mv1, ve1, rs1, "l1", 2 * n + 1, s["l1_z"])
                yield 5
                dve.wait_ge(s["l1_zt"], n + 1)
                dve.tensor_tensor(g1[:], grp(bA), bc(gain1[:, :, at], 3, S), ALU.mult).then_inc(s["l1_g"], 1)
                yield 8
                dve.wait_ge(s["l1_v"], n + 1)
                for b in range(GB):
                    for j in range(2):
                        lo = 64 * (b % 2)
                        src = bT[lo:lo + 64, (b // 2) * C:(b // 2 + 1) * C].rearrange("p (g h d) -> p g h d", h=2, d=D)
                        add = rowvec[lo:lo + 64, 0, :].rearrange("p (g h d) -> p g h d", h=2, d=D)
                        i = dve.tensor_tensor(vbd[64 * j:64 * j + 64, b, :, j, 0:D], src[:, :, j, :], add[:, :, j, :], ALU.add)
                i.then_inc(s["l1_vs"], 1)
                for u in range(4):
                    yield 10 + 4 * u
                    c = 4 * n + u + 1
                    dve.wait_ge(s["l1_e"], c)
                    e = bE[:].rearrange("p (h r) -> p h r", h=HC)
                    dve.tensor_reduce(nmax1[:, u % 2, :], e, AX.X, ALU.max, negate=True).then_inc(s["l1_max"], 1)
                    dve.wait_ge(s["l1_max"], c)
                    if u >= 2 or not isinstance(n, int) or n > 0:
                        dve.wait_ge(s["l1_pt"], c - 2)
                    dve.tensor_tensor(prob[:, u % 2, :, :], e, bc(nmax1[:, u % 2, :], 2, S), ALU.add).then_inc(s["l1_sub"], 1)
                    if u % 2:
                        t = u // 2
                        yield 14 + 4 * u
                        dve.wait_ge(s["l1_av"], c)
                        o = bA[:, 0:H * (D + 1)].rearrange("p (h d) -> p h d", h=H)
                        dve.reciprocal(rec1[:], o[:, :, D]).then_inc(s["l1_rec"], 1)
                        dve.wait_ge(s["l1_rec"], 2 * n + t + 1)
                        dve.scalar_tensor_tensor(orow[:, t, :].rearrange("p (h d) -> p h d", h=H), o[:, :, 0:D],
                                                 1.0 / C ** 0.5, bc(rec1[:], 2, D), ALU.mult, ALU.mult).then_inc(s["l1_o"], 1)
                yield 30
                dve.wait_ge(s["l1_wp"], n + 1)
                for k in range(KC):
                    i = dve.scalar_tensor_tensor(h1[:, k].rearrange("p b r -> p (b r)"), bA[:, k * GR:(k + 1) * GR],
                                                 V("L1bp", k), x1[:, k].rearrange("p b r -> p (b r)"), ALU.add, ALU.add)
                i.then_inc(s["l1_h1"], 1)
                yield 31
                dve.wait_ge(s["l1_row2"], n + 1)
                norm(lambda t: bA[:, t * C:(t + 1) * C], z1, st1, mv1, ve1, rs1, "l1", 2 * n + 2, s["l1_z"])
                yield 33
                dve.wait_ge(s["l1_zt2"], n + 1)
                dve.tensor_tensor(g1[:], grp(bA), bc(gain1[:, :, at], 3, S), ALU.mult).then_inc(s["l1_g2"], 1)
                yield 34
                dve.wait_ge(s["l1_b2"], n + 1)
                reach(dve, s["l2_x"], n)
                dve.tensor_tensor(x2[:], g1[:], h1[:], ALU.add).then_inc(s["l1_x2"], 1)

            def stream2(n):
                at = bass.ds(GB * n, GB)
                yield 3
                dve.wait_ge(s["l2_row"], n + 1)
                norm(lambda t: bX[:, t * C:(t + 1) * C], z2, st2, mv2, ve2, rs2, "l2", 2 * n + 1, s["l2_z"])
                yield 8
                dve.wait_ge(s["l2_kt"], n + 1)
                kk = k2t[:].rearrange("p k b r -> p (k b) r")
                dve.tensor_reduce(kmax[:], kk, AX.X, ALU.max, negate=True).then_inc(s["l2_kmax"], 1)
                yield 9
                dve.wait_ge(s["l2_q"], n + 1)
                qq = q2[:].rearrange("p t h d -> p (t h) d")
                dve.tensor_tensor(q2[:].rearrange("p t h d -> p t (h d)"), bY[:].rearrange("p (t c) -> p t c", t=2),
                                  bc(rowvec[:, 1, :], 1, 2), ALU.add).then_inc(s["l2_qb"], 1)
                dve.wait_ge(s["l2_qb"], n + 1)
                dve.tensor_reduce(qmax[:], qq, AX.X, ALU.max, negate=True).then_inc(s["l2_qmax"], 1)
                yield 10
                dve.wait_ge(s["l2_v"], n + 1)
                for b in range(2):
                    lo, hi = 64 * b, 64 * b + 64
                    src = bX[lo:hi, :].rearrange("p (t c d) -> p t c d", t=2, c=KC)
                    add = bc(rowvec[lo:hi, 2, :].rearrange("p (c d) -> p c d", c=KC), 1, 2)
                    i = dve.tensor_tensor(vsep[lo:hi, :, b, :].rearrange("p (t c) d -> p t c d", t=2), src, add, ALU.add)
                i.then_inc(s["l2_vs"], 1)
                yield 13
                dve.wait_ge(s["l2_ke"], n + 1)
                dve.tensor_reduce(krec[:], kk, AX.X, ALU.add).then_inc(s["l2_ksum"], 1)
                dve.wait_ge(s["l2_ksum"], n + 1)
                dve.reciprocal(krec[:], krec[:]).then_inc(s["l2_krec"], 1)
                dve.wait_ge(s["l2_qe"], n + 1)
                dve.tensor_reduce(qrec[:].rearrange("p t h -> p (t h)"), qq, AX.X, ALU.add).then_inc(s["l2_qsum"], 1)
                dve.wait_ge(s["l2_qsum"], n + 1)
                dve.reciprocal(qrec[:], qrec[:]).then_inc(s["l2_qrec"], 1)
                yield 17
                dve.wait_ge(s["l2_krec"], n + 1)
                dve.wait_ge(s["l2_ctx"], n + 1)
                for t, bk in enumerate((bX, bY)):
                    for c in range(KC):
                        for b in range(2):
                            g = c * GB + 2 * t + b
                            i = dve.scalar_tensor_tensor(ctxbd[:, t, c, b, :], bk[:, (2 * c + b) * P:(2 * c + b + 1) * P],
                                                         krec[:, g:g + 1], mask_bd[:], ALU.mult, ALU.mult)
                i.then_inc(s["l2_ctxs"], 1)
                yield 21
                dve.wait_ge(s["l2_qrec"], n + 1)
                dve.wait_ge(s["l2_y"], n + 1)
                for t, bk in enumerate((bX, bY)):
                    for b in range(2):
                        lo, hi = 64 * b, 64 * b + 64
                        for c in range(KC):
                            i = dve.tensor_tensor(yrow[lo:hi, t, c * P:(c + 1) * P].rearrange("p (h d) -> p h d", d=D),
                                                  bk[lo:hi, (2 * c + b) * P:(2 * c + b + 1) * P].rearrange("p (h d) -> p h d", d=D),
                                                  bc(qrec[lo:hi, t, c * HC:(c + 1) * HC], 2, D), ALU.mult)
                i.then_inc(s["l2_yr"], 1)
                dve.wait_ge(s["l2_yr"], n + 1)
                norm(lambda t: yrow[:, t, :], z2, st2, mv2, ve2, rs2, "l2", 2 * n + 2, s["l2_yz"])
                yield 27
                dve.wait_ge(s["l2_yt"], n + 1)
                dve.tensor_tensor(h2[:], grp(bX), bc(gain2[:, :, at], 3, S), ALU.mult).then_inc(s["l2_g"], 1)
                yield 29
                dve.wait_ge(s["l2_e"], n + 1)
                dve.tensor_scalar(e2[:], e2[:], 1.0, None, ALU.add).then_inc(s["l2_e1"], 1)
                dve.wait_ge(s["l2_e1"], n + 1)
                dve.reciprocal(e2[:], e2[:]).then_inc(s["l2_r"], 1)
                yield 32
                dve.wait_ge(s["l2_o"], n + 1)
                for k in range(KC):
                    i = dve.scalar_tensor_tensor(e2[:, k], grp(bX)[:, k], V("L2out_b", k), bc(cond_t[:, k, at], 2, S),
                                                 ALU.add, ALU.mult)
                i.then_inc(s["l2_og"], 1)

            def stream3(n):
                at = bass.ds(GB * n, GB)
                yield 3
                dve.wait_ge(s["l3_sfp"], n + 1)
                for k in range(KC):
                    i = dve.scalar_tensor_tensor(nzq[:, k], b1[:, 0:GR].rearrange("p (b r) -> p b r", b=GB), 0.0,
                                                 bc(qself[:, k, at], 2, S), ALU.not_equal, ALU.mult)
                i.then_inc(s["l3_nz"], 1)
                dve.wait_ge(s["l3_nz"], n + 1)
                for k in range(KC):
                    i = dve.scalar_tensor_tensor(sf[:, k].rearrange("p b r -> p (b r)"), b0[:, k * GR:(k + 1) * GR],
                                                 V("L3b_self", k), nzq[:, k].rearrange("p b r -> p (b r)"), ALU.add, ALU.add)
                i.then_inc(s["l3_sf"], 1)
                yield 5
                dve.wait_ge(s["l3_adj"], 32 * (n + 1))
                av = adj[:].rearrange("p q (j l) -> p (q j) l", l=L)
                wv = adjw[:].rearrange("p q (j l) -> p (q j) l", l=L)
                dve.tensor_tensor(wv, av, bc(w_label[:], 1, 4 * NG), ALU.mult).then_inc(s["l3_aw"], 1)
                dve.tensor_reduce(cnt[:].rearrange("p q j -> p (q j)"), av, AX.X, ALU.add).then_inc(s["l3_cnt"], 1)
                dve.wait_ge(s["l3_aw"], n + 1)
                dve.tensor_reduce(vb[:].rearrange("p q j -> p (q j)"), wv, AX.X, ALU.add).then_inc(s["l3_vb"], 1)
                dve.wait_ge(s["l3_cnt"], n + 1)
                dve.tensor_scalar(cnt[:], cnt[:], 0.0, NEG, ALU.is_le, ALU.mult).then_inc(s["l3_t0"], 1)
                dve.wait_ge(s["l3_vb"], n + 1)
                dve.wait_ge(s["l3_t0"], 2 * n + 1)
                dve.tensor_scalar(vb[:], vb[:], b_label[:, 0:1], None, ALU.add).then_inc(s["l3_t0"], 1)
                dve.wait_ge(s["l3_t0"], 2 * n + 2)
                dve.tensor_tensor(tmask[:], cnt[:], vb[:], ALU.add).then_inc(s["l3_t"], 1)
                for b, bk in enumerate((b0, b1, b2, b0)):
                    yield 8 + b
                    dve.wait_ge(s["l3_v"], 4 * n + b + 1)
                    for d in range(2):
                        i = dve.tensor_tensor(vbd3[:, b, d, :, 0:D].rearrange("p (q h) d -> p q h d", h=HQ),
                                              bk[0:KQ, d * C:(d + 1) * C].rearrange("p (q h d) -> p q h d", h=HQ, d=D),
                                              bc(bc(mask_q[:], 1, 4), 3, D), ALU.mult)
                    i.then_inc(s["l3_vs"], 1)
                for u in range(4):
                    t, d = u // 2, u % 2
                    c = 4 * n + u + 1
                    yield 16 + 4 * u
                    if u == 0:
                        dve.wait_ge(s["l3_t"], n + 1)
                    dve.wait_ge(s["l3_aff"], c)
                    if u >= 2 or not isinstance(n, int) or n > 0:
                        dve.wait_ge(s["l3_pt"], c - 2)
                    for k, bk in enumerate((b0, b1)):
                        for b in range(2):
                            lo, hi = 64 * b, 64 * b + 64
                            i = dve.tensor_tensor(z3[lo:hi, u % 2, k * HC:(k + 1) * HC, :],
                                                  bk[lo:hi, b * HC * NG:(b + 1) * HC * NG].rearrange("p (h j) -> p h j", h=HC),
                                                  bc(tmask[lo:hi, 2 * d + t, :], 1, HC), ALU.add)
                    i.then_inc(s["l3_z"], 1)
                    dve.wait_ge(s["l3_z"], c)
                    dve.tensor_reduce(max3[:, u % 2, :], z3[:, u % 2], AX.X, ALU.max, negate=True).then_inc(s["l3_max"], 1)
                    dve.wait_ge(s["l3_max"], c)
                    dve.tensor_tensor(z3[:, u % 2], z3[:, u % 2], bc(max3[:, u % 2, :], 2, NG), ALU.add).then_inc(s["l3_sub"], 1)
                    yield 21 + 4 * u
                    dve.wait_ge(s["l3_av"], c)
                    o = b2[:, 0:H * (D + 1)].rearrange("p (h d) -> p h d", h=H)
                    dve.reciprocal(rec3[:, u % 2, :], o[:, :, D]).then_inc(s["l3_rec"], 1)
                    dve.wait_ge(s["l3_rec"], c)
                    dve.tensor_tensor(att[:, t, d, :].rearrange("p (h d) -> p h d", h=H), o[:, :, 0:D],
                                      bc(rec3[:, u % 2, :], 2, D), ALU.mult).then_inc(s["l3_o"], 1)
                yield 33.5
                dve.wait_ge(s["l3_o"], 4 * n + 4)
                dve.tensor_tensor(atts[:], att[:, :, 0, :], att[:, :, 1, :], ALU.add).then_inc(s["l3_sum"], 1)
                yield 35
                dve.wait_ge(s["l3_at"], n + 1)
                for k in range(KC):
                    i = dve.scalar_tensor_tensor(nzq[:, k].rearrange("p b r -> p (b r)"), b0[:, k * GR:(k + 1) * GR],
                                                 bout[:, k:k + 1], sf[:, k].rearrange("p b r -> p (b r)"), ALU.add, ALU.add)
                i.then_inc(s["l3_r"], 1)
                dve.wait_ge(s["l3_r"], n + 1)
                reach(dve, s["l3_out"], 16 * n)
                dve.scalar_tensor_tensor(fin[:].rearrange("p k b r -> p (k b r)"), nzq[:].rearrange("p k b r -> p (k b r)"),
                                         0.0, xr3[:].rearrange("p k b r -> p (k b r)"), ALU.max, ALU.add).then_inc(s["l3_fin"], 1)

            bodies(dve, stream1, stream2, stream3)


def kernel(**inputs):
    import numpy as np
    import concourse.bacc as bacc
    from concourse.bass_utils import run_bass_kernel_spmd

    i = {k: np.asarray(v) for k, v in inputs.items()}
    wqkv = i["L1_cond_Wqkv"].reshape(H, D, 3, C)
    bqkv = i["L1_cond_bqkv"].reshape(H, D, 3)
    l1w = [wqkv[:, :, j, :].reshape(C, C).T for j in range(3)]
    l1b = [bqkv[:, :, j].reshape(C) for j in range(3)]
    first = [i["L1_cond_Wg"].T, i["L1_cond_Wb"].T, i["L2_cond_emb_W"][:, :C], i["L2_cond_emb_W"][:, C:],
             i["L3_cond_W_self"][:, C:].T]
    weights = [*l1w, i["L1_cond_Wp"].T,
               i["L2_cond_Wq"], i["L2_cond_Wk"], i["L2_cond_Wv"], i["L2_cond_out_W"],
               i["L3_cond_W_self"][:, :C].T,
               i["L3_cond_Wq"][0].T, i["L3_cond_Wq"][1].T, i["L3_cond_Wk"][0].T, i["L3_cond_Wk"][1].T,
               i["L3_cond_Wout"][0].reshape(C, C).T, i["L3_cond_Wout"][1].reshape(C, C).T]
    vectors = [i["L1_cond_ln_g"], i["L1_cond_ln_b"], i["L1_cond_bg"], i["L1_cond_bb"], l1b[0], l1b[1], i["L1_cond_bp"],
               i["L2_cond_norm_g"], i["L2_cond_norm_b"], i["L2_cond_bk"], i["L2_cond_emb_b"][:C], i["L2_cond_emb_b"][C:],
               i["L2_cond_sn_g"], i["L2_cond_sn_b"], i["L2_cond_out_b"], i["L3_cond_b_self"],
               i["L3_cond_bq"][0], i["L3_cond_bq"][1], i["L3_cond_bk"][0], i["L3_cond_bk"][1],
               i["L3_cond_bout"][0], i["L3_cond_bout"][1]]
    adj = i["mask_BxSxSx11_ik0"]
    at = np.arange(P)
    arrays = {
        "x_t": i["x"].reshape(B * S, C).T,
        "cond": i["cond_1024"], "cond_t": i["cond_1024"].T,
        "first_w": np.stack(first), "w": np.stack(weights),
        "vec": np.stack(vectors).reshape(len(VECTORS), KC, P).transpose(2, 0, 1),
        "rowvec": np.stack([l1b[2], i["L2_cond_bq"], i["L2_cond_bv"]]),
        "ident": np.eye(P, dtype=np.float32), "ones": np.ones((P, P), np.float32),
        "mask_h": (at[:, None] // D == np.arange(HC)).astype(np.float32),
        "mask_bd": (at[:, None] // D == at // D).astype(np.float32),
        "mask_q": (np.arange(KQ)[:, None] // NG == np.arange(HQ)).astype(np.float32),
        "w_label": i["L3_cond_w_bias"], "b_label": i["L3_cond_b_bias"].reshape(1),
        "adj": np.stack([adj[:, :, :NG, :].reshape(B * S, NG * L),
                         adj[:, :NG, :, :].transpose(0, 2, 1, 3).reshape(B * S, NG * L)]),
    }
    nc = bacc.Bacc("TRN2", target_bir_lowering=False, num_devices=1)
    feeds, aps = {}, {}
    for name, v in arrays.items():
        v = np.ascontiguousarray(v)
        feeds[f"in_{name}"] = v
        aps[name] = nc.dram_tensor(f"in_{name}", v.shape, mybir.dt.from_np(v.dtype), kind="ExternalInput").ap()
    out = nc.dram_tensor("out_t", (C, B * S), F32, kind="ExternalOutput").ap()
    build(nc, aps, out)
    r = run_bass_kernel_spmd(nc, [feeds], core_ids=[0])
    return np.ascontiguousarray(r.results[0]["out_t"].T).reshape(B, S, C)
```

```python
from contextlib import ExitStack

import concourse.bass as bass
from concourse import mybir

P = 128
B, S, C = 64, 64, 256
H, D = 16, 16
KC = C // P
GB = 4
GR = GB * S
GROUPS = B // GB
HC = H // KC
NG, L = 20, 11
HQ = 4
KQ = HQ * NG
EPS = 1e-5
NEG = -9000000000000000.0
ORDER = {
    "sp": "333",
    "pool": "120320232032313322132",
    "act": "23123233131021121013201213332331323",
    "pe": "12310123332101113011201121231231333133230313323",
    "dve": "10233012011231221232133133232103123",
}
KEEP = C // 2
P_KEEP = 0.9
LOG_MIN, LOG_MAX = -103.972, 88.7229

F32 = mybir.dt.float32
I32 = mybir.dt.int32
ALU = mybir.AluOpType
ACT = mybir.ActivationFunctionType
AX = mybir.AxisListType

FIRST_WEIGHTS = ["L1g", "L1b", "L2scale", "L2shift", "L3sq"]
WEIGHTS = ["L1q", "L1k", "L1v", "L1p", "L2q", "L2k", "L2v", "L2o", "L3s", "L3q0", "L3q1", "L3k0", "L3k1", "L3o0", "L3o1"]
VECTORS = ["L1ln_g", "L1ln_b", "L1bg", "L1bb", "L1bq", "L1bk", "L1bp", "L2norm_g", "L2norm_b", "L2bk",
           "L2scale_b", "L2shift_b", "L2sn_g", "L2sn_b", "L2out_b", "L3b_self", "L3bq0", "L3bq1",
           "L3bk0", "L3bk1", "L3bout0", "L3bout1"]
ROWVECS = ["L1bv", "L2bq", "L2bv"]


def bc(ap, axis, n):
    a = ap.unsqueeze(axis)
    shape = list(a.shape)
    shape[axis] = n
    return a.to_broadcast(shape)


def reach(eng, sem, value, wait=None):
    if isinstance(value, int) and value <= 0:
        return
    if wait is None:
        eng.wait_ge(sem, value)
    else:
        wait(eng, sem, value)


def turns(order, streams):
    for f in streams.values():
        next(f)
    for k in order:
        if int(k) in streams:
            next(streams[int(k)], None)


def build(nc, a, out):
    ctx = ExitStack()
    with ctx:
        def sb(name, shape, dt=F32):
            return ctx.enter_context(nc.sbuf_tensor(name, shape, dt))

        def bank(name):
            return ctx.enter_context(nc.psum_tensor(name, [P, 512], F32))

        def sem(name):
            return ctx.enter_context(nc.semaphore(name))

        w = sb("w", [P, len(WEIGHTS), KC, C])
        vec = sb("vec", [P, len(VECTORS), KC])
        rowvec = sb("rowvec", [P, len(ROWVECS), C])
        ident = sb("ident", [P, P])
        ones = sb("ones", [P, P])
        mask_h = sb("mask_h", [P, HC])
        mask_bd = sb("mask_bd", [P, P])
        mask_q = sb("mask_q", [KQ, HQ])
        w_label = sb("w_label", [P, L])
        b_label = sb("b_label", [P, 1])
        neg_half = sb("neg_half", [P, 2])

        def W(name, k, lo, hi):
            if name in FIRST_WEIGHTS:
                return first_w[:, FIRST_WEIGHTS.index(name), k, lo:hi]
            return w[:, WEIGHTS.index(name), k, lo:hi]

        def V(name, k=None):
            i = VECTORS.index(name)
            return vec[:, i, :] if k is None else vec[:, i, k:k + 1]

        cond_t = sb("cond_t", [P, KC, B])
        mask_t = sb("mask_t", [P, KC, B])
        gain1 = sb("gain1", [P, KC, B])
        bias1 = sb("bias1", [P, KC, B])
        gain2 = sb("gain2", [P, KC, B])
        bias2 = sb("bias2", [P, KC, B])
        qself = sb("qself", [P, KC, B])
        q0b = sb("q0b", [P, 2, KC])
        bout = sb("bout", [P, KC])

        x_all = sb("x_all", [P, KC, B, S])
        score_t = sb("score_t", [P, KC, B])
        top8 = sb("top8", [B, 8])
        sums = sb("sums", [B, 4])

        x1 = sb("x1", [P, KC, GB, S])
        z0 = sb("z0", [P, 2, C])
        z1 = sb("z1", [P, 2, C])
        x1b = sb("x1b", [P, KC, GB, S])
        ht = sb("ht", [P, KC, GR])
        g1 = sb("g1", [P, KC, GB, S])
        q1t = sb("q1t", [P, KC, GR])
        k1t = sb("k1t", [P, KC, GR])
        kbd = sb("kbd", [P, 4, 2, HC, S])
        vbd = sb("vbd", [P, GB, H // 2, 2, D + 1])
        prob = sb("prob", [P, 2, HC, S])
        probt = sb("probt", [P, 2, HC // 2, P])
        nmax1 = sb("nmax1", [P, 2, HC])
        rec1 = sb("rec1", [P, H])
        orow = sb("orow", [P, 2, C])
        ot = sb("ot", [P, KC, GR])
        h1 = sb("h1", [P, KC, GB, S])
        x2 = sb("x2", [P, KC, GB, S])
        st1, mv1, ve1, rs1, nm1 = (sb(x, [P, 2, *y]) for x, y in (("st1", (6,)), ("mv1", (2,)), ("ve1", ()), ("rs1", ()), ("nm1", ())))
        xr2 = sb("xr2", [P, KC, GB, S])
        z2 = sb("z2", [P, 2, C])
        xn = sb("xn", [P, KC, GR])
        k2t = sb("k2t", [P, KC, GB, S])
        ekrow = sb("ekrow", [P, 2, C])
        vsep = sb("vsep", [P, 4, 2, P])
        kmax = sb("kmax", [P, KC * GB])
        krec = sb("krec", [P, KC * GB])
        q2 = sb("q2", [P, 2, H, D])
        qmax = sb("qmax", [P, 2 * H])
        qrec = sb("qrec", [P, 2, H])
        eqt = sb("eqt", [P, KC, GR])
        ctxbd = sb("ctxbd", [P, 2, KC, 2, P])
        yrow = sb("yrow", [P, 2, C])
        h2 = sb("h2", [P, KC, GB, S])
        e2 = sb("e2", [P, KC, GB, S])
        s2 = sb("s2", [P, KC, GR])
        x3 = sb("x3", [P, KC, GB, S])
        st2, mv2, ve2, rs2, nm2 = (sb(x, [P, 2, *y]) for x, y in (("st2", (6,)), ("mv2", (2,)), ("ve2", ()), ("rs2", ()), ("nm2", ())))
        st0, mv0, ve0, rs0, nm0 = (sb(x, [P, 2, *y]) for x, y in (("st0", (6,)), ("mv0", (2,)), ("ve0", ()), ("rs0", ()), ("nm0", ())))
        xr3 = sb("xr3", [P, KC, GB, S])
        nzq = sb("nzq", [P, KC, GB, S])
        sf = sb("sf", [P, KC, GB, S])
        q3t = sb("q3t", [P, 2, KC, GR])
        k3t = sb("k3t", [P, 2, KC, GB, NG])
        kbd3 = sb("kbd3", [P, 2, KC, GB, HC, NG])
        vrow = sb("vrow", [P, 2, C])
        vbd3 = sb("vbd3", [KQ, GB, 2, H, D + 1])
        adj = sb("adj", [P, 4, NG * L], I32)
        adjw = sb("adjw", [P, 4, NG * L])
        cnt = sb("cnt", [P, 4, NG])
        vb = sb("vb", [P, 4, NG])
        tmask = sb("tmask", [P, 4, NG])
        z3 = sb("z3", [P, 2, H, NG])
        max3 = sb("max3", [P, 2, H])
        p3t = sb("p3t", [KQ, 2, 4, P])
        rec3 = sb("rec3", [P, 2, H])
        att = sb("att", [P, 2, C])
        att1 = sb("att1", [P, C])
        fin = sb("fin", [P, KC, GB, S])

        spare = kbd[:].rearrange("p u b h r -> p (u b h r)")
        cond, score, lnr, lkey, work, keepm = (spare[0:B, j * C:(j + 1) * C] for j in range(6))
        esil, fsil = (spare[:, 6 * C + j * KC * B:6 * C + (j + 1) * KC * B].rearrange("p (k b) -> p k b", k=KC) for j in range(2))
        first_w = kbd3[:].rearrange("p d k b h j -> p (d k b h j)").rearrange("p (w k n) -> p w k n", k=KC, n=C)

        bZ, bA, bE, bT = bank("bZ"), bank("bA"), bank("bE"), bank("bT")
        bX, bY = bank("bX"), bank("bY")
        b0, b1 = bank("b0"), bank("b1")

        names = """held zeros ld_c ld_fw ld_w ld_x ld_x2 ld_x3 ld_x4 pro_v pro_pe pro_a pro_g own
        n0_st n0_mv n0_ve n0_rs n0_nm n0_z n1_st n1_mv n1_ve n1_rs n1_nm n1_z n2_st n2_mv n2_ve n2_rs n2_nm n2_z
        l0_x l0_row l0_zt l0_g l0_h l0_q l0_qt l0_k l0_kt l0_v l0_vs l0_kbd
        l1_e l1_max l1_sub l1_p l1_pt l1_pts l1_av l1_rec l1_o l1_ot l1_ots l1_wp l1_xb l1_h1 l1_row l1_zt l1_g l1_b l1_x2
        l2_x l2_row l2_zt l2_xn l2_k l2_kt l2_kmax l2_ksub l2_ke l2_ksum l2_krec l2_kd l2_q l2_qb
        l2_qmax l2_qsub l2_qe l2_qsum l2_qrec l2_v l2_vs l2_ekt l2_ek l2_eqt l2_eq l2_ctx l2_ctxs l2_y l2_yr
        l2_yt l2_g l2_h l2_e l2_r l2_s l2_o l2_og l2_x3
        l3_x l3_sfp l3_nz l3_sf l3_q l3_qt l3_k l3_kt l3_kbd l3_v l3_vr l3_vd l3_adj l3_aw l3_cnt l3_vb l3_t0 l3_t l3_aff
        l3_z l3_max l3_sub l3_p l3_pt l3_pts l3_av l3_rec l3_o l3_sum l3_at l3_r l3_fin l3_out""".split()
        s = {name: sem(name) for name in names}


        block = ctx.enter_context(nc.Block())
        PARTS = [s["ld_x"], s["ld_x2"], s["ld_x3"], s["ld_x4"]]
        out_v = out.rearrange("(k p) r -> p k r", p=P)

        def hold(eng, sem_, value):
            eng.wait_ge(sem_, value)
            eng.sem_inc(s["held"], 1)

        def own(bk):
            return bk[:].rearrange("p (k b r) -> p k b r", k=KC, b=GB)

        def bodies(eng, order, streams):
            last = 3

            def turn(i, has):
                turns(order, {k: f(i - k) for k, f in streams.items() if has(k)})
            for i in range(last + 1):
                turn(i, lambda k: i >= k)
            with eng.Fori(last + 1, GROUPS) as i:
                turn(i, lambda k: True)
            for i in range(GROUPS, GROUPS + last):
                turn(i, lambda k: i - k < GROUPS)

        @block.sync
        def _(sp):
            for part in range(4):
                n = B // 4
                sp.dma_start(x_all[:, :, part * n:(part + 1) * n, :],
                             a["x_t"].rearrange("(k p) (b r) -> p k b r", p=P, r=S)[:, :, part * n:(part + 1) * n, :]
                             ).then_inc(PARTS[part], 16)

            def stream3(n):
                yield
                reach(sp, s["l3_cnt"], n, hold)
                for d in range(2):
                    sp.dma_start(adj[:, 2 * d:2 * d + 2, :],
                                 a["adj"][d].rearrange("(t p) e -> p t e", p=P)[:, bass.ds(2 * n, 2), :]
                                 ).then_inc(s["l3_adj"], 16)
                yield
                hold(sp, s["l3_vr"], n + 1)
                reach(sp, s["l3_av"], 4 * n)
                for b in range(GB):
                    for h in range(HQ):
                        sp.dma_start(vbd3[NG * h:NG * h + NG, b].rearrange("p d (q h) e -> p (d q) h e", h=HQ)[:, :, h, 0:D],
                                     vrow[32 * b:32 * b + NG].rearrange("p d (q h e) -> p (d q) h e", h=HQ, e=D)[:, :, h, :]
                                     ).then_inc(s["l3_vd"], 16)
                yield
                hold(sp, s["l3_fin"], n + 1)
                sp.dma_start(out_v[:, :, bass.ds(GR * n, GR)], fin[:, :, :, :].rearrange("p k b r -> p k (b r)")
                             ).then_inc(s["l3_out"], 16)

            bodies(sp, ORDER["sp"], {3: stream3})
            sp.wait_ge(s["l3_out"], 16 * GROUPS)

        @block.gpsimd
        def _(pool):
            pool.memset(neg_half[:], -0.5).then_inc(s["zeros"], 1)
            pool.memset(vbd[:], 0.0).then_inc(s["zeros"], 1)
            pool.memset(vsep[:], 0.0).then_inc(s["zeros"], 1)
            pool.memset(vbd3[:], 0.0).then_inc(s["zeros"], 1)
            pool.wait_ge(s["zeros"], 4)
            for j in range(2):
                pool.memset(vbd[64 * j:64 * j + 64, :, :, j, D:D + 1], 1.0).then_inc(s["zeros"], 1)
                pool.wait_ge(s["zeros"], 5 + j)
            pool.wait_ge(s["ld_c"], 16 * 11)
            for b in range(GB):
                for d in range(2):
                    i = pool.tensor_copy(vbd3[:, b, d, :, D].rearrange("p (q h) -> p q h", h=HQ), bc(mask_q[:], 1, 4))
            i.then_inc(s["zeros"], 1)

            def norm_scale(ve, rs, nm, name, count):
                pool.wait_ge(s[name + "_ve"], count)
                pool.tensor_tensor(rs[:], ve[:], neg_half[:], ALU.pow).then_inc(s[name + "_rs"], 1)
                pool.wait_ge(s[name + "_rs"], count)
                pool.tensor_tensor(nm[:], nm[:], rs[:], ALU.mult).then_inc(s[name + "_nm"], 1)

            def stream0(n):
                yield
                norm_scale(ve0, rs0, nm0, "n0", n + 1)
                yield
                hold(pool, s["l0_g"], n + 1)
                hv = ht[:].rearrange("p k (b r) -> p k b r", b=GB)
                pool.tensor_tensor(hv, hv, bc(bias1[:, :, bass.ds(GB * n, GB)], 3, S), ALU.add).then_inc(s["l0_h"], 1)
                yield
                reach(pool, s["l1_e"], 4 * n)
                pool.wait_ge(s["l0_kt"], n + 1)
                kv = k1t[:].rearrange("p k (b r) -> p k b r", b=GB)
                for u in range(4):
                    t, c = u // 2, u % 2
                    pool.tensor_tensor(kbd[:, u], bc(kv[:, c, 2 * t:2 * t + 2, :], 2, HC),
                                       bc(bc(mask_h[:], 2, S), 1, 2), ALU.mult).then_inc(s["l0_kbd"], 1)

            def stream1(n):
                yield
                reach(pool, s["l1_h1"], n, hold)
                at = bass.ds(GB * n, GB)
                pool.tensor_tensor(x1b[:], x_all[:, :, at, :], bc(mask_t[:, :, at], 3, S), ALU.mult).then_inc(s["l1_xb"], 1)
                yield
                norm_scale(ve1, rs1, nm1, "n1", n + 1)
                yield
                hold(pool, s["l1_g"], n + 1)
                pool.tensor_tensor(g1[:], g1[:], bc(bias1[:, :, bass.ds(GB * n, GB)], 3, S), ALU.add).then_inc(s["l1_b"], 1)

            def stream2(n):
                yield
                norm_scale(ve2, rs2, nm2, "n2", 2 * n + 1)
                yield
                pool.wait_ge(s["l2_kmax"], n + 1)
                kk = k2t[:].rearrange("p k b r -> p (k b) r")
                pool.tensor_tensor(kk, kk, bc(kmax[:], 2, S), ALU.add).then_inc(s["l2_ksub"], 1)
                yield
                pool.wait_ge(s["l2_qmax"], n + 1)
                qq = q2[:].rearrange("p t h d -> p (t h) d")
                pool.tensor_tensor(qq, qq, bc(qmax[:], 2, D), ALU.add).then_inc(s["l2_qsub"], 1)
                yield
                pool.wait_ge(s["l2_krec"], n + 1)
                pool.tensor_tensor(kk, kk, bc(krec[:], 2, S), ALU.mult).then_inc(s["l2_kd"], 1)
                yield
                norm_scale(ve2, rs2, nm2, "n2", 2 * n + 2)
                yield
                hold(pool, s["l2_g"], n + 1)
                pool.tensor_tensor(h2[:], h2[:], bc(bias2[:, :, bass.ds(GB * n, GB)], 3, S), ALU.add).then_inc(s["l2_h"], 1)
                yield
                pool.wait_ge(s["l2_r"], n + 1)
                pool.tensor_tensor(s2[:].rearrange("p k (b r) -> p k b r", b=GB), h2[:], e2[:], ALU.mult).then_inc(s["l2_s"], 1)
                yield
                reach(pool, s["l3_x"], n)
                pool.wait_ge(s["l2_og"], n + 1)
                pool.tensor_tensor(x3[:], e2[:], xr2[:], ALU.add).then_inc(s["l2_x3"], 1)

            def stream3(n):
                yield
                reach(pool, s["l3_aff"], 4 * n)
                pool.wait_ge(s["l3_kt"], n + 1)
                for d in range(2):
                    for k in range(KC):
                        pool.tensor_tensor(kbd3[:, d, k], bc(k3t[:, d, k], 2, HC), bc(bc(mask_h[:], 2, NG), 1, GB),
                                           ALU.mult).then_inc(s["l3_kbd"], 1)
                for u in range(4):
                    yield
                    pool.wait_ge(s["l3_max"], 4 * n + u + 1)
                    pool.tensor_tensor(z3[:, u % 2], z3[:, u % 2], bc(max3[:, u % 2, :], 2, NG), ALU.add).then_inc(s["l3_sub"], 1)
                    if u >= 2:
                        t = u - 2
                        yield
                        pool.wait_ge(s["l3_o"], 4 * n + 2 * t + 2)
                        pool.tensor_tensor(att[:, t, :], att[:, t, :], att1[:], ALU.add).then_inc(s["l3_sum"], 1)

            bodies(pool, ORDER["pool"], {0: stream0, 1: stream1, 2: stream2, 3: stream3})

        @block.scalar
        def _(act):
            act.dma_start(cond_t[:], a["cond_t"].rearrange("(k p) b -> p k b", p=P)).then_inc(s["ld_c"], 16)
            act.dma_start(cond[:], a["cond"]).then_inc(s["ld_c"], 16)
            act.dma_start(vec[:], a["vec"]).then_inc(s["ld_c"], 16)
            act.dma_start(rowvec[:], a["rowvec"].rearrange("(o v) c -> o v c", o=1).to_broadcast([P, len(ROWVECS), C])
                          ).then_inc(s["ld_c"], 16)
            act.dma_start(ident[:], a["ident"]).then_inc(s["ld_c"], 16)
            act.dma_start(mask_h[:], a["mask_h"]).then_inc(s["ld_c"], 16)
            act.dma_start(mask_bd[:], a["mask_bd"]).then_inc(s["ld_c"], 16)
            act.dma_start(mask_q[:], a["mask_q"]).then_inc(s["ld_c"], 16)
            act.dma_start(w_label[:], a["w_label"].rearrange("(o l) -> o l", o=1).to_broadcast([P, L])).then_inc(s["ld_c"], 16)
            act.dma_start(b_label[:], a["b_label"].rearrange("(o l) -> o l", o=1).to_broadcast([P, 1])).then_inc(s["ld_c"], 16)
            act.dma_start(ones[:], a["ones"]).then_inc(s["ld_c"], 16)
            for i in range(len(FIRST_WEIGHTS)):
                act.dma_start(first_w[:, i, :, :], a["first_w"][i].rearrange("(k p) n -> p k n", p=P)).then_inc(s["ld_fw"], 16)
            for i in range(len(WEIGHTS)):
                act.dma_start(w[:, i, :, :], a["w"][i].rearrange("(k p) n -> p k n", p=P)).then_inc(s["ld_w"], 16)
            act.wait_ge(s["pro_v"], 1)
            act.activation(lnr[:], cond[:], ACT.Ln).then_inc(s["pro_a"], 1)
            act.activation(esil[:], cond_t[:], ACT.Exp, scale=-1.0).then_inc(s["pro_a"], 1)

            def normalize(z, src, rs, nm, name, count):
                act.wait_ge(s[name + "_nm"], count)
                for t in range(2):
                    i = act.activation(z[:, t, :], src(t), ACT.Identity, bias=nm[:, t:t + 1], scale=rs[:, t:t + 1])
                i.then_inc(s[name + "_z"], 1)

            def stream0(n):
                yield
                normalize(z0, lambda t: bZ[:, t * C:(t + 1) * C], rs0, nm0, "n0", n + 1)
                yield
                reach(act, s["l1_e"], 4 * n)
                act.wait_ge(s["l0_q"], n + 1)
                for k in range(KC):
                    i = act.activation(q1t[:, k, :], bZ[:, k * GR:(k + 1) * GR], ACT.Identity, bias=V("L1bq", k))
                i.then_inc(s["l0_qt"], 1)
                yield
                act.wait_ge(s["l0_k"], n + 1)
                for k in range(KC):
                    i = act.activation(k1t[:, k, :], bZ[:, k * GR:(k + 1) * GR], ACT.Identity, bias=V("L1bk", k))
                i.then_inc(s["l0_kt"], 1)

            def stream1(n):
                for u in range(5):
                    if u < 4:
                        yield
                        act.wait_ge(s["l1_sub"], 4 * n + u + 1)
                        pv = prob[:, u % 2, :, :]
                        act.activation(pv, pv, ACT.Exp).then_inc(s["l1_p"], 1)
                        yield
                        act.wait_ge(s["l1_pt"], 4 * n + u + 1)
                        act.activation(probt[:, u % 2, :, :], bT[:].rearrange("p (j r) -> p j r", r=P), ACT.Copy).then_inc(s["l1_pts"], 1)
                yield
                act.wait_ge(s["l1_ot"], n + 1)
                act.activation(ot[:], bA[:].rearrange("p (k r) -> p k r", k=KC), ACT.Copy).then_inc(s["l1_ots"], 1)
                yield
                normalize(z1, lambda t: bA[:, t * C:(t + 1) * C], rs1, nm1, "n1", n + 1)

            def stream2(n):
                yield
                act.wait_ge(s["l1_x2"], n + 1)
                reach(act, s["l2_x3"], n)
                act.activation(xr2[:], x2[:], ACT.Copy).then_inc(s["l2_x"], 1)
                yield
                normalize(z2, lambda t: bX[:, t * C:(t + 1) * C], rs2, nm2, "n2", 2 * n + 1)
                yield
                act.wait_ge(s["l2_zt"], n + 1)
                for k in range(KC):
                    i = act.activation(xn[:, k, :], bX[:, k * GR:(k + 1) * GR], ACT.Identity, bias=V("L2norm_b", k),
                                       scale=V("L2norm_g", k))
                i.then_inc(s["l2_xn"], 1)
                yield
                act.wait_ge(s["l2_k"], n + 1)
                for k in range(KC):
                    i = act.activation(k2t[:, k, :, :], bX[:, k * GR:(k + 1) * GR].rearrange("p (b r) -> p b r", b=GB),
                                       ACT.Identity, bias=V("L2bk", k))
                i.then_inc(s["l2_kt"], 1)
                yield
                act.wait_ge(s["l2_ksub"], n + 1)
                act.activation(k2t[:], k2t[:], ACT.Exp).then_inc(s["l2_ke"], 1)
                yield
                act.wait_ge(s["l2_qsub"], n + 1)
                act.activation(q2[:], q2[:], ACT.Exp).then_inc(s["l2_qe"], 1)
                yield
                act.wait_ge(s["l2_ekt"], n + 1)
                act.activation(ekrow[:], bX[:].rearrange("p (t c) -> p t c", t=2), ACT.Copy).then_inc(s["l2_ek"], 1)
                act.wait_ge(s["l2_eqt"], n + 1)
                act.activation(eqt[:], bY[:].rearrange("p (k r) -> p k r", k=KC), ACT.Copy).then_inc(s["l2_eq"], 1)
                yield
                normalize(z2, lambda t: yrow[:, t, :], rs2, nm2, "n2", 2 * n + 2)
                yield
                act.wait_ge(s["l2_h"], n + 1)
                act.activation(e2[:], h2[:], ACT.Tanh, scale=0.5).then_inc(s["l2_e"], 1)

            def stream3(n):
                yield
                act.wait_ge(s["l2_x3"], n + 1)
                reach(act, s["l3_fin"], n)
                act.activation(xr3[:], x3[:], ACT.Copy).then_inc(s["l3_x"], 1)
                for d, bk in enumerate((b0, b1)):
                    yield
                    act.wait_ge(s["l3_q"], 2 * n + d + 1)
                    for k in range(KC):
                        i = act.activation(q3t[:, d, k, :], bk[:, k * GR:(k + 1) * GR], ACT.Identity,
                                           bias=q0b[:, d, k:k + 1], scale=0.25)
                    i.then_inc(s["l3_qt"], 1)
                yield
                act.wait_ge(s["l3_k"], n + 1)
                for d in range(2):
                    for k in range(KC):
                        at = (d * KC + k) * GB * NG
                        i = act.activation(k3t[:, d, k, :, :], b0[:, at:at + GB * NG].rearrange("p (b j) -> p b j", b=GB),
                                           ACT.Identity, bias=V(f"L3bk{d}", k))
                i.then_inc(s["l3_kt"], 1)
                yield
                act.wait_ge(s["l3_v"], n + 1)
                act.activation(vrow[:], b1[:].rearrange("p (d c) -> p d c", d=2), ACT.Copy).then_inc(s["l3_vr"], 1)
                for u in range(4):
                    yield
                    act.wait_ge(s["l3_sub"], 4 * n + u + 1)
                    act.activation(z3[:, u % 2], z3[:, u % 2], ACT.Exp).then_inc(s["l3_p"], 1)
                    yield
                    act.wait_ge(s["l3_pt"], 4 * n + u + 1)
                    act.activation(p3t[:, u % 2, :, :], b1[0:KQ, :].rearrange("p (j r) -> p j r", r=P), ACT.Copy).then_inc(s["l3_pts"], 1)

            bodies(act, ORDER["act"], {0: stream0, 1: stream1, 2: stream2, 3: stream3})

        @block.tensor
        def _(pe):
            def project_t(bk, name, rhs, done, cols=None, at=0):
                nn = GR if cols is None else cols
                for mh in range(KC):
                    for k in range(KC):
                        i = pe.matmul(bk[:, at + mh * nn:at + (mh + 1) * nn], W(name, k, mh * P, mh * P + P), rhs(k),
                                      start=(k == 0), stop=(k == KC - 1))
                if done is not None:
                    i.then_inc(done, 1)

            def project_row(bk, name, src, done):
                for t in range(2):
                    for k in range(KC):
                        i = pe.matmul(bk[:, t * C:(t + 1) * C], src[:, k, t * P:(t + 1) * P], W(name, k, 0, C),
                                      start=(k == 0), stop=(k == KC - 1))
                i.then_inc(done, 1)

            def swap(bk, src, done):
                for x in range(2):
                    for y in range(2):
                        i = pe.transpose(bk[:, (y * 2 + x) * P:(y * 2 + x + 1) * P], src[:, x, y * P:(y + 1) * P], ident[:])
                i.then_inc(done, 1)

            def flat(t):
                return t[:].rearrange("p k b r -> p k (b r)")

            pe.wait_ge(s["ld_c"], 16 * 11)
            pe.wait_ge(s["ld_fw"], 16 * len(FIRST_WEIGHTS))
            rhs = lambda k: cond_t[:, k, :]
            project_t(b0, "L1g", rhs, None, B, 0)
            project_t(b0, "L1b", rhs, None, B, 128)
            project_t(b0, "L3sq", rhs, s["pro_pe"], B, 256)
            pe.wait_ge(s["pro_g"], 1)
            project_t(b1, "L2scale", lambda k: fsil[:, k, :], None, B, 0)
            project_t(b1, "L2shift", lambda k: fsil[:, k, :], s["pro_pe"], B, 128)
            pe.wait_ge(s["pro_v"], 2)
            for k in range(KC):
                i = pe.transpose(bX[0:B, k * P:(k + 1) * P], score_t[:, k, :], ident[:])
            i.then_inc(s["pro_pe"], 1)
            pe.wait_ge(s["ld_w"], 16 * len(WEIGHTS))
            pe.wait_ge(s["pro_v"], 3)
            for k in range(KC):
                i = pe.transpose(bY[:, k * B:(k + 1) * B], keepm[:, k * P:(k + 1) * P], ident[0:B, 0:B])
            i.then_inc(s["pro_pe"], 1)

            def stream0(n):
                yield
                pe.wait_ge(s["l0_x"], n + 1)
                reach(pe, s["l0_vs"], n)
                swap(bZ, flat(x1), s["l0_row"])
                yield
                pe.wait_ge(s["n0_z"], n + 1)
                swap(bZ, z0, s["l0_zt"])
                yield
                pe.wait_ge(s["l0_h"], n + 1)
                project_t(bZ, "L1q", lambda k: ht[:, k, :], s["l0_q"])
                yield
                pe.wait_ge(s["l0_qt"], n + 1)
                project_t(bZ, "L1k", lambda k: ht[:, k, :], s["l0_k"])
                yield
                pe.wait_ge(s["l0_kt"], n + 1)
                project_row(bZ, "L1v", ht, s["l0_v"])

            def stream1(n):
                def energies(u):
                    t, c = u // 2, u % 2
                    pe.wait_ge(s["l0_kbd"], 4 * n + u + 1)
                    reach(pe, s["l1_sub"], 4 * n + u)
                    for b in range(2):
                        i = pe.matmul(bE[64 * b:64 * b + 64, :], q1t[:, c, (2 * t + b) * S:(2 * t + b + 1) * S],
                                      kbd[:, u, b, :, :].rearrange("p h r -> p (h r)"), start=True, stop=True)
                    i.then_inc(s["l1_e"], 1)

                def turn(u):
                    pe.wait_ge(s["l1_p"], 4 * n + u + 1)
                    reach(pe, s["l1_pts"], 4 * n + u)
                    for j in range(HC // 2):
                        i = pe.transpose(bT[:, j * P:(j + 1) * P],
                                         prob[:, u % 2, 2 * j:2 * j + 2, :].rearrange("p h r -> p (h r)"), ident[:])
                    i.then_inc(s["l1_pt"], 1)

                def weigh(u):
                    t, c = u // 2, u % 2
                    pe.wait_ge(s["l1_pts"], 4 * n + u + 1)
                    if u == 0:
                        pe.wait_ge(s["l0_vs"], n + 1)
                        reach(pe, s["l1_g"], n)
                    elif u == 2:
                        pe.wait_ge(s["l1_o"], 2 * n + 1)
                    for j in range(HC // 2):
                        for b in range(2):
                            at = (c * HC + 2 * j) * (D + 1)
                            i = pe.matmul(bA[64 * b:64 * b + 64, at:at + 2 * (D + 1)],
                                          probt[:, u % 2, j, 64 * b:64 * b + 64],
                                          vbd[:, 2 * t + b, c * (HC // 2) + j, :, :].rearrange("p h d -> p (h d)"),
                                          start=True, stop=True)
                    i.then_inc(s["l1_av"], 1)
                for u in range(5):
                    if u < 4:
                        yield
                        energies(u)
                    if u > 0:
                        yield
                        weigh(u - 1)
                    if u < 4:
                        yield
                        turn(u)
                yield
                pe.wait_ge(s["l1_o"], 2 * n + 2)
                swap(bA, orow, s["l1_ot"])
                yield
                pe.wait_ge(s["l1_ots"], n + 1)
                project_t(bA, "L1p", lambda k: ot[:, k, :], s["l1_wp"])
                yield
                pe.wait_ge(s["l1_h1"], n + 1)
                swap(bA, flat(h1), s["l1_row"])
                yield
                pe.wait_ge(s["n1_z"], n + 1)
                swap(bA, z1, s["l1_zt"])

            def stream2(n):
                yield
                pe.wait_ge(s["l2_x"], n + 1)
                reach(pe, s["l2_og"], n)
                swap(bX, flat(xr2), s["l2_row"])
                yield
                pe.wait_ge(s["n2_z"], 2 * n + 1)
                swap(bX, z2, s["l2_zt"])
                yield
                pe.wait_ge(s["l2_xn"], n + 1)
                project_t(bX, "L2k", lambda k: xn[:, k, :], s["l2_k"])
                project_row(bY, "L2q", xn, s["l2_q"])
                yield
                pe.wait_ge(s["l2_kt"], n + 1)
                project_row(bX, "L2v", xn, s["l2_v"])
                yield
                pe.wait_ge(s["l2_vs"], n + 1)
                pe.wait_ge(s["l2_kd"], n + 1)
                swap(bX, flat(k2t), s["l2_ekt"])
                pe.wait_ge(s["l2_qe"], n + 1)
                swap(bY, q2[:].rearrange("p t h d -> p t (h d)"), s["l2_eqt"])
                yield
                pe.wait_ge(s["l2_ek"], n + 1)
                pe.wait_ge(s["l2_eq"], n + 1)
                for t, bk in enumerate((bX, bY)):
                    for c in range(KC):
                        i = pe.matmul(bk[:, c * 256:(c + 1) * 256], ekrow[:, t, c * P:(c + 1) * P],
                                      vsep[:, 2 * t + c, :, :].rearrange("p b d -> p (b d)"), start=True, stop=True)
                    i.then_inc(s["l2_ctx"], 1)
                yield
                pe.wait_ge(s["l2_ctxs"], 2 * n + 2)
                for t in range(2):
                    for c in range(KC):
                        for b in range(2):
                            i = pe.matmul(bX[64 * b:64 * b + 64, (2 * t + c) * P:(2 * t + c + 1) * P],
                                          eqt[:, c, (2 * t + b) * S:(2 * t + b + 1) * S], ctxbd[:, t, c, b, :],
                                          start=True, stop=True)
                i.then_inc(s["l2_y"], 1)
                yield
                pe.wait_ge(s["n2_z"], 2 * n + 2)
                swap(bX, z2, s["l2_yt"])
                yield
                pe.wait_ge(s["l2_s"], n + 1)
                project_t(bX, "L2o", lambda k: s2[:, k, :], s["l2_o"])

            def stream3(n):
                yield
                pe.wait_ge(s["l3_x"], n + 1)
                reach(pe, s["l3_r"], n)
                project_t(b0, "L3s", lambda k: flat(xr3)[:, k, :], None)
                for k in range(KC):
                    i = pe.matmul(b1[:, 0:GR], ones[:], flat(xr3)[:, k, :], start=(k == 0), stop=(k == KC - 1))
                i.then_inc(s["l3_sfp"], 1)
                yield
                pe.wait_ge(s["l3_sf"], n + 1)
                project_t(b0, "L3q0", lambda k: flat(sf)[:, k, :], s["l3_q"])
                project_t(b1, "L3q1", lambda k: flat(sf)[:, k, :], s["l3_q"])
                yield
                pe.wait_ge(s["l3_qt"], 2 * n + 1)
                for d in range(2):
                    project_t(b0, f"L3k{d}", lambda k: sf[:, k, :, 0:NG], s["l3_k"] if d else None, GB * NG, d * KC * GB * NG)
                yield
                pe.wait_ge(s["l3_qt"], 2 * n + 2)
                o = WEIGHTS.index("L3o0")
                for k in range(KC):
                    for b in range(GB):
                        i = pe.matmul(b1[32 * b:32 * b + 32, :], sf[:, k, b, 0:32], w[:, o:o + 2, k, :],
                                      start=(k == 0), stop=(k == KC - 1))
                i.then_inc(s["l3_v"], 1)
                def affinities(u):
                    t, d = u // 2, u % 2
                    pe.wait_ge(s["l3_kbd"], 4 * n + 2 * d + 2)
                    reach(pe, s["l3_z"], 4 * n + u)
                    for c in range(KC):
                        for b in range(2):
                            i = pe.matmul(b0[64 * b:64 * b + 64, c * HC * NG:(c + 1) * HC * NG],
                                          q3t[:, d, c, (2 * t + b) * S:(2 * t + b + 1) * S],
                                          kbd3[:, d, c, 2 * t + b, :, :].rearrange("p h j -> p (h j)"),
                                          start=True, stop=True)
                    i.then_inc(s["l3_aff"], 1)

                def turn(u):
                    pe.wait_ge(s["l3_p"], 4 * n + u + 1)
                    if u == 0:
                        pe.wait_ge(s["l3_vr"], n + 1)
                    else:
                        pe.wait_ge(s["l3_o"], 4 * n + u)
                    for j in range(4):
                        i = pe.transpose(b1[0:KQ, j * P:(j + 1) * P],
                                         z3[:, u % 2, HQ * j:HQ * j + HQ, :].rearrange("p h j -> p (h j)"), ident[:])
                    i.then_inc(s["l3_pt"], 1)

                def weigh(u):
                    t, d = u // 2, u % 2
                    pe.wait_ge(s["l3_pts"], 4 * n + u + 1)
                    if u == 0:
                        pe.wait_ge(s["l3_vd"], 16 * GB * HQ * (n + 1))
                    for j in range(4):
                        for b in range(2):
                            at = j * HQ * (D + 1)
                            i = pe.matmul(b1[64 * b:64 * b + 64, at:at + HQ * (D + 1)], p3t[:, u % 2, j, 64 * b:64 * b + 64],
                                          vbd3[:, 2 * t + b, d, HQ * j:HQ * j + HQ, :].rearrange("p h d -> p (h d)"),
                                          start=True, stop=True)
                    i.then_inc(s["l3_av"], 1)
                for u in range(5):
                    if u < 4:
                        yield
                        affinities(u)
                    if u > 0:
                        yield
                        turn(u - 1)
                        yield
                        weigh(u - 1)
                yield
                pe.wait_ge(s["l3_sum"], 2 * n + 2)
                swap(b0, att, s["l3_at"])

            bodies(pe, ORDER["pe"], {0: stream0, 1: stream1, 2: stream2, 3: stream3})

        @block.vector
        def _(dve):
            count = [0]

            def link(i):
                count[0] += 1
                i.then_inc(s["own"], 1)
                dve.wait_ge(s["own"], count[0])

            dve.wait_ge(s["ld_c"], 16 * 11)
            dve.tensor_scalar(work[:], cond[:], P_KEEP, None, ALU.is_lt).then_inc(s["own"], 1)
            count[0] += 1
            dve.wait_ge(s["own"], count[0])
            dve.tensor_scalar(cond[:], cond[:], 1e-18, None, ALU.max).then_inc(s["pro_v"], 1)
            dve.wait_ge(s["pro_a"], 2)
            link(dve.tensor_scalar(esil[:], esil[:], 1.0, None, ALU.add))
            link(dve.reciprocal(esil[:], esil[:]))
            dve.tensor_tensor(fsil[:], cond_t[:], esil[:], ALU.mult).then_inc(s["pro_g"], 1)
            dve.wait_ge(s["pro_pe"], 1)

            def part(bk, at):
                return bk[:, at:at + KC * B].rearrange("p (k b) -> p k b", k=KC)

            def chan(name):
                return bc(V(name), 2, B)
            link(dve.tensor_tensor(gain1[:], part(b0, 0), chan("L1bg"), ALU.add))
            link(dve.tensor_tensor(bias1[:], gain1[:], chan("L1ln_b"), ALU.mult))
            link(dve.tensor_tensor(gain1[:], gain1[:], chan("L1ln_g"), ALU.mult))
            link(dve.tensor_tensor(bias1[:], part(b0, 128), bias1[:], ALU.add))
            link(dve.tensor_tensor(bias1[:], bias1[:], chan("L1bb"), ALU.add))
            link(dve.tensor_copy(qself[:], part(b0, 256)))
            dve.wait_ge(s["pro_pe"], 2)
            link(dve.tensor_tensor(gain2[:], part(b1, 0), chan("L2scale_b"), ALU.add))
            link(dve.tensor_scalar(gain2[:], gain2[:], 1.0, None, ALU.add))
            link(dve.tensor_tensor(bias2[:], gain2[:], chan("L2sn_b"), ALU.mult))
            link(dve.tensor_tensor(gain2[:], gain2[:], chan("L2sn_g"), ALU.mult))
            link(dve.tensor_tensor(bias2[:], part(b1, 128), bias2[:], ALU.add))
            link(dve.tensor_tensor(bias2[:], bias2[:], chan("L2shift_b"), ALU.add))
            for d in range(2):
                link(dve.tensor_scalar(q0b[:, d, :], V(f"L3bq{d}"), 0.25, None, ALU.mult))
            link(dve.tensor_tensor(bout[:], V("L3bout0"), V("L3bout1"), ALU.add))
            q = B // 4
            for p_ in range(4):
                dve.wait_ge(PARTS[p_], 16)
                for k in range(KC):
                    link(dve.tensor_reduce(score_t[:, k, p_ * q:(p_ + 1) * q], x_all[:, k, p_ * q:(p_ + 1) * q, :], AX.X, ALU.add))
            dve.tensor_scalar(score_t[:], score_t[:], 1.0 / S, None, ALU.mult).then_inc(s["pro_v"], 1)
            dve.wait_ge(s["pro_pe"], 3)
            link(dve.tensor_copy(score[:], bX[0:B, 0:C]))
            link(dve.reciprocal(lkey[:], score[:]))
            link(dve.tensor_tensor(lkey[:], lkey[:], lnr[:], ALU.mult))
            link(dve.tensor_scalar(lkey[:], lkey[:], LOG_MIN, LOG_MAX, ALU.max, ALU.min))
            link(dve.tensor_copy(keepm[:], lkey[:]))
            for r in range(KEEP // 8):
                link(dve.max(top8[:], keepm[:]))
                if r < KEEP // 8 - 1:
                    link(dve.match_replace(keepm[:], top8[:], keepm[:], -1e30))
            link(dve.tensor_scalar(keepm[:], lkey[:], top8[:, 7:8], None, ALU.is_ge))
            link(dve.tensor_tensor(lkey[:], keepm[:], score[:], ALU.mult))
            link(dve.tensor_reduce(sums[:, 0:1], lkey[:], AX.X, ALU.add))
            link(dve.tensor_reduce(sums[:, 1:2], score[:], AX.X, ALU.add))
            link(dve.reciprocal(sums[:, 2:3], sums[:, 0:1]))
            link(dve.tensor_tensor(sums[:, 3:4], sums[:, 2:3], sums[:, 1:2], ALU.mult))
            link(dve.tensor_tensor(keepm[:], keepm[:], work[:], ALU.mult))
            dve.tensor_scalar(keepm[:], keepm[:], sums[:, 3:4], None, ALU.mult).then_inc(s["pro_v"], 1)
            dve.wait_ge(s["pro_pe"], 4)
            link(dve.tensor_copy(mask_t[:], part(bY, 0)))
            dve.wait_ge(s["zeros"], 7)

            def norm(src, st, mv, ve, nm, name, c):
                for t in range(2):
                    i = dve.bn_stats(st[:, t, :], src(t))
                i.then_inc(s[name + "_st"], 1)
                hold(dve, s[name + "_st"], c)
                for t in range(2):
                    i = dve.bn_aggr(mv[:, t, :], st[:, t, :])
                i.then_inc(s[name + "_mv"], 1)
                dve.wait_ge(s[name + "_mv"], c)
                dve.tensor_scalar(nm[:], mv[:, :, 0], -1.0, None, ALU.mult)
                dve.tensor_scalar(ve[:], mv[:, :, 1], EPS, None, ALU.add).then_inc(s[name + "_ve"], 1)

            def stream0(n):
                at = bass.ds(GB * n, GB)
                yield
                dve.tensor_tensor(x1[:], x_all[:, :, at, :], bc(mask_t[:, :, at], 3, S), ALU.mult).then_inc(s["l0_x"], 1)
                yield
                dve.wait_ge(s["l0_row"], n + 1)
                norm(lambda t: bZ[:, t * C:(t + 1) * C], st0, mv0, ve0, nm0, "n0", n + 1)
                yield
                dve.wait_ge(s["l0_zt"], n + 1)
                dve.tensor_tensor(ht[:].rearrange("p k (b r) -> p k b r", b=GB), own(bZ), bc(gain1[:, :, at], 3, S),
                                  ALU.mult).then_inc(s["l0_g"], 1)
                yield
                reach(dve, s["l1_av"], 4 * n)
                dve.wait_ge(s["l0_v"], n + 1)
                for b in range(GB):
                    for j in range(2):
                        lo = 64 * (b % 2)
                        src = bZ[lo:lo + 64, (b // 2) * C:(b // 2 + 1) * C].rearrange("p (g h d) -> p g h d", h=2, d=D)
                        add = rowvec[lo:lo + 64, 0, :].rearrange("p (g h d) -> p g h d", h=2, d=D)
                        i = dve.tensor_tensor(vbd[64 * j:64 * j + 64, b, :, j, 0:D], src[:, :, j, :], add[:, :, j, :], ALU.add)
                i.then_inc(s["l0_vs"], 1)

            def stream1(n):
                at = bass.ds(GB * n, GB)
                for u in range(4):
                    yield
                    c = 4 * n + u + 1
                    dve.wait_ge(s["l1_e"], c)
                    e = bE[:].rearrange("p (h r) -> p h r", h=HC)
                    dve.tensor_reduce(nmax1[:, u % 2, :], e, AX.X, ALU.max, negate=True).then_inc(s["l1_max"], 1)
                    dve.wait_ge(s["l1_max"], c)
                    if u >= 2 or not isinstance(n, int) or n > 0:
                        dve.wait_ge(s["l1_pt"], c - 2)
                    dve.tensor_tensor(prob[:, u % 2, :, :], e, bc(nmax1[:, u % 2, :], 2, S), ALU.add).then_inc(s["l1_sub"], 1)
                    if u >= 2:
                        t = u - 2
                        yield
                        dve.wait_ge(s["l1_av"], 4 * n + 2 * t + 2)
                        o = bA[:, 0:H * (D + 1)].rearrange("p (h d) -> p h d", h=H)
                        dve.reciprocal(rec1[:], o[:, :, D]).then_inc(s["l1_rec"], 1)
                        dve.wait_ge(s["l1_rec"], 2 * n + t + 1)
                        dve.scalar_tensor_tensor(orow[:, t, :].rearrange("p (h d) -> p h d", h=H), o[:, :, 0:D],
                                                 1.0 / C ** 0.5, bc(rec1[:], 2, D), ALU.mult, ALU.mult).then_inc(s["l1_o"], 1)
                yield
                dve.wait_ge(s["l1_xb"], n + 1)
                dve.wait_ge(s["l1_wp"], n + 1)
                for k in range(KC):
                    i = dve.scalar_tensor_tensor(h1[:, k].rearrange("p b r -> p (b r)"), bA[:, k * GR:(k + 1) * GR],
                                                 V("L1bp", k), x1b[:, k].rearrange("p b r -> p (b r)"), ALU.add, ALU.add)
                i.then_inc(s["l1_h1"], 1)
                yield
                dve.wait_ge(s["l1_row"], n + 1)
                norm(lambda t: bA[:, t * C:(t + 1) * C], st1, mv1, ve1, nm1, "n1", n + 1)
                yield
                dve.wait_ge(s["l1_zt"], n + 1)
                dve.tensor_tensor(g1[:], own(bA), bc(gain1[:, :, at], 3, S), ALU.mult).then_inc(s["l1_g"], 1)
                yield
                reach(dve, s["l2_x"], n)
                dve.wait_ge(s["l1_b"], n + 1)
                dve.tensor_tensor(x2[:], g1[:], h1[:], ALU.add).then_inc(s["l1_x2"], 1)

            def stream2(n):
                at = bass.ds(GB * n, GB)
                yield
                dve.wait_ge(s["l2_row"], n + 1)
                norm(lambda t: bX[:, t * C:(t + 1) * C], st2, mv2, ve2, nm2, "n2", 2 * n + 1)
                yield
                dve.wait_ge(s["l2_kt"], n + 1)
                kk = k2t[:].rearrange("p k b r -> p (k b) r")
                dve.tensor_reduce(kmax[:], kk, AX.X, ALU.max, negate=True).then_inc(s["l2_kmax"], 1)
                yield
                dve.wait_ge(s["l2_q"], n + 1)
                qq = q2[:].rearrange("p t h d -> p (t h) d")
                dve.tensor_tensor(q2[:].rearrange("p t h d -> p t (h d)"), bY[:].rearrange("p (t c) -> p t c", t=2),
                                  bc(rowvec[:, 1, :], 1, 2), ALU.add).then_inc(s["l2_qb"], 1)
                dve.wait_ge(s["l2_qb"], n + 1)
                dve.tensor_reduce(qmax[:], qq, AX.X, ALU.max, negate=True).then_inc(s["l2_qmax"], 1)
                yield
                dve.wait_ge(s["l2_ke"], n + 1)
                dve.tensor_reduce(krec[:], kk, AX.X, ALU.add).then_inc(s["l2_ksum"], 1)
                dve.wait_ge(s["l2_ksum"], n + 1)
                dve.reciprocal(krec[:], krec[:]).then_inc(s["l2_krec"], 1)
                dve.wait_ge(s["l2_v"], n + 1)
                for b in range(2):
                    lo, hi = 64 * b, 64 * b + 64
                    src = bX[lo:hi, :].rearrange("p (t c d) -> p t c d", t=2, c=KC)
                    add = bc(rowvec[lo:hi, 2, :].rearrange("p (c d) -> p c d", c=KC), 1, 2)
                    i = dve.tensor_tensor(vsep[lo:hi, :, b, :].rearrange("p (t c) d -> p t c d", t=2), src, add, ALU.add)
                i.then_inc(s["l2_vs"], 1)
                yield
                dve.wait_ge(s["l2_qe"], n + 1)
                dve.tensor_reduce(qrec[:].rearrange("p t h -> p (t h)"), qq, AX.X, ALU.add).then_inc(s["l2_qsum"], 1)
                dve.wait_ge(s["l2_qsum"], n + 1)
                dve.reciprocal(qrec[:], qrec[:]).then_inc(s["l2_qrec"], 1)
                yield
                for t, bk in enumerate((bX, bY)):
                    dve.wait_ge(s["l2_ctx"], 2 * n + t + 1)
                    dve.tensor_tensor(ctxbd[:, t].rearrange("p c b d -> p (c b) d"), bk[:].rearrange("p (g d) -> p g d", d=P),
                                      bc(mask_bd[:], 1, 4), ALU.mult).then_inc(s["l2_ctxs"], 1)
                yield
                dve.wait_ge(s["l2_qrec"], n + 1)
                dve.wait_ge(s["l2_y"], n + 1)
                dve.tensor_tensor(yrow[:].rearrange("p t (h d) -> p (t h) d", d=D), bX[:].rearrange("p (h d) -> p h d", d=D),
                                  bc(qrec[:].rearrange("p t h -> p (t h)"), 2, D), ALU.mult).then_inc(s["l2_yr"], 1)
                hold(dve, s["l2_yr"], n + 1)
                norm(lambda t: yrow[:, t, :], st2, mv2, ve2, nm2, "n2", 2 * n + 2)
                yield
                dve.wait_ge(s["l2_yt"], n + 1)
                dve.tensor_tensor(h2[:], own(bX), bc(gain2[:, :, at], 3, S), ALU.mult).then_inc(s["l2_g"], 1)
                yield
                dve.wait_ge(s["l2_e"], n + 1)
                dve.tensor_scalar(e2[:], e2[:], 0.5, 0.5, ALU.mult, ALU.add).then_inc(s["l2_r"], 1)
                yield
                dve.wait_ge(s["l2_o"], n + 1)
                for k in range(KC):
                    i = dve.scalar_tensor_tensor(e2[:, k], own(bX)[:, k], V("L2out_b", k), bc(cond_t[:, k, at], 2, S),
                                                 ALU.add, ALU.mult)
                i.then_inc(s["l2_og"], 1)

            def stream3(n):
                at = bass.ds(GB * n, GB)
                yield
                dve.wait_ge(s["l3_sfp"], n + 1)
                for k in range(KC):
                    i = dve.scalar_tensor_tensor(nzq[:, k], b1[:, 0:GR].rearrange("p (b r) -> p b r", b=GB), 0.0,
                                                 bc(qself[:, k, at], 2, S), ALU.not_equal, ALU.mult)
                i.then_inc(s["l3_nz"], 1)
                dve.wait_ge(s["l3_nz"], n + 1)
                for k in range(KC):
                    i = dve.scalar_tensor_tensor(sf[:, k].rearrange("p b r -> p (b r)"), b0[:, k * GR:(k + 1) * GR],
                                                 V("L3b_self", k), nzq[:, k].rearrange("p b r -> p (b r)"), ALU.add, ALU.add)
                i.then_inc(s["l3_sf"], 1)
                yield
                dve.wait_ge(s["l3_adj"], 32 * (n + 1))
                av = adj[:].rearrange("p q (j l) -> p (q j) l", l=L)
                wv = adjw[:].rearrange("p q (j l) -> p (q j) l", l=L)
                dve.tensor_tensor(wv, av, bc(w_label[:], 1, 4 * NG), ALU.mult).then_inc(s["l3_aw"], 1)
                dve.tensor_reduce(cnt[:].rearrange("p q j -> p (q j)"), av, AX.X, ALU.add).then_inc(s["l3_cnt"], 1)
                dve.wait_ge(s["l3_aw"], n + 1)
                dve.tensor_reduce(vb[:].rearrange("p q j -> p (q j)"), wv, AX.X, ALU.add).then_inc(s["l3_vb"], 1)
                dve.wait_ge(s["l3_cnt"], n + 1)
                dve.tensor_scalar(cnt[:], cnt[:], 0.0, NEG, ALU.is_le, ALU.mult).then_inc(s["l3_t0"], 1)
                dve.wait_ge(s["l3_vb"], n + 1)
                dve.wait_ge(s["l3_t0"], 2 * n + 1)
                dve.tensor_scalar(vb[:], vb[:], b_label[:, 0:1], None, ALU.add).then_inc(s["l3_t0"], 1)
                dve.wait_ge(s["l3_t0"], 2 * n + 2)
                dve.tensor_tensor(tmask[:], cnt[:], vb[:], ALU.add).then_inc(s["l3_t"], 1)

                def divide(u):
                    t, d = u // 2, u % 2
                    dve.wait_ge(s["l3_av"], 4 * n + u + 1)
                    o = b1[:, 0:H * (D + 1)].rearrange("p (h d) -> p h d", h=H)
                    dve.reciprocal(rec3[:, d, :], o[:, :, D]).then_inc(s["l3_rec"], 1)
                    dve.wait_ge(s["l3_rec"], 4 * n + u + 1)
                    if u == 3:
                        dve.wait_ge(s["l3_sum"], 2 * n + 1)
                    dst = att1[:] if d else att[:, t, :]
                    dve.tensor_tensor(dst.rearrange("p (h d) -> p h d", h=H), o[:, :, 0:D], bc(rec3[:, d, :], 2, D),
                                      ALU.mult).then_inc(s["l3_o"], 1)
                for u in range(4):
                    t, d = u // 2, u % 2
                    c = 4 * n + u + 1
                    yield
                    if u == 0:
                        dve.wait_ge(s["l3_t"], n + 1)
                    dve.wait_ge(s["l3_aff"], c)
                    if u >= 2 or not isinstance(n, int) or n > 0:
                        dve.wait_ge(s["l3_pt"], c - 2)
                    dve.tensor_tensor(z3[:, u % 2], b0[:, 0:H * NG].rearrange("p (h j) -> p h j", h=H),
                                      bc(tmask[:, 2 * d + t, :], 1, H), ALU.add).then_inc(s["l3_z"], 1)
                    dve.wait_ge(s["l3_z"], c)
                    dve.tensor_reduce(max3[:, u % 2, :], z3[:, u % 2], AX.X, ALU.max, negate=True).then_inc(s["l3_max"], 1)
                    if u > 0:
                        yield
                        divide(u - 1)
                yield
                divide(3)
                yield
                dve.wait_ge(s["l3_at"], n + 1)
                for k in range(KC):
                    i = dve.scalar_tensor_tensor(nzq[:, k].rearrange("p b r -> p (b r)"), b0[:, k * GR:(k + 1) * GR],
                                                 bout[:, k:k + 1], sf[:, k].rearrange("p b r -> p (b r)"), ALU.add, ALU.add)
                i.then_inc(s["l3_r"], 1)
                dve.wait_ge(s["l3_r"], n + 1)
                reach(dve, s["l3_out"], 16 * n)
                dve.scalar_tensor_tensor(fin[:].rearrange("p k b r -> p (k b r)"), nzq[:].rearrange("p k b r -> p (k b r)"),
                                         0.0, xr3[:].rearrange("p k b r -> p (k b r)"), ALU.max, ALU.add).then_inc(s["l3_fin"], 1)

            bodies(dve, ORDER["dve"], {0: stream0, 1: stream1, 2: stream2, 3: stream3})


def kernel(**inputs):
    import numpy as np
    import concourse.bacc as bacc
    from concourse.bass_utils import run_bass_kernel_spmd

    i = {k: np.asarray(v) for k, v in inputs.items()}
    wqkv = i["L1_cond_Wqkv"].reshape(H, D, 3, C)
    bqkv = i["L1_cond_bqkv"].reshape(H, D, 3)
    l1w = [wqkv[:, :, j, :].reshape(C, C).T for j in range(3)]
    l1b = [bqkv[:, :, j].reshape(C) for j in range(3)]
    first = [i["L1_cond_Wg"].T, i["L1_cond_Wb"].T, i["L2_cond_emb_W"][:, :C], i["L2_cond_emb_W"][:, C:],
             i["L3_cond_W_self"][:, C:].T]
    weights = [*l1w, i["L1_cond_Wp"].T,
               i["L2_cond_Wq"], i["L2_cond_Wk"], i["L2_cond_Wv"], i["L2_cond_out_W"],
               i["L3_cond_W_self"][:, :C].T,
               i["L3_cond_Wq"][0].T, i["L3_cond_Wq"][1].T, i["L3_cond_Wk"][0].T, i["L3_cond_Wk"][1].T,
               i["L3_cond_Wout"][0].reshape(C, C).T, i["L3_cond_Wout"][1].reshape(C, C).T]
    vectors = [i["L1_cond_ln_g"], i["L1_cond_ln_b"], i["L1_cond_bg"], i["L1_cond_bb"], l1b[0], l1b[1], i["L1_cond_bp"],
               i["L2_cond_norm_g"], i["L2_cond_norm_b"], i["L2_cond_bk"], i["L2_cond_emb_b"][:C], i["L2_cond_emb_b"][C:],
               i["L2_cond_sn_g"], i["L2_cond_sn_b"], i["L2_cond_out_b"], i["L3_cond_b_self"],
               i["L3_cond_bq"][0], i["L3_cond_bq"][1], i["L3_cond_bk"][0], i["L3_cond_bk"][1],
               i["L3_cond_bout"][0], i["L3_cond_bout"][1]]
    adj = i["mask_BxSxSx11_ik0"]
    at = np.arange(P)
    arrays = {
        "x_t": i["x"].reshape(B * S, C).T,
        "cond": i["cond_1024"], "cond_t": i["cond_1024"].T,
        "first_w": np.stack(first), "w": np.stack(weights),
        "vec": np.stack(vectors).reshape(len(VECTORS), KC, P).transpose(2, 0, 1),
        "rowvec": np.stack([l1b[2], i["L2_cond_bq"], i["L2_cond_bv"]]),
        "ident": np.eye(P, dtype=np.float32), "ones": np.ones((P, P), np.float32),
        "mask_h": (at[:, None] // D == np.arange(HC)).astype(np.float32),
        "mask_bd": (at[:, None] // D == at // D).astype(np.float32),
        "mask_q": (np.arange(KQ)[:, None] // NG == np.arange(HQ)).astype(np.float32),
        "w_label": i["L3_cond_w_bias"], "b_label": i["L3_cond_b_bias"].reshape(1),
        "adj": np.stack([adj[:, :, :NG, :].reshape(B * S, NG * L),
                         adj[:, :NG, :, :].transpose(0, 2, 1, 3).reshape(B * S, NG * L)]),
    }
    nc = bacc.Bacc("TRN2", target_bir_lowering=False, num_devices=1)
    feeds, aps = {}, {}
    for name, v in arrays.items():
        v = np.ascontiguousarray(v)
        feeds[f"in_{name}"] = v
        aps[name] = nc.dram_tensor(f"in_{name}", v.shape, mybir.dt.from_np(v.dtype), kind="ExternalInput").ap()
    out = nc.dram_tensor("out_t", (C, B * S), F32, kind="ExternalOutput").ap()
    build(nc, aps, out)
    r = run_bass_kernel_spmd(nc, [feeds], core_ids=[0])
    return np.ascontiguousarray(r.results[0]["out_t"].T).reshape(B, S, C)
```

```python
from contextlib import ExitStack

import concourse.bass as bass
from concourse import mybir

P = 128
B, S, C = 64, 64, 256
H, D = 16, 16
KC = C // P
GB = 4
GR = GB * S
GROUPS = B // GB
HC = H // KC
NG, L = 20, 11
HQ = 4
KQ = HQ * NG
EPS = 1e-5
NEG = -9000000000000000.0
BEHIND = (0, 1, 2, 3, 2)
ORDER = {
    "sp": ("333", "333", "333"),
    "pool": ("32002232313300233341403140",
             "32012320233003233341403140",
             "32322012300332333414301400"),
    "act": ("112121033312222311302213033132333413",
            "112122102133322330221101333132333413",
            "112122333111202233122130033132333413"),
    "pe": ("1233111302131102112203321213023213231331331433031343",
           "1233111323011220112330132201122331231331334313031343",
           "1233111312312110021233122132321320313313341330031343"),
    "dve": ("1120333113011021212212332323212323133413400134133",
            "1123331013011212220221133322312323133413400134313",
            "1123311100133120212322213323212323133413041034133"),
}
KEEP = C // 2
P_KEEP = 0.9
LOG_MIN, LOG_MAX = -103.972, 88.7229

F32 = mybir.dt.float32
I32 = mybir.dt.int32
ALU = mybir.AluOpType
ACT = mybir.ActivationFunctionType
AX = mybir.AxisListType

FIRST_WEIGHTS = ["L1g", "L1b", "L2scale", "L2shift", "L3sq"]
WEIGHTS = ["L1q", "L1k", "L1v", "L1p", "L2q", "L2k", "L2v", "L2o", "L3s", "L3q0", "L3q1", "L3k0", "L3k1", "L3o0", "L3o1"]
WEIGHT_LOADS = [(0, 4), (4, 8), (8, len(WEIGHTS))]
VECTORS = ["L1ln_g", "L1ln_b", "L1bg", "L1bb", "L1bq", "L1bk", "L1bp", "L2norm_g", "L2norm_b", "L2bk",
           "L2scale_b", "L2shift_b", "L2sn_g", "L2sn_b", "L2out_b", "L3b_self", "L3bq0", "L3bq1",
           "L3bk0", "L3bk1", "L3bout0", "L3bout1"]
ROWVECS = ["L1bv", "L2bq", "L2bv"]


def bc(ap, axis, n):
    a = ap.unsqueeze(axis)
    shape = list(a.shape)
    shape[axis] = n
    return a.to_broadcast(shape)


def reach(eng, sem, value, wait=None):
    if isinstance(value, int) and value <= 0:
        return
    if wait is None:
        eng.wait_ge(sem, value)
    else:
        wait(eng, sem, value)


def turns(order, streams):
    for f in streams.values():
        next(f)
    for k in order:
        if int(k) in streams:
            next(streams[int(k)], None)


def build(nc, a, out):
    ctx = ExitStack()
    with ctx:
        def sb(name, shape, dt=F32):
            return ctx.enter_context(nc.sbuf_tensor(name, shape, dt))

        def bank(name):
            return ctx.enter_context(nc.psum_tensor(name, [P, 512], F32))

        def sem(name):
            return ctx.enter_context(nc.semaphore(name))

        w = sb("w", [P, len(WEIGHTS), KC, C])
        vec = sb("vec", [P, len(VECTORS), KC])
        rowvec = sb("rowvec", [P, len(ROWVECS), C])
        ident = sb("ident", [P, P])
        ones = sb("ones", [P, P])
        mask_h = sb("mask_h", [P, HC])
        mask_bd = sb("mask_bd", [P, P])
        mask_q = sb("mask_q", [KQ, HQ])
        w_label = sb("w_label", [P, L])
        b_label = sb("b_label", [P, 1])
        neg_half = sb("neg_half", [P, 2])

        def W(name, k, lo, hi):
            if name in FIRST_WEIGHTS:
                return first_w[:, FIRST_WEIGHTS.index(name), k, lo:hi]
            return w[:, WEIGHTS.index(name), k, lo:hi]

        def V(name, k=None):
            i = VECTORS.index(name)
            return vec[:, i, :] if k is None else vec[:, i, k:k + 1]

        cond_t = sb("cond_t", [P, KC, B])
        mask_t = sb("mask_t", [P, KC, B])
        gain1 = sb("gain1", [P, KC, B])
        bias1 = sb("bias1", [P, KC, B])
        gain2 = sb("gain2", [P, KC, B])
        bias2 = sb("bias2", [P, KC, B])
        qself = sb("qself", [P, KC, B])
        q0b = sb("q0b", [P, 2, KC])
        bout = sb("bout", [P, KC])

        x_all = sb("x_all", [P, KC, B, S])
        score_t = sb("score_t", [P, KC, B])
        top8 = sb("top8", [B, 8])
        sums = sb("sums", [B, 4])

        x1 = sb("x1", [P, KC, GB, S])
        z0 = sb("z0", [P, 2, C])
        z1 = sb("z1", [P, 2, C])
        x1b = sb("x1b", [P, KC, GB, S])
        ht = sb("ht", [P, KC, GR])
        g1 = sb("g1", [P, KC, GB, S])
        q1t = sb("q1t", [P, KC, GR])
        k1t = sb("k1t", [P, KC, GR])
        kbd = sb("kbd", [P, 4, 2, HC, S])
        vbd = sb("vbd", [P, GB, H // 2, 2, D + 1])
        prob = sb("prob", [P, 2, HC, S])
        probt = sb("probt", [P, 2, HC // 2, P])
        nmax1 = sb("nmax1", [P, 2, HC])
        rec1 = sb("rec1", [P, H])
        orow = sb("orow", [P, 2, C])
        ot = sb("ot", [P, KC, GR])
        h1 = sb("h1", [P, KC, GB, S])
        x2 = sb("x2", [P, KC, GB, S])
        st1, mv1, ve1, rs1, nm1 = (sb(x, [P, 2, *y]) for x, y in (("st1", (6,)), ("mv1", (2,)), ("ve1", ()), ("rs1", ()), ("nm1", ())))
        xr2 = sb("xr2", [P, KC, GB, S])
        z2 = sb("z2", [P, 2, C])
        xn = sb("xn", [P, KC, GR])
        k2t = sb("k2t", [P, KC, GB, S])
        ekrow = sb("ekrow", [P, 2, C])
        vsep = sb("vsep", [P, 4, 2, P])
        kmax = sb("kmax", [P, KC * GB])
        krec = sb("krec", [P, KC * GB])
        q2 = sb("q2", [P, 2, H, D])
        qmax = sb("qmax", [P, 2 * H])
        qrec = sb("qrec", [P, 2, H])
        eqt = sb("eqt", [P, KC, GR])
        ctxbd = sb("ctxbd", [P, 2, KC, 2, P])
        yrow = sb("yrow", [P, 2, C])
        h2 = sb("h2", [P, KC, GB, S])
        e2 = sb("e2", [P, KC, GB, S])
        s2 = sb("s2", [P, KC, GR])
        x3 = sb("x3", [P, KC, GB, S])
        st2, mv2, ve2, rs2, nm2 = (sb(x, [P, 2, *y]) for x, y in (("st2", (6,)), ("mv2", (2,)), ("ve2", ()), ("rs2", ()), ("nm2", ())))
        st0, mv0, ve0, rs0, nm0 = (sb(x, [P, 2, *y]) for x, y in (("st0", (6,)), ("mv0", (2,)), ("ve0", ()), ("rs0", ()), ("nm0", ())))
        xr3 = sb("xr3", [P, KC, GB, S])
        nzq = sb("nzq", [P, KC, GB, S])
        sf = sb("sf", [P, KC, GB, S])
        q3t = sb("q3t", [P, 2, KC, GR])
        k3t = sb("k3t", [P, 2, KC, GB, NG])
        kbd3 = sb("kbd3", [P, 2, KC, GB, HC, NG])
        vrow = sb("vrow", [P, 2, C])
        vbd3 = sb("vbd3", [KQ, GB, 2, H, D + 1])
        adj = sb("adj", [P, 4, NG * L], I32)
        adjw = sb("adjw", [P, 4, NG * L])
        cnt = sb("cnt", [P, 4, NG])
        vb = sb("vb", [P, 4, NG])
        tmask = sb("tmask", [P, 4, NG])
        z3 = sb("z3", [P, 2, H, NG])
        max3 = sb("max3", [P, 2, H])
        p3t = sb("p3t", [KQ, 2, 4, P])
        rec3 = sb("rec3", [P, 2, H])
        att = sb("att", [P, 2, C])
        att1 = sb("att1", [P, C])
        fin = sb("fin", [P, KC, GB, S])

        spare = kbd[:].rearrange("p u b h r -> p (u b h r)")
        cond, score, lnr, lkey, work, keepm = (spare[0:B, j * C:(j + 1) * C] for j in range(6))
        esil, fsil = (spare[:, 6 * C + j * KC * B:6 * C + (j + 1) * KC * B].rearrange("p (k b) -> p k b", k=KC) for j in range(2))
        first_w = kbd3[:].rearrange("p d k b h j -> p (d k b h j)").rearrange("p (w k n) -> p w k n", k=KC, n=C)

        bZ, bA, bE, bT = bank("bZ"), bank("bA"), bank("bE"), bank("bT")
        bX, bY = bank("bX"), bank("bY")
        b0, b1 = bank("b0"), bank("b1")

        names = """held zeros ld_cond ld_c ld_c2 ld_fw ld_w ld_x ld_x2 ld_x3 ld_x4 pro_v pro_pe pro_a pro_g pro_p own
        n0_st n0_mv n0_ve n0_rs n0_nm n0_z n1_st n1_mv n1_ve n1_rs n1_nm n1_z n2_st n2_mv n2_ve n2_rs n2_nm n2_z
        l0_x l0_row l0_zt l0_g l0_h l0_q l0_qt l0_k l0_kt l0_v l0_vs l0_kbd
        l1_e l1_max l1_sub l1_p l1_pt l1_pts l1_av l1_rec l1_o l1_ot l1_ots l1_wp l1_xb l1_h1 l1_row l1_zt l1_g l1_b l1_x2
        l2_x l2_row l2_zt l2_xn l2_k l2_kt l2_kmax l2_ksub l2_ke l2_ksum l2_krec l2_kd l2_q l2_qb
        l2_qmax l2_qsub l2_qe l2_qsum l2_qrec l2_v l2_vs l2_ekt l2_ek l2_eqt l2_eq l2_ctx l2_ctxs l2_y l2_yr
        l2_yt l2_g l2_h l2_e l2_r l2_s l2_o l2_og l2_x3
        l3_x l3_xs l3_sfp l3_nz l3_sf l3_q l3_qt l3_k l3_kt l3_kbd l3_v l3_vr l3_vd l3_adj l3_aw l3_cnt l3_vb l3_t0 l3_t l3_aff
        l3_z l3_max l3_sub l3_p l3_pt l3_pts l3_av l3_rec l3_o l3_sum l3_at l3_r l3_fin l3_out""".split()
        s = {name: sem(name) for name in names}


        block = ctx.enter_context(nc.Block())
        PARTS = [s["ld_x"], s["ld_x2"], s["ld_x3"], s["ld_x4"]]
        out_v = out.rearrange("(k p) r -> p k r", p=P)

        def hold(eng, sem_, value):
            eng.wait_ge(sem_, value)
            eng.sem_inc(s["held"], 1)

        def own(bk):
            return bk[:].rearrange("p (k b r) -> p k b r", k=KC, b=GB)

        def bodies(eng, orders, streams):
            last = max(BEHIND)

            def turn(i, order, has):
                turns(order, {k: f(i - BEHIND[k]) for k, f in streams.items() if has(BEHIND[k])})
            for i in range(last + 1):
                turn(i, orders[0], lambda lag: i >= lag)
            with eng.Fori(last + 1, GROUPS) as i:
                turn(i, orders[1], lambda lag: True)
            for i in range(GROUPS, GROUPS + last):
                turn(i, orders[2], lambda lag: i - lag < GROUPS)

        @block.sync
        def _(sp):
            for part in range(4):
                n = B // 4
                sp.dma_start(x_all[:, :, part * n:(part + 1) * n, :],
                             a["x_t"].rearrange("(k p) (b r) -> p k b r", p=P, r=S)[:, :, part * n:(part + 1) * n, :]
                             ).then_inc(PARTS[part], 16)
            w_in = a["w"].rearrange("w (k p) n -> p (w k) n", p=P)
            w_sb = w[:].rearrange("p w k n -> p (w k) n")
            for lo, hi in WEIGHT_LOADS:
                sp.dma_start(w_sb[:, KC * lo:KC * hi, :], w_in[:, KC * lo:KC * hi, :]).then_inc(s["ld_w"], 16)

            def stream3(n):
                yield
                reach(sp, s["l3_cnt"], n, hold)
                for d in range(2):
                    sp.dma_start(adj[:, 2 * d:2 * d + 2, :],
                                 a["adj"][d].rearrange("(t p) e -> p t e", p=P)[:, bass.ds(2 * n, 2), :]
                                 ).then_inc(s["l3_adj"], 16)
                yield
                hold(sp, s["l3_vr"], n + 1)
                reach(sp, s["l3_av"], 4 * n)
                for b in range(GB):
                    for h in range(HQ):
                        sp.dma_start(vbd3[NG * h:NG * h + NG, b].rearrange("p d (q h) e -> p (d q) h e", h=HQ)[:, :, h, 0:D],
                                     vrow[32 * b:32 * b + NG].rearrange("p d (q h e) -> p (d q) h e", h=HQ, e=D)[:, :, h, :]
                                     ).then_inc(s["l3_vd"], 16)
                yield
                hold(sp, s["l3_fin"], n + 1)
                sp.dma_start(out_v[:, :, bass.ds(GR * n, GR)], fin[:, :, :, :].rearrange("p k b r -> p k (b r)")
                             ).then_inc(s["l3_out"], 16)

            bodies(sp, ORDER["sp"], {3: stream3})
            sp.wait_ge(s["l3_out"], 16 * GROUPS)

        @block.gpsimd
        def _(pool):
            pool.memset(neg_half[:], -0.5).then_inc(s["zeros"], 1)
            pool.memset(vbd[:], 0.0).then_inc(s["zeros"], 1)
            pool.memset(vsep[:], 0.0).then_inc(s["zeros"], 1)
            pool.memset(vbd3[:], 0.0).then_inc(s["zeros"], 1)
            pool.wait_ge(s["zeros"], 4)
            for j in range(2):
                pool.memset(vbd[64 * j:64 * j + 64, :, :, j, D:D + 1], 1.0).then_inc(s["zeros"], 1)
                pool.wait_ge(s["zeros"], 5 + j)
            pool.wait_ge(s["ld_c2"], 16 * 7)
            for b in range(GB):
                for d in range(2):
                    i = pool.tensor_copy(vbd3[:, b, d, :, D].rearrange("p (q h) -> p q h", h=HQ), bc(mask_q[:], 1, 4))
            i.then_inc(s["zeros"], 1)

            steps = [0]

            def link(dst, x, y, op):
                steps[0] += 1
                pool.tensor_tensor(dst[:], x[:], y, op).then_inc(s["pro_p"], 1)
                pool.wait_ge(s["pro_p"], steps[0])
            pool.wait_ge(s["pro_g"], 1)
            pool.wait_ge(s["pro_a"], 4)
            link(gain2, gain2, bc(bc(ones[:, 0], 1, KC), 2, B), ALU.add)
            for gain, bias, norm_g, norm_b in ((gain1, bias1, "L1ln_g", "L1ln_b"), (gain2, bias2, "L2sn_g", "L2sn_b")):
                link(esil, gain, bc(V(norm_b), 2, B), ALU.mult)
                link(bias, bias, esil[:], ALU.add)
                link(gain, gain, bc(V(norm_g), 2, B), ALU.mult)

            def norm_scale(ve, rs, nm, name, count):
                pool.wait_ge(s[name + "_ve"], count)
                pool.tensor_tensor(rs[:], ve[:], neg_half[:], ALU.pow).then_inc(s[name + "_rs"], 1)
                pool.wait_ge(s[name + "_rs"], count)
                pool.tensor_tensor(nm[:], nm[:], rs[:], ALU.mult).then_inc(s[name + "_nm"], 1)

            def stream0(n):
                yield
                norm_scale(ve0, rs0, nm0, "n0", n + 1)
                yield
                hold(pool, s["l0_g"], n + 1)
                hv = ht[:].rearrange("p k (b r) -> p k b r", b=GB)
                pool.tensor_tensor(hv, hv, bc(bias1[:, :, bass.ds(GB * n, GB)], 3, S), ALU.add).then_inc(s["l0_h"], 1)
                yield
                reach(pool, s["l1_e"], 4 * n)
                pool.wait_ge(s["l0_kt"], n + 1)
                kv = k1t[:].rearrange("p k (b r) -> p k b r", b=GB)
                for u in range(4):
                    if u > 0:
                        yield
                    t, c = u // 2, u % 2
                    pool.tensor_tensor(kbd[:, u], bc(kv[:, c, 2 * t:2 * t + 2, :], 2, HC),
                                       bc(bc(mask_h[:], 2, S), 1, 2), ALU.mult).then_inc(s["l0_kbd"], 1)

            def stream1(n):
                yield
                reach(pool, s["l1_h1"], n, hold)
                at = bass.ds(GB * n, GB)
                pool.tensor_tensor(x1b[:], x_all[:, :, at, :], bc(mask_t[:, :, at], 3, S), ALU.mult).then_inc(s["l1_xb"], 1)
                yield
                norm_scale(ve1, rs1, nm1, "n1", n + 1)
                yield
                hold(pool, s["l1_g"], n + 1)
                pool.tensor_tensor(g1[:], g1[:], bc(bias1[:, :, bass.ds(GB * n, GB)], 3, S), ALU.add).then_inc(s["l1_b"], 1)

            def stream2(n):
                yield
                norm_scale(ve2, rs2, nm2, "n2", 2 * n + 1)
                yield
                pool.wait_ge(s["l2_kmax"], n + 1)
                kk = k2t[:].rearrange("p k b r -> p (k b) r")
                pool.tensor_tensor(kk, kk, bc(kmax[:], 2, S), ALU.add).then_inc(s["l2_ksub"], 1)
                yield
                pool.wait_ge(s["l2_qmax"], n + 1)
                qq = q2[:].rearrange("p t h d -> p (t h) d")
                pool.tensor_tensor(qq, qq, bc(qmax[:], 2, D), ALU.add).then_inc(s["l2_qsub"], 1)
                yield
                pool.wait_ge(s["l2_krec"], n + 1)
                pool.tensor_tensor(kk, kk, bc(krec[:], 2, S), ALU.mult).then_inc(s["l2_kd"], 1)
                yield
                norm_scale(ve2, rs2, nm2, "n2", 2 * n + 2)

            def stream4(n):
                yield
                hold(pool, s["l2_g"], n + 1)
                pool.tensor_tensor(h2[:], h2[:], bc(bias2[:, :, bass.ds(GB * n, GB)], 3, S), ALU.add).then_inc(s["l2_h"], 1)
                yield
                pool.wait_ge(s["l2_r"], n + 1)
                pool.tensor_tensor(s2[:].rearrange("p k (b r) -> p k b r", b=GB), h2[:], e2[:], ALU.mult).then_inc(s["l2_s"], 1)
                yield
                reach(pool, s["l3_x"], n)
                reach(pool, s["l3_sfp"], n)
                pool.wait_ge(s["l2_og"], n + 1)
                pool.tensor_tensor(x3[:], e2[:], xr2[:], ALU.add).then_inc(s["l2_x3"], 1)

            def stream3(n):
                yield
                pool.wait_ge(s["l2_x3"], n + 1)
                xv = x3[:].rearrange("p k b r -> p k (b r)")
                pool.tensor_tensor(att1[:], xv[:, 0, :], xv[:, 1, :], ALU.add).then_inc(s["l3_xs"], 1)
                for d in range(2):
                    yield
                    if d == 0:
                        reach(pool, s["l3_aff"], 4 * n)
                        pool.wait_ge(s["l3_kt"], n + 1)
                    for k in range(KC):
                        pool.tensor_tensor(kbd3[:, d, k], bc(k3t[:, d, k], 2, HC), bc(bc(mask_h[:], 2, NG), 1, GB),
                                           ALU.mult).then_inc(s["l3_kbd"], 1)
                for u in range(4):
                    yield
                    pool.wait_ge(s["l3_max"], 4 * n + u + 1)
                    pool.tensor_tensor(z3[:, u % 2], z3[:, u % 2], bc(max3[:, u % 2, :], 2, NG), ALU.add).then_inc(s["l3_sub"], 1)
                    if u >= 2:
                        t = u - 2
                        yield
                        pool.wait_ge(s["l3_o"], 4 * n + 2 * t + 2)
                        pool.tensor_tensor(att[:, t, :], att[:, t, :], att1[:], ALU.add).then_inc(s["l3_sum"], 1)

            bodies(pool, ORDER["pool"], {0: stream0, 1: stream1, 2: stream2, 3: stream3, 4: stream4})

        @block.scalar
        def _(act):
            act.dma_start(cond[:], a["cond"]).then_inc(s["ld_cond"], 16)
            act.dma_start(cond_t[:], a["cond_t"].rearrange("(k p) b -> p k b", p=P)).then_inc(s["ld_c"], 16)
            act.dma_start(ident[:], a["ident"]).then_inc(s["ld_c"], 16)
            act.dma_start(vec[:], a["vec"]).then_inc(s["ld_c"], 16)
            act.dma_start(first_w.rearrange("p w k n -> p (w k) n"), a["first_w"].rearrange("w (k p) n -> p (w k) n", p=P)
                          ).then_inc(s["ld_fw"], 16)
            act.wait_ge(s["pro_v"], 1)
            act.activation(lnr[:], cond[:], ACT.Ln).then_inc(s["pro_a"], 1)
            act.wait_ge(s["ld_c"], 16 * 3)
            act.activation(esil[:], cond_t[:], ACT.Exp, scale=-1.0).then_inc(s["pro_a"], 1)
            act.dma_start(rowvec[:], a["rowvec"].rearrange("(o v) c -> o v c", o=1).to_broadcast([P, len(ROWVECS), C])
                          ).then_inc(s["ld_c2"], 16)
            act.dma_start(mask_h[:], a["mask_h"]).then_inc(s["ld_c2"], 16)
            act.dma_start(mask_bd[:], a["mask_bd"]).then_inc(s["ld_c2"], 16)
            act.dma_start(mask_q[:], a["mask_q"]).then_inc(s["ld_c2"], 16)
            act.dma_start(w_label[:], a["w_label"].rearrange("(o l) -> o l", o=1).to_broadcast([P, L])).then_inc(s["ld_c2"], 16)
            act.dma_start(b_label[:], a["b_label"].rearrange("(o l) -> o l", o=1).to_broadcast([P, 1])).then_inc(s["ld_c2"], 16)
            act.dma_start(ones[:], a["ones"]).then_inc(s["ld_c2"], 16)

            def with_bias(dst, bk, at, name):
                for k in range(KC):
                    i = act.activation(dst[:, k, :], bk[:, at + k * B:at + (k + 1) * B], ACT.Identity, bias=V(name, k))
                return i
            act.wait_ge(s["pro_pe"], 2)
            with_bias(gain1, b0, 0, "L1bg")
            with_bias(bias1, b0, 128, "L1bb")
            act.activation(qself[:].rearrange("p k b -> p (k b)"), b0[:, 256:256 + KC * B], ACT.Copy).then_inc(s["pro_a"], 1)
            act.wait_ge(s["pro_pe"], 3)
            with_bias(gain2, b1, 0, "L2scale_b")
            with_bias(bias2, b1, 128, "L2shift_b").then_inc(s["pro_a"], 1)

            def normalize(z, src, rs, nm, name, count):
                act.wait_ge(s[name + "_nm"], count)
                for t in range(2):
                    i = act.activation(z[:, t, :], src(t), ACT.Identity, bias=nm[:, t:t + 1], scale=rs[:, t:t + 1])
                i.then_inc(s[name + "_z"], 1)

            def stream0(n):
                yield
                normalize(z0, lambda t: bZ[:, t * C:(t + 1) * C], rs0, nm0, "n0", n + 1)
                yield
                reach(act, s["l1_e"], 4 * n)
                act.wait_ge(s["l0_q"], n + 1)
                for k in range(KC):
                    i = act.activation(q1t[:, k, :], bZ[:, k * GR:(k + 1) * GR], ACT.Identity, bias=V("L1bq", k))
                i.then_inc(s["l0_qt"], 1)
                yield
                act.wait_ge(s["l0_k"], n + 1)
                for k in range(KC):
                    i = act.activation(k1t[:, k, :], bZ[:, k * GR:(k + 1) * GR], ACT.Identity, bias=V("L1bk", k))
                i.then_inc(s["l0_kt"], 1)

            def stream1(n):
                for u in range(5):
                    if u < 4:
                        yield
                        act.wait_ge(s["l1_sub"], 4 * n + u + 1)
                        pv = prob[:, u % 2, :, :]
                        act.activation(pv, pv, ACT.Exp).then_inc(s["l1_p"], 1)
                        yield
                        act.wait_ge(s["l1_pt"], 4 * n + u + 1)
                        act.activation(probt[:, u % 2, :, :], bT[:].rearrange("p (j r) -> p j r", r=P), ACT.Copy).then_inc(s["l1_pts"], 1)
                yield
                act.wait_ge(s["l1_ot"], n + 1)
                act.activation(ot[:], bA[:].rearrange("p (k r) -> p k r", k=KC), ACT.Copy).then_inc(s["l1_ots"], 1)
                yield
                normalize(z1, lambda t: bA[:, t * C:(t + 1) * C], rs1, nm1, "n1", n + 1)

            def stream2(n):
                yield
                normalize(z2, lambda t: bY[:, t * C:(t + 1) * C], rs2, nm2, "n2", 2 * n + 1)
                yield
                act.wait_ge(s["l2_zt"], n + 1)
                for k in range(KC):
                    i = act.activation(xn[:, k, :], bY[:, k * GR:(k + 1) * GR], ACT.Identity, bias=V("L2norm_b", k),
                                       scale=V("L2norm_g", k))
                i.then_inc(s["l2_xn"], 1)
                yield
                reach(act, s["l2_x3"], n)
                act.activation(xr2[:], x2[:], ACT.Copy).then_inc(s["l2_x"], 1)
                yield
                act.wait_ge(s["l2_k"], n + 1)
                for k in range(KC):
                    i = act.activation(k2t[:, k, :, :], bX[:, k * GR:(k + 1) * GR].rearrange("p (b r) -> p b r", b=GB),
                                       ACT.Identity, bias=V("L2bk", k))
                i.then_inc(s["l2_kt"], 1)
                yield
                act.wait_ge(s["l2_ksub"], n + 1)
                act.activation(k2t[:], k2t[:], ACT.Exp).then_inc(s["l2_ke"], 1)
                yield
                act.wait_ge(s["l2_qsub"], n + 1)
                act.activation(q2[:], q2[:], ACT.Exp).then_inc(s["l2_qe"], 1)
                yield
                act.wait_ge(s["l2_ekt"], n + 1)
                act.activation(ekrow[:], bX[:].rearrange("p (t c) -> p t c", t=2), ACT.Copy).then_inc(s["l2_ek"], 1)
                yield
                act.wait_ge(s["l2_eqt"], n + 1)
                act.activation(eqt[:], bY[:].rearrange("p (k r) -> p k r", k=KC), ACT.Copy).then_inc(s["l2_eq"], 1)
                yield
                normalize(z2, lambda t: yrow[:, t, :], rs2, nm2, "n2", 2 * n + 2)

            def stream4(n):
                yield
                act.wait_ge(s["l2_h"], n + 1)
                act.activation(e2[:], h2[:], ACT.Tanh, scale=0.5).then_inc(s["l2_e"], 1)

            def stream3(n):
                yield
                act.wait_ge(s["l3_v"], n + 1)
                act.activation(vrow[:], b1[:].rearrange("p (d c) -> p d c", d=2), ACT.Copy).then_inc(s["l3_vr"], 1)
                yield
                act.wait_ge(s["l3_k"], n + 1)
                for d in range(2):
                    for k in range(KC):
                        at = (d * KC + k) * GB * NG
                        i = act.activation(k3t[:, d, k, :, :], b0[:, at:at + GB * NG].rearrange("p (b j) -> p b j", b=GB),
                                           ACT.Identity, bias=V(f"L3bk{d}", k))
                i.then_inc(s["l3_kt"], 1)
                yield
                act.wait_ge(s["l2_x3"], n + 1)
                reach(act, s["l3_fin"], n)
                act.activation(xr3[:], x3[:], ACT.Copy).then_inc(s["l3_x"], 1)
                for d, bk in enumerate((b1, b0)):
                    yield
                    act.wait_ge(s["l3_q"], 2 * n + d + 1)
                    for k in range(KC):
                        i = act.activation(q3t[:, d, k, :], bk[:, k * GR:(k + 1) * GR], ACT.Identity,
                                           bias=q0b[:, d, k:k + 1], scale=0.25)
                    i.then_inc(s["l3_qt"], 1)
                for u in range(4):
                    yield
                    act.wait_ge(s["l3_sub"], 4 * n + u + 1)
                    act.activation(z3[:, u % 2], z3[:, u % 2], ACT.Exp).then_inc(s["l3_p"], 1)
                    yield
                    act.wait_ge(s["l3_pt"], 4 * n + u + 1)
                    act.activation(p3t[:, u % 2, :, :], b1[0:KQ, :].rearrange("p (j r) -> p j r", r=P), ACT.Copy).then_inc(s["l3_pts"], 1)

            bodies(act, ORDER["act"], {0: stream0, 1: stream1, 2: stream2, 3: stream3, 4: stream4})

        @block.tensor
        def _(pe):
            def project_t(bk, name, rhs, done, cols=None, at=0):
                nn = GR if cols is None else cols
                for mh in range(KC):
                    for k in range(KC):
                        i = pe.matmul(bk[:, at + mh * nn:at + (mh + 1) * nn], W(name, k, mh * P, mh * P + P), rhs(k),
                                      start=(k == 0), stop=(k == KC - 1))
                if done is not None:
                    i.then_inc(done, 1)

            def project_row(bk, name, src, done):
                for t in range(2):
                    for k in range(KC):
                        i = pe.matmul(bk[:, t * C:(t + 1) * C], src[:, k, t * P:(t + 1) * P], W(name, k, 0, C),
                                      start=(k == 0), stop=(k == KC - 1))
                i.then_inc(done, 1)

            def swap(bk, src, done):
                for x in range(2):
                    for y in range(2):
                        i = pe.transpose(bk[:, (y * 2 + x) * P:(y * 2 + x + 1) * P], src[:, x, y * P:(y + 1) * P], ident[:])
                i.then_inc(done, 1)

            def flat(t):
                return t[:].rearrange("p k b r -> p k (b r)")

            pe.wait_ge(s["ld_c"], 16 * 3)
            pe.wait_ge(s["pro_v"], 2)
            for k in range(KC):
                i = pe.transpose(bX[0:B, k * P:(k + 1) * P], score_t[:, k, :], ident[:])
            i.then_inc(s["pro_pe"], 1)
            pe.wait_ge(s["ld_fw"], 16)
            rhs = lambda k: cond_t[:, k, :]
            project_t(b0, "L1g", rhs, None, B, 0)
            project_t(b0, "L1b", rhs, None, B, 128)
            project_t(b0, "L3sq", rhs, s["pro_pe"], B, 256)
            pe.wait_ge(s["pro_g"], 1)
            project_t(b1, "L2scale", lambda k: fsil[:, k, :], None, B, 0)
            project_t(b1, "L2shift", lambda k: fsil[:, k, :], s["pro_pe"], B, 128)
            pe.wait_ge(s["ld_w"], 16 * len(WEIGHT_LOADS))
            pe.wait_ge(s["ld_c2"], 16 * 7)
            pe.wait_ge(s["pro_v"], 3)
            for k in range(KC):
                i = pe.transpose(bY[:, k * B:(k + 1) * B], keepm[:, k * P:(k + 1) * P], ident[0:B, 0:B])
            i.then_inc(s["pro_pe"], 1)

            def stream0(n):
                yield
                pe.wait_ge(s["l0_x"], n + 1)
                reach(pe, s["l0_vs"], n)
                swap(bZ, flat(x1), s["l0_row"])
                yield
                pe.wait_ge(s["n0_z"], n + 1)
                swap(bZ, z0, s["l0_zt"])
                yield
                pe.wait_ge(s["l0_h"], n + 1)
                project_t(bZ, "L1q", lambda k: ht[:, k, :], s["l0_q"])
                yield
                pe.wait_ge(s["l0_qt"], n + 1)
                project_t(bZ, "L1k", lambda k: ht[:, k, :], s["l0_k"])
                yield
                pe.wait_ge(s["l0_kt"], n + 1)
                project_row(bZ, "L1v", ht, s["l0_v"])

            def stream1(n):
                def energies(u):
                    t, c = u // 2, u % 2
                    pe.wait_ge(s["l0_kbd"], 4 * n + u + 1)
                    reach(pe, s["l1_sub"], 4 * n + u)
                    for b in range(2):
                        i = pe.matmul(bE[64 * b:64 * b + 64, :], q1t[:, c, (2 * t + b) * S:(2 * t + b + 1) * S],
                                      kbd[:, u, b, :, :].rearrange("p h r -> p (h r)"), start=True, stop=True)
                    i.then_inc(s["l1_e"], 1)

                def turn(u):
                    pe.wait_ge(s["l1_p"], 4 * n + u + 1)
                    reach(pe, s["l1_pts"], 4 * n + u)
                    for j in range(HC // 2):
                        i = pe.transpose(bT[:, j * P:(j + 1) * P],
                                         prob[:, u % 2, 2 * j:2 * j + 2, :].rearrange("p h r -> p (h r)"), ident[:])
                    i.then_inc(s["l1_pt"], 1)

                def weigh(u):
                    t, c = u // 2, u % 2
                    pe.wait_ge(s["l1_pts"], 4 * n + u + 1)
                    if u == 0:
                        pe.wait_ge(s["l0_vs"], n + 1)
                        reach(pe, s["l1_g"], n)
                    elif u == 2:
                        pe.wait_ge(s["l1_o"], 2 * n + 1)
                    for j in range(HC // 2):
                        for b in range(2):
                            at = (c * HC + 2 * j) * (D + 1)
                            i = pe.matmul(bA[64 * b:64 * b + 64, at:at + 2 * (D + 1)],
                                          probt[:, u % 2, j, 64 * b:64 * b + 64],
                                          vbd[:, 2 * t + b, c * (HC // 2) + j, :, :].rearrange("p h d -> p (h d)"),
                                          start=True, stop=True)
                    i.then_inc(s["l1_av"], 1)
                for u in range(5):
                    if u < 4:
                        yield
                        energies(u)
                    if u > 0:
                        yield
                        weigh(u - 1)
                    if u < 4:
                        yield
                        turn(u)
                yield
                pe.wait_ge(s["l1_o"], 2 * n + 2)
                swap(bA, orow, s["l1_ot"])
                yield
                pe.wait_ge(s["l1_ots"], n + 1)
                project_t(bA, "L1p", lambda k: ot[:, k, :], s["l1_wp"])
                yield
                pe.wait_ge(s["l1_h1"], n + 1)
                swap(bA, flat(h1), s["l1_row"])
                yield
                pe.wait_ge(s["n1_z"], n + 1)
                swap(bA, z1, s["l1_zt"])

            def stream2(n):
                yield
                pe.wait_ge(s["l1_x2"], n + 1)
                reach(pe, s["l2_ctxs"], 2 * n)
                swap(bY, flat(x2), s["l2_row"])
                yield
                pe.wait_ge(s["n2_z"], 2 * n + 1)
                swap(bY, z2, s["l2_zt"])
                yield
                pe.wait_ge(s["l2_xn"], n + 1)
                reach(pe, s["l2_og"], n)
                project_t(bX, "L2k", lambda k: xn[:, k, :], s["l2_k"])
                yield
                project_row(bY, "L2q", xn, s["l2_q"])
                yield
                pe.wait_ge(s["l2_kt"], n + 1)
                project_row(bX, "L2v", xn, s["l2_v"])
                yield
                pe.wait_ge(s["l2_vs"], n + 1)
                pe.wait_ge(s["l2_kd"], n + 1)
                swap(bX, flat(k2t), s["l2_ekt"])
                yield
                pe.wait_ge(s["l2_qe"], n + 1)
                swap(bY, q2[:].rearrange("p t h d -> p t (h d)"), s["l2_eqt"])
                yield
                pe.wait_ge(s["l2_ek"], n + 1)
                pe.wait_ge(s["l2_eq"], n + 1)
                for t, bk in enumerate((bX, bY)):
                    if t > 0:
                        yield
                    for c in range(KC):
                        i = pe.matmul(bk[:, c * 256:(c + 1) * 256], ekrow[:, t, c * P:(c + 1) * P],
                                      vsep[:, 2 * t + c, :, :].rearrange("p b d -> p (b d)"), start=True, stop=True)
                    i.then_inc(s["l2_ctx"], 1)
                yield
                pe.wait_ge(s["l2_ctxs"], 2 * n + 2)
                for t in range(2):
                    for c in range(KC):
                        for b in range(2):
                            i = pe.matmul(bX[64 * b:64 * b + 64, (2 * t + c) * P:(2 * t + c + 1) * P],
                                          eqt[:, c, (2 * t + b) * S:(2 * t + b + 1) * S], ctxbd[:, t, c, b, :],
                                          start=True, stop=True)
                i.then_inc(s["l2_y"], 1)

            def stream4(n):
                yield
                pe.wait_ge(s["n2_z"], 2 * n + 2)
                swap(bX, z2, s["l2_yt"])
                yield
                pe.wait_ge(s["l2_s"], n + 1)
                project_t(bX, "L2o", lambda k: s2[:, k, :], s["l2_o"])

            def stream3(n):
                yield
                pe.wait_ge(s["l2_x3"], n + 1)
                reach(pe, s["l3_r"], n)
                project_t(b0, "L3s", lambda k: flat(x3)[:, k, :], None)
                yield
                pe.wait_ge(s["l3_xs"], n + 1)
                pe.matmul(b1[:, 0:GR], ones[:], att1[:], start=True, stop=True).then_inc(s["l3_sfp"], 1)
                yield
                pe.wait_ge(s["l3_sf"], n + 1)
                o = WEIGHTS.index("L3o0")
                for k in range(KC):
                    for b in range(GB):
                        i = pe.matmul(b1[32 * b:32 * b + 32, :], sf[:, k, b, 0:32], w[:, o:o + 2, k, :],
                                      start=(k == 0), stop=(k == KC - 1))
                i.then_inc(s["l3_v"], 1)
                yield
                for d in range(2):
                    project_t(b0, f"L3k{d}", lambda k: sf[:, k, :, 0:NG], s["l3_k"] if d else None, GB * NG, d * KC * GB * NG)
                yield
                pe.wait_ge(s["l3_vr"], n + 1)
                project_t(b1, "L3q0", lambda k: flat(sf)[:, k, :], s["l3_q"])
                yield
                pe.wait_ge(s["l3_kt"], n + 1)
                project_t(b0, "L3q1", lambda k: flat(sf)[:, k, :], s["l3_q"])

                def affinities(u):
                    t, d = u // 2, u % 2
                    if u == 0:
                        pe.wait_ge(s["l3_qt"], 2 * n + 2)
                    pe.wait_ge(s["l3_kbd"], 4 * n + 2 * d + 2)
                    reach(pe, s["l3_z"], 4 * n + u)
                    for c in range(KC):
                        for b in range(2):
                            i = pe.matmul(b0[64 * b:64 * b + 64, c * HC * NG:(c + 1) * HC * NG],
                                          q3t[:, d, c, (2 * t + b) * S:(2 * t + b + 1) * S],
                                          kbd3[:, d, c, 2 * t + b, :, :].rearrange("p h j -> p (h j)"),
                                          start=True, stop=True)
                    i.then_inc(s["l3_aff"], 1)

                def turn(u):
                    pe.wait_ge(s["l3_p"], 4 * n + u + 1)
                    if u > 0:
                        pe.wait_ge(s["l3_o"], 4 * n + u)
                    for j in range(4):
                        i = pe.transpose(b1[0:KQ, j * P:(j + 1) * P],
                                         z3[:, u % 2, HQ * j:HQ * j + HQ, :].rearrange("p h j -> p (h j)"), ident[:])
                    i.then_inc(s["l3_pt"], 1)

                def weigh(u):
                    t, d = u // 2, u % 2
                    pe.wait_ge(s["l3_pts"], 4 * n + u + 1)
                    if u == 0:
                        pe.wait_ge(s["l3_vd"], 16 * GB * HQ * (n + 1))
                    for j in range(4):
                        for b in range(2):
                            at = j * HQ * (D + 1)
                            i = pe.matmul(b1[64 * b:64 * b + 64, at:at + HQ * (D + 1)], p3t[:, u % 2, j, 64 * b:64 * b + 64],
                                          vbd3[:, 2 * t + b, d, HQ * j:HQ * j + HQ, :].rearrange("p h d -> p (h d)"),
                                          start=True, stop=True)
                    i.then_inc(s["l3_av"], 1)
                for u in range(5):
                    if u < 4:
                        yield
                        affinities(u)
                    if u > 0:
                        yield
                        turn(u - 1)
                        yield
                        weigh(u - 1)
                yield
                pe.wait_ge(s["l3_sum"], 2 * n + 2)
                swap(b0, att, s["l3_at"])

            bodies(pe, ORDER["pe"], {0: stream0, 1: stream1, 2: stream2, 3: stream3, 4: stream4})

        @block.vector
        def _(dve):
            count = [0]

            def link(i):
                count[0] += 1
                i.then_inc(s["own"], 1)
                dve.wait_ge(s["own"], count[0])

            dve.wait_ge(s["ld_cond"], 16)
            link(dve.tensor_scalar(work[:], cond[:], P_KEEP, None, ALU.is_lt))
            dve.tensor_scalar(cond[:], cond[:], 1e-18, None, ALU.max).then_inc(s["pro_v"], 1)
            q = B // 4
            for p_ in range(4):
                dve.wait_ge(PARTS[p_], 16)
                for k in range(KC):
                    link(dve.tensor_reduce(score_t[:, k, p_ * q:(p_ + 1) * q], x_all[:, k, p_ * q:(p_ + 1) * q, :], AX.X, ALU.add))
                if p_ == 1:
                    dve.wait_ge(s["pro_a"], 2)
                    link(dve.tensor_scalar(esil[:], esil[:], 1.0, None, ALU.add))
                    link(dve.reciprocal(esil[:], esil[:]))
                    dve.tensor_tensor(fsil[:], cond_t[:], esil[:], ALU.mult).then_inc(s["pro_g"], 1)
            dve.tensor_scalar(score_t[:], score_t[:], 1.0 / S, None, ALU.mult).then_inc(s["pro_v"], 1)
            for d in range(2):
                link(dve.tensor_scalar(q0b[:, d, :], V(f"L3bq{d}"), 0.25, None, ALU.mult))
            link(dve.tensor_tensor(bout[:], V("L3bout0"), V("L3bout1"), ALU.add))
            dve.wait_ge(s["pro_pe"], 1)
            link(dve.tensor_copy(score[:], bX[0:B, 0:C]))
            link(dve.reciprocal(lkey[:], score[:]))
            link(dve.tensor_tensor(lkey[:], lkey[:], lnr[:], ALU.mult))
            link(dve.tensor_scalar(lkey[:], lkey[:], LOG_MIN, LOG_MAX, ALU.max, ALU.min))
            for r in range(KEEP // 8):
                left = keepm if r else lkey
                link(dve.max(top8[:], left[:]))
                if r < KEEP // 8 - 1:
                    link(dve.match_replace(keepm[:], top8[:], left[:], -1e30))
            link(dve.tensor_scalar(keepm[:], lkey[:], top8[:, 7:8], None, ALU.is_ge))
            link(dve.tensor_tensor(lkey[:], keepm[:], score[:], ALU.mult))
            link(dve.tensor_reduce(sums[:, 0:1], lkey[:], AX.X, ALU.add))
            link(dve.tensor_reduce(sums[:, 1:2], score[:], AX.X, ALU.add))
            link(dve.reciprocal(sums[:, 2:3], sums[:, 0:1]))
            link(dve.tensor_tensor(sums[:, 3:4], sums[:, 2:3], sums[:, 1:2], ALU.mult))
            link(dve.tensor_tensor(keepm[:], keepm[:], work[:], ALU.mult))
            dve.tensor_scalar(keepm[:], keepm[:], sums[:, 3:4], None, ALU.mult).then_inc(s["pro_v"], 1)
            dve.wait_ge(s["pro_pe"], 4)
            link(dve.tensor_copy(mask_t[:], bY[:, 0:KC * B].rearrange("p (k b) -> p k b", k=KC)))
            dve.wait_ge(s["pro_p"], 7)
            dve.wait_ge(s["zeros"], 7)

            def norm(src, st, mv, ve, nm, name, c):
                for t in range(2):
                    i = dve.bn_stats(st[:, t, :], src(t))
                i.then_inc(s[name + "_st"], 1)
                hold(dve, s[name + "_st"], c)
                for t in range(2):
                    i = dve.bn_aggr(mv[:, t, :], st[:, t, :])
                i.then_inc(s[name + "_mv"], 1)
                dve.wait_ge(s[name + "_mv"], c)
                dve.tensor_scalar(nm[:], mv[:, :, 0], -1.0, None, ALU.mult)
                dve.tensor_scalar(ve[:], mv[:, :, 1], EPS, None, ALU.add).then_inc(s[name + "_ve"], 1)

            def stream0(n):
                at = bass.ds(GB * n, GB)
                yield
                dve.tensor_tensor(x1[:], x_all[:, :, at, :], bc(mask_t[:, :, at], 3, S), ALU.mult).then_inc(s["l0_x"], 1)
                yield
                dve.wait_ge(s["l0_row"], n + 1)
                norm(lambda t: bZ[:, t * C:(t + 1) * C], st0, mv0, ve0, nm0, "n0", n + 1)
                yield
                dve.wait_ge(s["l0_zt"], n + 1)
                dve.tensor_tensor(ht[:].rearrange("p k (b r) -> p k b r", b=GB), own(bZ), bc(gain1[:, :, at], 3, S),
                                  ALU.mult).then_inc(s["l0_g"], 1)
                yield
                reach(dve, s["l1_av"], 4 * n)
                dve.wait_ge(s["l0_v"], n + 1)
                for b in range(GB):
                    if b % 2 == 0 and b > 0:
                        yield
                    for j in range(2):
                        lo = 64 * (b % 2)
                        src = bZ[lo:lo + 64, (b // 2) * C:(b // 2 + 1) * C].rearrange("p (g h d) -> p g h d", h=2, d=D)
                        add = rowvec[lo:lo + 64, 0, :].rearrange("p (g h d) -> p g h d", h=2, d=D)
                        i = dve.tensor_tensor(vbd[64 * j:64 * j + 64, b, :, j, 0:D], src[:, :, j, :], add[:, :, j, :], ALU.add)
                i.then_inc(s["l0_vs"], 1)

            def stream1(n):
                at = bass.ds(GB * n, GB)
                for u in range(4):
                    yield
                    c = 4 * n + u + 1
                    dve.wait_ge(s["l1_e"], c)
                    e = bE[:].rearrange("p (h r) -> p h r", h=HC)
                    dve.tensor_reduce(nmax1[:, u % 2, :], e, AX.X, ALU.max, negate=True).then_inc(s["l1_max"], 1)
                    yield
                    dve.wait_ge(s["l1_max"], c)
                    if u >= 2 or not isinstance(n, int) or n > 0:
                        dve.wait_ge(s["l1_pt"], c - 2)
                    dve.tensor_tensor(prob[:, u % 2, :, :], e, bc(nmax1[:, u % 2, :], 2, S), ALU.add).then_inc(s["l1_sub"], 1)
                    if u >= 2:
                        t = u - 2
                        yield
                        dve.wait_ge(s["l1_av"], 4 * n + 2 * t + 2)
                        o = bA[:, 0:H * (D + 1)].rearrange("p (h d) -> p h d", h=H)
                        dve.reciprocal(rec1[:], o[:, :, D]).then_inc(s["l1_rec"], 1)
                        dve.wait_ge(s["l1_rec"], 2 * n + t + 1)
                        dve.scalar_tensor_tensor(orow[:, t, :].rearrange("p (h d) -> p h d", h=H), o[:, :, 0:D],
                                                 1.0 / C ** 0.5, bc(rec1[:], 2, D), ALU.mult, ALU.mult).then_inc(s["l1_o"], 1)
                yield
                dve.wait_ge(s["l1_xb"], n + 1)
                dve.wait_ge(s["l1_wp"], n + 1)
                for k in range(KC):
                    i = dve.scalar_tensor_tensor(h1[:, k].rearrange("p b r -> p (b r)"), bA[:, k * GR:(k + 1) * GR],
                                                 V("L1bp", k), x1b[:, k].rearrange("p b r -> p (b r)"), ALU.add, ALU.add)
                i.then_inc(s["l1_h1"], 1)
                yield
                dve.wait_ge(s["l1_row"], n + 1)
                norm(lambda t: bA[:, t * C:(t + 1) * C], st1, mv1, ve1, nm1, "n1", n + 1)
                yield
                dve.wait_ge(s["l1_zt"], n + 1)
                dve.tensor_tensor(g1[:], own(bA), bc(gain1[:, :, at], 3, S), ALU.mult).then_inc(s["l1_g"], 1)
                yield
                reach(dve, s["l2_x"], n)
                reach(dve, s["l2_row"], n)
                dve.wait_ge(s["l1_b"], n + 1)
                dve.tensor_tensor(x2[:], g1[:], h1[:], ALU.add).then_inc(s["l1_x2"], 1)

            def stream2(n):
                at = bass.ds(GB * n, GB)
                yield
                dve.wait_ge(s["l2_row"], n + 1)
                norm(lambda t: bY[:, t * C:(t + 1) * C], st2, mv2, ve2, nm2, "n2", 2 * n + 1)
                yield
                dve.wait_ge(s["l2_kt"], n + 1)
                kk = k2t[:].rearrange("p k b r -> p (k b) r")
                dve.tensor_reduce(kmax[:], kk, AX.X, ALU.max, negate=True).then_inc(s["l2_kmax"], 1)
                yield
                dve.wait_ge(s["l2_q"], n + 1)
                qq = q2[:].rearrange("p t h d -> p (t h) d")
                dve.tensor_tensor(q2[:].rearrange("p t h d -> p t (h d)"), bY[:].rearrange("p (t c) -> p t c", t=2),
                                  bc(rowvec[:, 1, :], 1, 2), ALU.add).then_inc(s["l2_qb"], 1)
                yield
                dve.wait_ge(s["l2_qb"], n + 1)
                dve.tensor_reduce(qmax[:], qq, AX.X, ALU.max, negate=True).then_inc(s["l2_qmax"], 1)
                yield
                dve.wait_ge(s["l2_ke"], n + 1)
                dve.tensor_reduce(krec[:], kk, AX.X, ALU.add).then_inc(s["l2_ksum"], 1)
                dve.wait_ge(s["l2_ksum"], n + 1)
                dve.reciprocal(krec[:], krec[:]).then_inc(s["l2_krec"], 1)
                yield
                dve.wait_ge(s["l2_v"], n + 1)
                for b in range(2):
                    lo, hi = 64 * b, 64 * b + 64
                    src = bX[lo:hi, :].rearrange("p (t c d) -> p t c d", t=2, c=KC)
                    add = bc(rowvec[lo:hi, 2, :].rearrange("p (c d) -> p c d", c=KC), 1, 2)
                    i = dve.tensor_tensor(vsep[lo:hi, :, b, :].rearrange("p (t c) d -> p t c d", t=2), src, add, ALU.add)
                i.then_inc(s["l2_vs"], 1)
                yield
                dve.wait_ge(s["l2_qe"], n + 1)
                dve.tensor_reduce(qrec[:].rearrange("p t h -> p (t h)"), qq, AX.X, ALU.add).then_inc(s["l2_qsum"], 1)
                dve.wait_ge(s["l2_qsum"], n + 1)
                dve.reciprocal(qrec[:], qrec[:]).then_inc(s["l2_qrec"], 1)
                yield
                for t, bk in enumerate((bX, bY)):
                    if t > 0:
                        yield
                    dve.wait_ge(s["l2_ctx"], 2 * n + t + 1)
                    dve.tensor_tensor(ctxbd[:, t].rearrange("p c b d -> p (c b) d"), bk[:].rearrange("p (g d) -> p g d", d=P),
                                      bc(mask_bd[:], 1, 4), ALU.mult).then_inc(s["l2_ctxs"], 1)
                yield
                dve.wait_ge(s["l2_qrec"], n + 1)
                dve.wait_ge(s["l2_y"], n + 1)
                dve.tensor_tensor(yrow[:].rearrange("p t (h d) -> p (t h) d", d=D), bX[:].rearrange("p (h d) -> p h d", d=D),
                                  bc(qrec[:].rearrange("p t h -> p (t h)"), 2, D), ALU.mult).then_inc(s["l2_yr"], 1)
                yield
                hold(dve, s["l2_yr"], n + 1)
                norm(lambda t: yrow[:, t, :], st2, mv2, ve2, nm2, "n2", 2 * n + 2)

            def stream4(n):
                at = bass.ds(GB * n, GB)
                yield
                dve.wait_ge(s["l2_yt"], n + 1)
                dve.tensor_tensor(h2[:], own(bX), bc(gain2[:, :, at], 3, S), ALU.mult).then_inc(s["l2_g"], 1)
                yield
                dve.wait_ge(s["l2_e"], n + 1)
                dve.tensor_scalar(e2[:], e2[:], 0.5, 0.5, ALU.mult, ALU.add).then_inc(s["l2_r"], 1)
                yield
                dve.wait_ge(s["l2_o"], n + 1)
                for k in range(KC):
                    i = dve.scalar_tensor_tensor(e2[:, k], own(bX)[:, k], V("L2out_b", k), bc(cond_t[:, k, at], 2, S),
                                                 ALU.add, ALU.mult)
                i.then_inc(s["l2_og"], 1)

            def stream3(n):
                at = bass.ds(GB * n, GB)
                yield
                reach(dve, s["l3_fin"], n)
                dve.wait_ge(s["l3_sfp"], n + 1)
                for k in range(KC):
                    i = dve.scalar_tensor_tensor(nzq[:, k], b1[:, 0:GR].rearrange("p (b r) -> p b r", b=GB), 0.0,
                                                 bc(qself[:, k, at], 2, S), ALU.not_equal, ALU.mult)
                i.then_inc(s["l3_nz"], 1)
                yield
                dve.wait_ge(s["l3_nz"], n + 1)
                for k in range(KC):
                    i = dve.scalar_tensor_tensor(sf[:, k].rearrange("p b r -> p (b r)"), b0[:, k * GR:(k + 1) * GR],
                                                 V("L3b_self", k), nzq[:, k].rearrange("p b r -> p (b r)"), ALU.add, ALU.add)
                i.then_inc(s["l3_sf"], 1)
                yield
                dve.wait_ge(s["l3_adj"], 32 * (n + 1))
                av = adj[:].rearrange("p q (j l) -> p (q j) l", l=L)
                wv = adjw[:].rearrange("p q (j l) -> p (q j) l", l=L)
                dve.tensor_tensor(wv, av, bc(w_label[:], 1, 4 * NG), ALU.mult).then_inc(s["l3_aw"], 1)
                yield
                dve.tensor_reduce(cnt[:].rearrange("p q j -> p (q j)"), av, AX.X, ALU.add).then_inc(s["l3_cnt"], 1)
                yield
                dve.wait_ge(s["l3_aw"], n + 1)
                dve.tensor_reduce(vb[:].rearrange("p q j -> p (q j)"), wv, AX.X, ALU.add).then_inc(s["l3_vb"], 1)
                yield
                dve.wait_ge(s["l3_cnt"], n + 1)
                dve.tensor_scalar(cnt[:], cnt[:], 0.0, NEG, ALU.is_le, ALU.mult).then_inc(s["l3_t0"], 1)
                dve.wait_ge(s["l3_vb"], n + 1)
                dve.wait_ge(s["l3_t0"], 2 * n + 1)
                dve.tensor_scalar(vb[:], vb[:], b_label[:, 0:1], None, ALU.add).then_inc(s["l3_t0"], 1)
                dve.wait_ge(s["l3_t0"], 2 * n + 2)
                dve.tensor_tensor(tmask[:], cnt[:], vb[:], ALU.add).then_inc(s["l3_t"], 1)

                def divide(u):
                    t, d = u // 2, u % 2
                    dve.wait_ge(s["l3_av"], 4 * n + u + 1)
                    o = b1[:, 0:H * (D + 1)].rearrange("p (h d) -> p h d", h=H)
                    dve.reciprocal(rec3[:, d, :], o[:, :, D]).then_inc(s["l3_rec"], 1)
                    dve.wait_ge(s["l3_rec"], 4 * n + u + 1)
                    if u == 3:
                        dve.wait_ge(s["l3_sum"], 2 * n + 1)
                    dst = att1[:] if d else att[:, t, :]
                    dve.tensor_tensor(dst.rearrange("p (h d) -> p h d", h=H), o[:, :, 0:D], bc(rec3[:, d, :], 2, D),
                                      ALU.mult).then_inc(s["l3_o"], 1)
                for u in range(4):
                    t, d = u // 2, u % 2
                    c = 4 * n + u + 1
                    yield
                    if u == 0:
                        dve.wait_ge(s["l3_t"], n + 1)
                    dve.wait_ge(s["l3_aff"], c)
                    if u >= 2 or not isinstance(n, int) or n > 0:
                        dve.wait_ge(s["l3_pt"], c - 2)
                    dve.tensor_tensor(z3[:, u % 2], b0[:, 0:H * NG].rearrange("p (h j) -> p h j", h=H),
                                      bc(tmask[:, 2 * d + t, :], 1, H), ALU.add).then_inc(s["l3_z"], 1)
                    dve.wait_ge(s["l3_z"], c)
                    dve.tensor_reduce(max3[:, u % 2, :], z3[:, u % 2], AX.X, ALU.max, negate=True).then_inc(s["l3_max"], 1)
                    if u > 0:
                        yield
                        divide(u - 1)
                yield
                divide(3)
                yield
                dve.wait_ge(s["l3_at"], n + 1)
                for k in range(KC):
                    i = dve.scalar_tensor_tensor(nzq[:, k].rearrange("p b r -> p (b r)"), b0[:, k * GR:(k + 1) * GR],
                                                 bout[:, k:k + 1], sf[:, k].rearrange("p b r -> p (b r)"), ALU.add, ALU.add)
                i.then_inc(s["l3_r"], 1)
                yield
                dve.wait_ge(s["l3_r"], n + 1)
                reach(dve, s["l3_out"], 16 * n)
                dve.scalar_tensor_tensor(fin[:].rearrange("p k b r -> p (k b r)"), nzq[:].rearrange("p k b r -> p (k b r)"),
                                         0.0, xr3[:].rearrange("p k b r -> p (k b r)"), ALU.max, ALU.add).then_inc(s["l3_fin"], 1)

            bodies(dve, ORDER["dve"], {0: stream0, 1: stream1, 2: stream2, 3: stream3, 4: stream4})


def kernel(**inputs):
    import numpy as np
    import concourse.bacc as bacc
    from concourse.bass_utils import run_bass_kernel_spmd

    i = {k: np.asarray(v) for k, v in inputs.items()}
    wqkv = i["L1_cond_Wqkv"].reshape(H, D, 3, C)
    bqkv = i["L1_cond_bqkv"].reshape(H, D, 3)
    l1w = [wqkv[:, :, j, :].reshape(C, C).T for j in range(3)]
    l1b = [bqkv[:, :, j].reshape(C) for j in range(3)]
    first = [i["L1_cond_Wg"].T, i["L1_cond_Wb"].T, i["L2_cond_emb_W"][:, :C], i["L2_cond_emb_W"][:, C:],
             i["L3_cond_W_self"][:, C:].T]
    weights = [*l1w, i["L1_cond_Wp"].T,
               i["L2_cond_Wq"], i["L2_cond_Wk"], i["L2_cond_Wv"], i["L2_cond_out_W"],
               i["L3_cond_W_self"][:, :C].T,
               i["L3_cond_Wq"][0].T, i["L3_cond_Wq"][1].T, i["L3_cond_Wk"][0].T, i["L3_cond_Wk"][1].T,
               i["L3_cond_Wout"][0].reshape(C, C).T, i["L3_cond_Wout"][1].reshape(C, C).T]
    vectors = [i["L1_cond_ln_g"], i["L1_cond_ln_b"], i["L1_cond_bg"], i["L1_cond_bb"], l1b[0], l1b[1], i["L1_cond_bp"],
               i["L2_cond_norm_g"], i["L2_cond_norm_b"], i["L2_cond_bk"], i["L2_cond_emb_b"][:C], i["L2_cond_emb_b"][C:],
               i["L2_cond_sn_g"], i["L2_cond_sn_b"], i["L2_cond_out_b"], i["L3_cond_b_self"],
               i["L3_cond_bq"][0], i["L3_cond_bq"][1], i["L3_cond_bk"][0], i["L3_cond_bk"][1],
               i["L3_cond_bout"][0], i["L3_cond_bout"][1]]
    adj = i["mask_BxSxSx11_ik0"]
    at = np.arange(P)
    arrays = {
        "x_t": i["x"].reshape(B * S, C).T,
        "cond": i["cond_1024"], "cond_t": i["cond_1024"].T,
        "first_w": np.stack(first), "w": np.stack(weights),
        "vec": np.stack(vectors).reshape(len(VECTORS), KC, P).transpose(2, 0, 1),
        "rowvec": np.stack([l1b[2], i["L2_cond_bq"], i["L2_cond_bv"]]),
        "ident": np.eye(P, dtype=np.float32), "ones": np.ones((P, P), np.float32),
        "mask_h": (at[:, None] // D == np.arange(HC)).astype(np.float32),
        "mask_bd": (at[:, None] // D == at // D).astype(np.float32),
        "mask_q": (np.arange(KQ)[:, None] // NG == np.arange(HQ)).astype(np.float32),
        "w_label": i["L3_cond_w_bias"], "b_label": i["L3_cond_b_bias"].reshape(1),
        "adj": np.stack([adj[:, :, :NG, :].reshape(B * S, NG * L),
                         adj[:, :NG, :, :].transpose(0, 2, 1, 3).reshape(B * S, NG * L)]),
    }
    nc = bacc.Bacc("TRN2", target_bir_lowering=False, num_devices=1)
    feeds, aps = {}, {}
    for name, v in arrays.items():
        v = np.ascontiguousarray(v)
        feeds[f"in_{name}"] = v
        aps[name] = nc.dram_tensor(f"in_{name}", v.shape, mybir.dt.from_np(v.dtype), kind="ExternalInput").ap()
    out = nc.dram_tensor("out_t", (C, B * S), F32, kind="ExternalOutput").ap()
    build(nc, aps, out)
    r = run_bass_kernel_spmd(nc, [feeds], core_ids=[0])
    return np.ascontiguousarray(r.results[0]["out_t"].T).reshape(B, S, C)
```
